# Optimizing a Trainium2 kernel written in Bass

```python
import numpy as np
import jax
import jax.numpy as jnp

def _softmax(x, axis=-1):
    return jax.nn.softmax(x, axis=axis)

def _gelu(x):
    return jax.nn.gelu(x, approximate=True)

def _silu(x):
    return jax.nn.silu(x)

def _sigmoid(x):
    return jax.nn.sigmoid(x)

def _layernorm(x, axis=-1, eps=1e-05):
    m = jnp.mean(x, axis=axis, keepdims=True)
    v = jnp.var(x, axis=axis, keepdims=True)
    return (x - m) / jnp.sqrt(v + eps)

def _scatter_add(tgt, idx, src, axis=0):
    return tgt.at[idx].add(src)

def _segment_sum(src, seg, n):
    return jax.ops.segment_sum(src, seg, n)
kernel_name = 'mk_recurrent_d2_jaxref_r8_ad037d'

def setup_inputs(seed: int=0):
    np.random.seed(seed)
    _w = jnp.asarray

    def _L0_attn_setup():
        import jax, jax.numpy as jnp
        import numpy as np
        import math
        N_EMBD = 128
        N_HEAD = 16
        HEAD = N_EMBD // N_HEAD
        LAMBDA_INIT = 0.8 - 0.6 * math.exp(-0.3 * (4 - 1))
        EPS = 1e-05
        key = jax.random.key(seed)
        ks = jax.random.split(key, 12)
        s = 1.0 / math.sqrt(N_EMBD)
        inp = {'x': jax.random.normal(ks[0], (2, 256, N_EMBD), dtype=jnp.float32), 'q1_w': jax.random.normal(ks[1], (N_EMBD, N_EMBD), dtype=jnp.float32) * s, 'q2_w': jax.random.normal(ks[2], (N_EMBD, N_EMBD), dtype=jnp.float32) * s, 'k1_w': jax.random.normal(ks[3], (N_EMBD, N_EMBD), dtype=jnp.float32) * s, 'k2_w': jax.random.normal(ks[4], (N_EMBD, N_EMBD), dtype=jnp.float32) * s, 'v_w': jax.random.normal(ks[5], (N_EMBD, 2 * N_EMBD), dtype=jnp.float32) * s, 'c_w': jax.random.normal(ks[6], (2 * N_EMBD, N_EMBD), dtype=jnp.float32) * (1.0 / math.sqrt(2 * N_EMBD)), 'lambda_q1': jax.random.normal(ks[7], (N_HEAD, HEAD), dtype=jnp.float32) * 0.1, 'lambda_k1': jax.random.normal(ks[8], (N_HEAD, HEAD), dtype=jnp.float32) * 0.1, 'lambda_q2': jax.random.normal(ks[9], (N_HEAD, HEAD), dtype=jnp.float32) * 0.1, 'lambda_k2': jax.random.normal(ks[10], (N_HEAD, HEAD), dtype=jnp.float32) * 0.1}
        return inp
    _L0_attn_in = _L0_attn_setup()

    def _L0_ffn_setup():
        import math
        import jax, jax.numpy as jnp
        import numpy as np
        B, S, D, H, E, K = (4, 256, 128, 512, 8, 2)
        CAPACITY_RATIO = 1.05
        key = jax.random.key(seed)
        k0, k1, k2, k3 = jax.random.split(key, 4)
        x = jax.random.normal(k0, (B, S, D), jnp.float32)
        Wg = jax.random.normal(k1, (D, E), jnp.float32) * 0.02
        W1 = jax.random.normal(k2, (E, D, H), jnp.float32) * 0.02
        b1 = jnp.zeros((E, H), jnp.float32)
        W2 = jax.random.normal(k3, (E, H, D), jnp.float32) * 0.02
        b2 = jnp.zeros((E, D), jnp.float32)
        return {'x': x, 'Wg': Wg, 'W1': W1, 'b1': b1, 'W2': W2, 'b2': b2}
    _L0_ffn_in = _L0_ffn_setup()

    def _L1_attn_setup():
        import jax, jax.numpy as jnp
        import numpy as np
        EMBED_DIM = 128
        NUM_HEADS = 16
        HEAD_DIM = EMBED_DIM // NUM_HEADS
        WINDOW = 128
        key = jax.random.key(seed)
        ks = jax.random.split(key, 9)
        B, T, C = (1, 256, EMBED_DIM)
        s = 1.0 / np.sqrt(C)
        inp = {'x': jax.random.normal(ks[0], (B, T, C), dtype=jnp.float32), 'wq': jax.random.normal(ks[1], (C, C), dtype=jnp.float32) * s, 'bq': jnp.zeros((C,), dtype=jnp.float32), 'wk': jax.random.normal(ks[2], (C, C), dtype=jnp.float32) * s, 'bk': jnp.zeros((C,), dtype=jnp.float32), 'wv': jax.random.normal(ks[3], (C, C), dtype=jnp.float32) * s, 'bv': jnp.zeros((C,), dtype=jnp.float32), 'wo': jax.random.normal(ks[4], (C, C), dtype=jnp.float32) * s, 'bo': jnp.zeros((C,), dtype=jnp.float32)}
        return inp
    _L1_attn_in = _L1_attn_setup()

    def _L1_ffn_setup():
        import jax, jax.numpy as jnp
        import numpy as np
        B, S, H = (4, 256, 128)
        D_FF = 4 * H
        NUM_EXPERTS = 8
        TOP_K = 2
        key = jax.random.key(seed)
        ks = jax.random.split(key, 6)
        scale = 0.02
        return {'hidden_states': jax.random.normal(ks[0], (B, S, H), dtype=jnp.float32), 'w_router': jax.random.normal(ks[1], (NUM_EXPERTS, H), dtype=jnp.float32) * scale, 'w1': jax.random.normal(ks[2], (NUM_EXPERTS, D_FF, H), dtype=jnp.float32) * scale, 'b1': jnp.zeros((NUM_EXPERTS, D_FF), dtype=jnp.float32), 'w2': jax.random.normal(ks[3], (NUM_EXPERTS, H, D_FF), dtype=jnp.float32) * scale, 'b2': jnp.zeros((NUM_EXPERTS, H), dtype=jnp.float32)}
    _L1_ffn_in = _L1_ffn_setup()
    _d = {'L0_attn_x': _L0_attn_in['x'], 'L0_attn_q1_w': _L0_attn_in['q1_w'], 'L0_attn_q2_w': _L0_attn_in['q2_w'], 'L0_attn_k1_w': _L0_attn_in['k1_w'], 'L0_attn_k2_w': _L0_attn_in['k2_w'], 'L0_attn_v_w': _L0_attn_in['v_w'], 'L0_attn_c_w': _L0_attn_in['c_w'], 'L0_attn_lambda_q1': _L0_attn_in['lambda_q1'], 'L0_attn_lambda_k1': _L0_attn_in['lambda_k1'], 'L0_attn_lambda_q2': _L0_attn_in['lambda_q2'], 'L0_attn_lambda_k2': _L0_attn_in['lambda_k2'], 'L0_ffn_Wg': _L0_ffn_in['Wg'], 'L0_ffn_W1': _L0_ffn_in['W1'], 'L0_ffn_b1': _L0_ffn_in['b1'], 'L0_ffn_W2': _L0_ffn_in['W2'], 'L0_ffn_b2': _L0_ffn_in['b2'], 'L1_attn_wq': _L1_attn_in['wq'], 'L1_attn_bq': _L1_attn_in['bq'], 'L1_attn_wk': _L1_attn_in['wk'], 'L1_attn_bk': _L1_attn_in['bk'], 'L1_attn_wv': _L1_attn_in['wv'], 'L1_attn_bv': _L1_attn_in['bv'], 'L1_attn_wo': _L1_attn_in['wo'], 'L1_attn_bo': _L1_attn_in['bo'], 'L1_ffn_w_router': _L1_ffn_in['w_router'], 'L1_ffn_w1': _L1_ffn_in['w1'], 'L1_ffn_b1': _L1_ffn_in['b1'], 'L1_ffn_w2': _L1_ffn_in['w2'], 'L1_ffn_b2': _L1_ffn_in['b2']}
    _x0 = _d['L0_attn_x']
    _d['L0_attn_x'] = jax.random.normal(jax.random.fold_in(jax.random.key(seed), 1), (16, 256, 128), dtype=_x0.dtype)
    del _x0
    return _d

def reference(L0_attn_x, L0_attn_q1_w, L0_attn_q2_w, L0_attn_k1_w, L0_attn_k2_w, L0_attn_v_w, L0_attn_c_w, L0_attn_lambda_q1, L0_attn_lambda_k1, L0_attn_lambda_q2, L0_attn_lambda_k2, L0_ffn_Wg, L0_ffn_W1, L0_ffn_b1, L0_ffn_W2, L0_ffn_b2, L1_attn_wq, L1_attn_bq, L1_attn_wk, L1_attn_bk, L1_attn_wv, L1_attn_bv, L1_attn_wo, L1_attn_bo, L1_ffn_w_router, L1_ffn_w1, L1_ffn_b1, L1_ffn_w2, L1_ffn_b2):

    def _L0_attn_ref(x, q1_w, q2_w, k1_w, k2_w, v_w, c_w, lambda_q1, lambda_k1, lambda_q2, lambda_k2):
        import jax, jax.numpy as jnp
        import numpy as np
        import math
        N_EMBD = 128
        N_HEAD = 16
        HEAD = N_EMBD // N_HEAD
        LAMBDA_INIT = 0.8 - 0.6 * math.exp(-0.3 * (4 - 1))
        EPS = 1e-05
        B, T, C = x.shape
        H, hs = (N_HEAD, HEAD)

        def heads(w, d):
            return (x @ w).reshape(B, T, H, d).transpose(0, 2, 1, 3)
        q1 = heads(q1_w, hs)
        q2 = heads(q2_w, hs)
        k1 = heads(k1_w, hs)
        k2 = heads(k2_w, hs)
        v = heads(v_w, 2 * hs)
        scale = 1.0 / math.sqrt(hs)
        causal = jnp.tril(jnp.ones((T, T), dtype=bool))
        neg = jnp.float32(-jnp.inf)
        att1 = jnp.einsum('bhqd,bhkd->bhqk', q1, k1) * scale
        att2 = jnp.einsum('bhqd,bhkd->bhqk', q2, k2) * scale
        att1 = jax.nn.softmax(jnp.where(causal, att1, neg), axis=-1)
        att2 = jax.nn.softmax(jnp.where(causal, att2, neg), axis=-1)
        lam1 = jnp.exp(jnp.sum(lambda_q1 * lambda_k1, axis=-1))
        lam2 = jnp.exp(jnp.sum(lambda_q2 * lambda_k2, axis=-1))
        lam = (lam1 - lam2 + LAMBDA_INIT)[None, :, None, None]
        att = att1 - lam * att2
        y = jnp.einsum('bhqk,bhkd->bhqd', att, v)
        mu = jnp.mean(y, axis=-1, keepdims=True)
        var = jnp.mean(jnp.square(y - mu), axis=-1, keepdims=True)
        y = (y - mu) / jnp.sqrt(var + EPS)
        y = y * (1.0 - LAMBDA_INIT)
        y = y.transpose(0, 2, 1, 3).reshape(B, T, 2 * C)
        return y @ c_w

    def _L0_ffn_ref(x, Wg, W1, b1, W2, b2):
        import math
        import jax, jax.numpy as jnp
        import numpy as np
        B, S, D, H, E, K = (4, 256, 128, 512, 8, 2)
        CAPACITY_RATIO = 1.05
        b, s, d = x.shape
        e = Wg.shape[1]
        n = b * s
        cap = int(math.ceil(n * K / e * CAPACITY_RATIO))
        xf = x.reshape(n, d)
        probs = jax.nn.softmax(xf @ Wg, axis=-1)
        topv, topi = jax.lax.top_k(probs, K)
        gates = topv / jnp.sum(topv, axis=-1, keepdims=True)
        eidx = topi.reshape(-1)
        oh = jax.nn.one_hot(eidx, e, dtype=jnp.int32)
        pos = jnp.sum(jnp.cumsum(oh, axis=0) * oh, axis=-1) - 1
        keep = pos < cap
        dest = jnp.where(keep, eidx * cap + pos, e * cap)
        xr = jnp.repeat(xf, K, axis=0)
        buf = jnp.zeros((e * cap + 1, d), x.dtype).at[dest].set(xr)
        expert_in = buf[:e * cap].reshape(e, cap, d)
        h = jax.nn.gelu(jnp.einsum('ecd,edh->ech', expert_in, W1) + b1[:, None, :])
        y = jnp.einsum('ech,ehd->ecd', h, W2) + b2[:, None, :]
        yf = jnp.concatenate([y.reshape(e * cap, d), jnp.zeros((1, d), y.dtype)], axis=0)
        gathered = yf[dest]
        w = (gates.reshape(-1) * keep.astype(gates.dtype))[:, None]
        out = (gathered * w).reshape(n, K, d).sum(axis=1).reshape(b, s, d)
        return out

    def _L1_attn_ref(x, wq, bq, wk, bk, wv, bv, wo, bo):
        import jax, jax.numpy as jnp
        import numpy as np
        EMBED_DIM = 128
        NUM_HEADS = 16
        HEAD_DIM = EMBED_DIM // NUM_HEADS
        WINDOW = 128
        B, T, C = x.shape
        H, D, W = (NUM_HEADS, HEAD_DIM, WINDOW)

        def proj(w, b):
            return (x @ w.T + b).reshape(B, T, H, D).transpose(0, 2, 1, 3)
        q = proj(wq, bq)
        k = proj(wk, bk)
        v = proj(wv, bv)
        idx = jnp.arange(T)[:, None] + jnp.arange(W)[None, :] - (W - 1)
        valid = idx >= 0
        idxc = jnp.clip(idx, 0, T - 1)
        kw = k[:, :, idxc]
        vw = v[:, :, idxc] * valid[None, None, :, :, None]
        scores = jnp.einsum('bhtd,bhtwd->bhtw', q, kw)
        scores = jnp.where(valid[None, None], scores, 0.0) / np.sqrt(D)
        attn = jax.nn.softmax(scores, axis=-1)
        ctx = jnp.einsum('bhtw,bhtwd->bhtd', attn, vw)
        out = ctx.transpose(0, 2, 1, 3).reshape(B, T, C)
        return out @ wo.T + bo

    def _L1_ffn_ref(hidden_states, w_router, w1, b1, w2, b2):
        import jax, jax.numpy as jnp
        import numpy as np
        B, S, H = (4, 256, 128)
        D_FF = 4 * H
        NUM_EXPERTS = 8
        TOP_K = 2
        Bc, Sc, Hc = hidden_states.shape
        E = w_router.shape[0]
        dtype = hidden_states.dtype
        router_logits = jnp.einsum('bsh,eh->bse', hidden_states, w_router)
        topk_values, topk_indices = jax.lax.top_k(router_logits, TOP_K)
        topk_weights = jax.nn.softmax(topk_values.astype(jnp.float32), axis=-1).astype(dtype)
        combine = jnp.sum(jax.nn.one_hot(topk_indices, E, dtype=dtype) * topk_weights[..., None], axis=-2)
        flat = hidden_states.reshape(-1, Hc)
        cw = combine.reshape(-1, E)
        mixed = jnp.zeros_like(flat)
        for e in range(E):
            h1 = jax.nn.gelu(flat @ w1[e].T + b1[e], approximate=False)
            mixed = mixed + cw[:, e:e + 1] * (h1 @ w2[e].T + b2[e])
        return mixed.reshape(Bc, Sc, Hc)
    x = L0_attn_x
    xn = _layernorm(x, axis=-1)
    s = _L0_attn_ref(xn, L0_attn_q1_w, L0_attn_q2_w, L0_attn_k1_w, L0_attn_k2_w, L0_attn_v_w, L0_attn_c_w, L0_attn_lambda_q1, L0_attn_lambda_k1, L0_attn_lambda_q2, L0_attn_lambda_k2)
    g = _silu(_L0_ffn_ref(xn, L0_ffn_Wg, L0_ffn_W1, L0_ffn_b1, L0_ffn_W2, L0_ffn_b2))
    x = x + s * g
    xn = _layernorm(x, axis=-1)
    s = _L1_attn_ref(xn, L1_attn_wq, L1_attn_bq, L1_attn_wk, L1_attn_bk, L1_attn_wv, L1_attn_bv, L1_attn_wo, L1_attn_bo)
    g = _silu(_L1_ffn_ref(xn, L1_ffn_w_router, L1_ffn_w1, L1_ffn_b1, L1_ffn_w2, L1_ffn_b2))
    x = x + s * g
    return x

_drawn_inputs = setup_inputs


def setup_inputs(seed=0):
    import zlib

    import numpy as np

    out = dict(_drawn_inputs(seed))
    spreads = {'L0_ffn_b1': (0.0, 0.8),
     'L0_ffn_b2': (0.0, 0.518),
     'L1_attn_bq': (0.0, 0.8),
     'L1_attn_bk': (0.0, 2.0),
     'L1_attn_bv': (0.0, 0.8),
     'L1_attn_bo': (0.0, 2.0),
     'L1_ffn_b1': (0.0, 0.8),
     'L1_ffn_b2': (0.0, 0.8)}
    factors = {'L0_attn_q1_w': 3.797,
     'L0_attn_q2_w': 6.199,
     'L0_attn_k1_w': 3.77,
     'L0_attn_k2_w': 6.173,
     'L0_attn_v_w': 3.144,
     'L0_attn_c_w': 3.125,
     'L0_attn_lambda_q1': 8.0,
     'L0_attn_lambda_k1': 8.0,
     'L0_attn_lambda_q2': 8.0,
     'L0_attn_lambda_k2': 8.0,
     'L0_ffn_Wg': 3.59,
     'L0_ffn_W1': 6.743,
     'L0_ffn_W2': 6.125,
     'L1_attn_wq': 8.0,
     'L1_attn_wk': 8.0,
     'L1_attn_wv': 8.0,
     'L1_attn_wo': 7.347,
     'L1_ffn_w_router': 7.532,
     'L1_ffn_w1': 8.0,
     'L1_ffn_w2': 8.0}
    for name, (base, spread) in spreads.items():
        noise = np.random.default_rng([zlib.crc32(name.encode()), seed]).standard_normal(out[name].shape)
        drawn = base * np.exp(spread * noise) if base else spread * noise
        out[name] = jnp.asarray(drawn.astype(out[name].dtype))
    for name, factor in factors.items():
        out[name] = (out[name] * factor).astype(out[name].dtype)
    return out
```

```python
from contextlib import ExitStack
import math

import concourse.bass as bass
from concourse import mybir

ALU = mybir.AluOpType
ACT = mybir.ActivationFunctionType
AX = mybir.AxisListType
F32 = mybir.dt.float32
BF16 = mybir.dt.bfloat16

P = 128
BATCH, SEQ, C = 16, 256, 128
NTOK = BATCH * SEQ
NT = NTOK // P
QB = SEQ // P
HEADS = 16
HD = C // HEADS
EXPERTS, HIDDEN, TOPK = 8, 512, 2
HB = HIDDEN // P
CAP = int(math.ceil(NTOK * TOPK / EXPERTS * 1.05))
LAMBDA_INIT = 0.8 - 0.6 * math.exp(-0.3 * (4 - 1))
EPS = 1e-5
SCALE = 1.0 / math.sqrt(HD)
MASKED = -1.0e30
BELOW = -3.0e38

Q_PIECE = (0, 0, 0, 1, 1, 2)
K_PIECE = (0, 1, 2, 0, 1, 0)
RUNS = ((0, 3), (3, 2), (5, 1))
SHIFT_ROW = len(Q_PIECE) * HD
NPIECE = 3


class Resident:
    pass


def build_constants(nc, R, D):
    with ExitStack() as ctx:
        sb = lambda name, shape, dt=F32: ctx.enter_context(nc.sbuf_tensor(f"const_{name}", shape, dt))
        lam4, lam_sum, lam_row_t = sb("lam4", [1, 4, C]), sb("lam_sum", [1, 2, HEADS]), sb("lam_row", [1, HEADS])
        ones_bf, zeros_bf = sb("ones_bf", [NPIECE, HEADS * SEQ], BF16), sb("zeros_bf", [NPIECE, HEADS * SEQ], BF16)
        m32 = sb("m32", [P, 4, P])
        loads = ctx.enter_context(nc.semaphore("const_loads"))
        lam_loads = ctx.enter_context(nc.semaphore("lam_loads"))
        filled = ctx.enter_context(nc.semaphore("const_filled"))
        cut = ctx.enter_context(nc.semaphore("const_cut"))
        lam_chain = ctx.enter_context(nc.semaphore("lam_chain"))
        lam_exp = ctx.enter_context(nc.semaphore("lam_exp"))
        lam_row = ctx.enter_context(nc.semaphore("lam_row"))
        lam_spread = ctx.enter_context(nc.semaphore("lam_spread"))
        ones_rows = ctx.enter_context(nc.semaphore("ones_rows"))
        block = ctx.enter_context(nc.Block())
        n_loads = [0]

        @block.sync
        def _(sp):
            def load(dst, src):
                n_loads[0] += 1
                sp.dma_start(dst, src).then_inc(loads, 16)
            for t, name in enumerate(("L0_attn_lambda_q1", "L0_attn_lambda_k1", "L0_attn_lambda_q2", "L0_attn_lambda_k2")):
                sp.dma_start(lam4[0:1, t, :], D[name]).then_inc(lam_loads, 16)
            for c in range(4):
                load(R.x[:, c * 8:(c + 1) * 8, :], D["L0_attn_x"].rearrange("(t p) d -> p t d", p=P)[:, c * 8:(c + 1) * 8, :])
            for t, name in enumerate(("L0_attn_q1_w", "L0_attn_k1_w", "L0_attn_q2_w", "L0_attn_k2_w")):
                load(R.wqk[0][:, t, :], D[name])
            load(R.wv[0][:], D["L0_attn_v_w"])
            load(R.wo[0][:], D["L0_attn_c_w"].rearrange("(b p) d -> p b d", p=P))
            load(R.wqk[1][:, 0, :], D["L1_attn_wq"])
            load(R.wqk[1][:, 1, :], D["L1_attn_wk"])
            load(R.wv[1][:], D["L1_attn_wv"])
            load(R.wo[1][:, 0, :], D["L1_attn_wo"])
            load(R.bqk[:, 0:1], D["L1_attn_bq"])
            load(R.bqk[:, 1:2], D["L1_attn_bk"])
            load(R.bv[:], D["L1_attn_bv"])
            load(R.bo[:], D["L1_attn_bo"])
            load(R.wr[0][:], D["L0_ffn_Wg"])
            load(R.wr[1][:], D["L1_ffn_w_router"])
            load(R.b2[0][:], D["L0_ffn_b2"])
            load(R.b2[1][:], D["L1_ffn_b2"])
            sp.wait_ge(ones_rows, 1)
            for par in range(2):
                for t in (1, 3):
                    load(R.stack[par][SHIFT_ROW:SHIFT_ROW + NPIECE, t, :, :], ones_bf[:].rearrange("p (h t) -> p h t", h=HEADS))
            load(D["zeros"], zeros_bf[:])
            sp.wait_ge(loads, 16 * n_loads[0])

        @block.gpsimd
        def _(pool):
            nc.gpsimd.memset(R.ident[:], 0.0).then_inc(filled, 1)
            nc.gpsimd.memset(R.ones[:], 1.0).then_inc(filled, 1)
            nc.gpsimd.memset(R.before[:], 1.0).then_inc(filled, 1)
            nc.gpsimd.memset(m32[:], 0.0).then_inc(filled, 1)
            pool.wait_ge(filled, 4)
            nc.gpsimd.affine_select(out=R.ident[:], in_=R.ident[:], compare_op=ALU.not_equal, fill=1.0, base=0,
                                    pattern=[[-1, P]], channel_multiplier=1).then_inc(cut, 1)
            nc.gpsimd.affine_select(out=R.before[:], in_=R.before[:], compare_op=ALU.is_gt, fill=0.0, base=0,
                                    pattern=[[1, P]], channel_multiplier=-1).then_inc(cut, 1)
            nc.gpsimd.affine_select(out=m32[:, 0, :], in_=m32[:, 0, :], compare_op=ALU.is_ge, fill=MASKED, base=0,
                                    pattern=[[-1, P]], channel_multiplier=1).then_inc(cut, 1)
            nc.gpsimd.affine_select(out=m32[:, 1, :], in_=m32[:, 1, :], compare_op=ALU.is_ge, fill=MASKED, base=0,
                                    pattern=[[1, P]], channel_multiplier=-1).then_inc(cut, 1)
            nc.gpsimd.affine_select(out=m32[:, 2, :], in_=m32[:, 2, :], compare_op=ALU.is_gt, fill=MASKED, base=0,
                                    pattern=[[1, P]], channel_multiplier=-1).then_inc(cut, 1)
            nc.gpsimd.affine_select(out=m32[:, 3, :], in_=m32[:, 3, :], compare_op=ALU.is_gt, fill=MASKED, base=0,
                                    pattern=[[-1, P]], channel_multiplier=1).then_inc(cut, 1)
            pool.wait_ge(cut, 6)
            nc.gpsimd.tensor_copy(R.ident_bf[:], R.ident[:])
            D0q, D0k, Wq, Wk = (m32[:, i, :] for i in range(4))
            for j in range(4):
                nc.gpsimd.tensor_copy(R.mask_diag_q[:, j, :], D0q)
                nc.gpsimd.tensor_copy(R.mask_diag_k[:, j, :], D0k)
            for j in range(2):
                nc.gpsimd.tensor_copy(R.mask_late_q[1][:, j, 0, :], Wq)
                nc.gpsimd.tensor_copy(R.mask_late_q[0][:, j, 1, :], D0q)
                nc.gpsimd.tensor_copy(R.mask_late_q[1][:, j, 1, :], D0q)
                nc.gpsimd.tensor_copy(R.mask_early_k[0][:, j, 0, :], D0k)
                nc.gpsimd.tensor_copy(R.mask_early_k[1][:, j, 0, :], D0k)
                nc.gpsimd.tensor_copy(R.mask_early_k[1][:, j, 1, :], Wk)
            for e in range(EXPERTS):
                nc.gpsimd.memset(R.rank[:, e:e + 1], float(EXPERTS - e))
            nc.gpsimd.iota(R.outside[:], [[0, 1]], base=P - 1, channel_multiplier=-1, allow_small_or_imprecise_dtypes=True).then_inc(cut, 1)
            pool.wait_ge(cut, 7)
            nc.gpsimd.tensor_scalar(R.no_outside[:], R.outside[:], 0.5, BELOW, ALU.is_lt, ALU.mult)

        @block.vector
        def _(dve):
            nc.vector.memset(zeros_bf[:], 0.0)
            nc.vector.memset(ones_bf[:], 1.0)
            for j in range(2):
                nc.vector.memset(R.mask_early_k[0][:, j, 1, :], 0.0)
                nc.vector.memset(R.mask_late_q[0][:, j, 0, :], 0.0)
            for par in range(2):
                for t in range(4):
                    last = nc.vector.memset(R.stack[par][:, t, :, :], 0.0)
            last.then_inc(ones_rows, 1)
            dve.wait_ge(lam_loads, 16 * 4)
            nc.vector.tensor_tensor(lam4[0:1, 0, :], lam4[0:1, 0, :], lam4[0:1, 1, :], ALU.mult).then_inc(lam_chain, 1)
            nc.vector.tensor_tensor(lam4[0:1, 2, :], lam4[0:1, 2, :], lam4[0:1, 3, :], ALU.mult).then_inc(lam_chain, 1)
            dve.wait_ge(lam_chain, 2)
            for i in range(2):
                nc.vector.tensor_reduce(lam_sum[0:1, i, :], lam4[0:1, 2 * i, :].rearrange("p (h d) -> p h d", d=HD),
                                        AX.X, ALU.add).then_inc(lam_chain, 1)
            dve.wait_ge(lam_exp, 1)
            nc.vector.tensor_tensor(lam_row_t[0:1, :], lam_sum[0:1, 0, :], lam_sum[0:1, 1, :], ALU.subtract).then_inc(lam_chain, 1)
            dve.wait_ge(lam_chain, 5)
            nc.vector.tensor_scalar(lam_row_t[0:1, :], lam_row_t[0:1, :], LAMBDA_INIT, None, ALU.add).then_inc(lam_row, 1)
            dve.wait_ge(lam_spread, 1)
            nc.vector.tensor_copy(R.lam[:], R.ps[:, 0, 0:HEADS])

        @block.scalar
        def _(act):
            act.wait_ge(lam_chain, 4)
            nc.scalar.activation(lam_sum[0:1, :, :], lam_sum[0:1, :, :], ACT.Exp).then_inc(lam_exp, 1)

        @block.tensor
        def _(pe):
            pe.wait_ge(lam_row, 1)
            pe.wait_ge(filled, 4)
            nc.tensor.matmul(R.ps[:, 0, 0:HEADS], R.ones[0:1, :], lam_row_t[0:1, :], start=True, stop=True).then_inc(lam_spread, 1)


def build_layernorm(nc, R, layer):
    CH = 4
    TC = NT // CH
    with ExitStack() as ctx:
        sem = lambda name: ctx.enter_context(nc.semaphore(f"ln{layer}_{name}"))
        sb = lambda name, shape: ctx.enter_context(nc.sbuf_tensor(f"ln{layer}_{name}", shape, F32))
        xn = sb("xn", [P, NT, C])
        total = sb("total", [P, NT])
        mean = sb("mean", [P, NT])
        sq = sb("sq", [P, TC, C])
        var = sb("var", [P, NT])
        rstd = sb("rstd", [P, NT])
        half = sb("half", [P, TC])
        chain, centred, squared, var_ready, rstd_ready, xn_ready, turned, evacuated, gated, half_ready = (
            sem(n) for n in ("chain", "centred", "squared", "var_ready", "rstd_ready", "xn_ready", "turned", "evacuated", "gated", "half_ready"))
        block = ctx.enter_context(nc.Block())
        cs = [slice(c * TC, (c + 1) * TC) for c in range(CH)]
        wide = lambda a: a.unsqueeze(2).broadcast_to([P, TC, C])

        @block.vector
        def _(dve):
            n = [0]

            def link(ins):
                n[0] += 1
                ins.then_inc(chain, 1)
                dve.wait_ge(chain, n[0])

            def mean_of(c):
                if layer:
                    dve.wait_ge(gated, c + 1)
                    link(nc.vector.tensor_tensor(R.g[:, cs[c], :], R.g[:, cs[c], :], R.s[:, cs[c], :], ALU.mult))
                    link(nc.vector.tensor_tensor(R.x[:, cs[c], :], R.x[:, cs[c], :], R.g[:, cs[c], :], ALU.add))
                link(nc.vector.tensor_reduce(total[:, cs[c]], R.x[:, cs[c], :], AX.X, ALU.add))
                link(nc.vector.tensor_scalar(mean[:, cs[c]], total[:, cs[c]], 1.0 / C, None, ALU.mult))
                nc.vector.tensor_tensor(xn[:, cs[c], :], R.x[:, cs[c], :], wide(mean[:, cs[c]]), ALU.subtract).then_inc(centred, 1)

            def variance(c):
                dve.wait_ge(squared, c + 1)
                link(nc.vector.tensor_reduce(total[:, cs[c]], sq[:], AX.X, ALU.add))
                nc.vector.tensor_scalar(var[:, cs[c]], total[:, cs[c]], 1.0 / C, EPS, ALU.mult, ALU.add).then_inc(var_ready, 1)

            def scale(c):
                dve.wait_ge(rstd_ready, c + 1)
                nc.vector.tensor_tensor(xn[:, cs[c], :], xn[:, cs[c], :], wide(rstd[:, cs[c]]), ALU.mult).then_inc(xn_ready, 1)

            for c in range(CH):
                mean_of(c)
                variance(c)
                if c:
                    scale(c - 1)
            scale(CH - 1)

        @block.scalar
        def _(act):
            if layer:
                for c in range(CH):
                    nc.scalar.activation(R.g[:, cs[c], :], R.g[:, cs[c], :], ACT.Silu).then_inc(gated, 1)
            for c in range(CH):
                act.wait_ge(centred, c + 1)
                if c:
                    act.wait_ge(var_ready, c)
                nc.scalar.activation(sq[:], xn[:, cs[c], :], ACT.Square).then_inc(squared, 1)
            for i in range(NT // 4):
                act.wait_ge(turned, i + 1)
                nc.scalar.copy(R.xnT[:, i * 4 * P:(i + 1) * 4 * P], R.ps[:, i % 4, :]).then_inc(evacuated, 1)

        @block.gpsimd
        def _(pool):
            nc.gpsimd.memset(half[:], -0.5).then_inc(half_ready, 1)
            pool.wait_ge(half_ready, 1)
            for c in range(CH):
                pool.wait_ge(var_ready, c + 1)
                nc.gpsimd.tensor_tensor(rstd[:, cs[c]], var[:, cs[c]], half[:], ALU.pow).then_inc(rstd_ready, 1)

        @block.tensor
        def _(pe):
            for i in range(NT // 4):
                pe.wait_ge(xn_ready, (4 * i) // TC + 1)
                if i >= 4:
                    pe.wait_ge(evacuated, i - 3)
                for j in range(4):
                    last = nc.tensor.transpose(R.ps[:, i % 4, j * P:(j + 1) * P], xn[:, 4 * i + j, :], R.ident[:])
                last.then_inc(turned, 1)


def build_router(nc, R, layer):
    E = EXPERTS
    with ExitStack() as ctx:
        sem = lambda name: ctx.enter_context(nc.semaphore(f"rt{layer}_{name}"))
        sb = lambda name, shape: ctx.enter_context(nc.sbuf_tensor(f"rt{layer}_{name}", shape, F32))
        logits = sb("logits", [P, NT, E])
        rest = sb("rest", [P, NT, E])
        ranked = sb("ranked", [P, NT, E])
        first = sb("first", [P, NT, E])
        second = sb("second", [P, NT, E])
        best = sb("best", [P, 2, NT])
        top_rank = sb("top_rank", [P, NT])
        gap = sb("gap", [P, NT])
        gate = sb("gate", [P, 2, NT])
        chosen = sb("chosen", [P, NT, E])
        upto = sb("upto", [P, NT, E])
        place = sb("place", [P, NT, E])
        one_row = sb("one_row", [P, NT])
        cwT = sb("cwT", [E, NTOK])
        scored, chain, gap_ready, gap_exp, chosen_ready, counted, cw_ready, cwt_ready, cwt_copied, seeded, seed_copied = (
            sem(n) for n in ("scored", "chain", "gap_ready", "gap_exp", "chosen_ready", "counted", "cw_ready", "cwt_ready", "cwt_copied", "seeded", "seed_copied"))
        block = ctx.enter_context(nc.Block())
        wide = lambda a: a.unsqueeze(2).broadcast_to([P, NT, E])
        rank_w = R.rank[:, :].unsqueeze(1).broadcast_to([P, NT, E])
        flat = lambda a: a.rearrange("p t e -> p (t e)")

        @block.tensor
        def _(pe):
            for t in range(NT):
                last = nc.tensor.matmul(R.ps[:, 0, t * E:(t + 1) * E], R.xnT[:, t * P:(t + 1) * P], R.wr[layer][:], start=True, stop=True)
            last.then_inc(scored, 1)
            if layer == 0:
                pe.wait_ge(chosen_ready, 1)
                nc.tensor.matmul(R.ps[:, 1, 0:NT * E], R.before[:], flat(chosen[:]), start=True, stop=True)
                nc.tensor.matmul(R.ps[:, 2, 0:NT * E], R.ones[:], flat(chosen[:]), start=True, stop=True).then_inc(counted, 1)
            pe.wait_ge(cw_ready, 1)
            for i in range(NT // 4):
                if i >= 2:
                    pe.wait_ge(cwt_copied, i - 1)
                for j in range(4):
                    last = nc.tensor.transpose(R.ps[0:E, 3 + i % 2, j * P:(j + 1) * P], R.cw[:, 4 * i + j, :], R.ident[:])
                last.then_inc(cwt_ready, 1)
            for i in range(NT // 4):
                pe.wait_ge(cwt_copied, i + 1)
                if i >= 2:
                    pe.wait_ge(seed_copied, i - 1)
                for j in range(4):
                    t = 4 * i + j
                    last = nc.tensor.matmul(R.ps[:, 5 + i % 2, j * P:(j + 1) * P], cwT[:, t * P:(t + 1) * P], R.b2[layer][:], start=True, stop=True)
                last.then_inc(seeded, 1)

        @block.scalar
        def _(act):
            act.wait_ge(gap_ready, 1)
            nc.scalar.activation(gap[:], gap[:], ACT.Exp).then_inc(gap_exp, 1)
            for i in range(NT // 4):
                act.wait_ge(cwt_ready, i + 1)
                nc.scalar.copy(cwT[:, i * 4 * P:(i + 1) * 4 * P], R.ps[0:E, 3 + i % 2, :]).then_inc(cwt_copied, 1)

        @block.vector
        def _(dve):
            n = [0]

            def link(ins):
                n[0] += 1
                ins.then_inc(chain, 1)
                dve.wait_ge(chain, n[0])

            def pick(onehot, scores, k):
                link(nc.vector.tensor_reduce(best[:, k, :], scores[:], AX.X, ALU.max))
                link(nc.vector.tensor_tensor(ranked[:], scores[:], wide(best[:, k, :]), ALU.is_equal))
                link(nc.vector.tensor_tensor(ranked[:], ranked[:], rank_w, ALU.mult))
                link(nc.vector.tensor_reduce(top_rank[:], ranked[:], AX.X, ALU.max))
                link(nc.vector.tensor_tensor(onehot[:], ranked[:], wide(top_rank[:]), ALU.is_equal))

            dve.wait_ge(scored, 1)
            link(nc.vector.tensor_copy(flat(logits[:]), R.ps[:, 0, 0:NT * E]))
            pick(first, logits, 0)
            link(nc.vector.scalar_tensor_tensor(out=flat(rest[:]), in0=flat(first[:]), scalar=BELOW, in1=flat(logits[:]), op0=ALU.mult, op1=ALU.add))
            pick(second, rest, 1)
            nc.vector.tensor_tensor(gap[:], best[:, 1, :], best[:, 0, :], ALU.subtract).then_inc(gap_ready, 1)
            dve.wait_ge(gap_exp, 1)
            link(nc.vector.tensor_scalar(gate[:, 1, :], gap[:], 1.0, None, ALU.add))
            link(nc.vector.reciprocal(gate[:, 0, :], gate[:, 1, :]))
            link(nc.vector.tensor_tensor(gate[:, 1, :], gap[:], gate[:, 0, :], ALU.mult))
            if layer == 0:
                ins = nc.vector.tensor_tensor(chosen[:], first[:], second[:], ALU.add)
                ins.then_inc(chosen_ready, 1)
            link(nc.vector.tensor_tensor(first[:], first[:], wide(gate[:, 0, :]), ALU.mult))
            link(nc.vector.tensor_tensor(second[:], second[:], wide(gate[:, 1, :]), ALU.mult))
            cw_ins = nc.vector.tensor_tensor(R.cw[:], first[:], second[:], ALU.add)
            if layer == 0:
                link(cw_ins)
                link(nc.vector.memset(one_row[:], 1.0))
                dve.wait_ge(counted, 1)
                link(nc.vector.tensor_copy(flat(ranked[:]), R.ps[:, 2, 0:NT * E]))
                for e in range(E):
                    link(nc.vector.tensor_tensor_scan(upto[:, :, e], one_row[:], ranked[:, :, e], 0.0, ALU.mult, ALU.add))
                link(nc.vector.tensor_tensor(upto[:], upto[:], ranked[:], ALU.subtract))
                link(nc.vector.tensor_tensor(flat(place[:]), R.ps[:, 1, 0:NT * E], flat(upto[:]), ALU.add))
                link(nc.vector.tensor_scalar(place[:], place[:], float(CAP), None, ALU.is_lt))
                nc.vector.tensor_tensor(R.cw[:], R.cw[:], place[:], ALU.mult).then_inc(cw_ready, 1)
            else:
                cw_ins.then_inc(cw_ready, 1)
            for i in range(NT // 4):
                dve.wait_ge(seeded, i + 1)
                nc.vector.tensor_copy(R.g[:, 4 * i:4 * i + 4, :].rearrange("p t c -> p (t c)"), R.ps[:, 5 + i % 2, :]).then_inc(seed_copied, 1)


def build_experts(nc, R, D, layer):
    W1, B1, W2 = D[f"L{layer}_w1"], D[f"L{layer}_b1"], D[f"L{layer}_w2"]
    TOKS = 512
    NCH = NTOK // TOKS
    TT = TOKS // P
    NU = NCH * HB
    gelu = ACT.Gelu if layer else ACT.Gelu_apprx_tanh
    with ExitStack() as ctx:
        sem = lambda name: ctx.enter_context(nc.semaphore(f"ex{layer}_{name}"))
        sb = lambda name, shape: ctx.enter_context(nc.sbuf_tensor(f"ex{layer}_{name}", shape, F32))
        w1 = [sb(f"w1_{p}", [P, HIDDEN]) for p in range(2)]
        w2 = [sb(f"w2_{p}", [P, HB, C]) for p in range(2)]
        b1 = [sb(f"b1_{p}", [P, HB]) for p in range(2)]
        gate = [sb(f"gate_{p}", [P, NT]) for p in range(2)]
        hid = [sb(f"hid_{p}", [P, HB, TOKS]) for p in range(2)]
        arrived = [sem(f"arrived_{p}") for p in range(2)]
        added = [sem(f"added_{p}") for p in range(2)]
        up, act_done, down, gate_ready = (sem(n) for n in ("up", "act_done", "down", "gate_ready"))
        block = ctx.enter_context(nc.Block())

        def wait(eng, s, value):
            if not (isinstance(value, int) and value <= 0):
                eng.wait_ge(s, value)

        def schedule(eng, body):
            body(0)
            with eng.Fori(0, EXPERTS // 2 - 1) as i:
                body(i + 1)

        @block.sync
        def _(sp):
            def body(j):
                for par in range(2):
                    e = j * 2 + par
                    wait(sp, added[par], j * NCH)
                    sp.dma_start(w1[par][:], W1[bass.ds(e, 1)].rearrange("o p h -> (o p) h")).then_inc(arrived[par], 16)
                    sp.dma_start(w2[par][:], W2[bass.ds(e, 1)].rearrange("o (b p) d -> (o p) b d", p=P)).then_inc(arrived[par], 16)
                    sp.dma_start(b1[par][:], B1[bass.ds(e, 1)].rearrange("o p h -> (o p) h")).then_inc(arrived[par], 16)
            schedule(sp, body)

        @block.tensor
        def _(pe):
            def upward(j, par, c):
                for hb in range(HB):
                    wait(pe, act_done, j * (2 * NU) + (par * NU + (c * HB + hb - (HB - 1) if c else 0)))
                    nc.tensor.matmul(R.ps[:, hb, :], w1[par][:, hb * P:(hb + 1) * P], R.xnT[:, c * TOKS:(c + 1) * TOKS],
                                     start=True, stop=True).then_inc(up, 1)

            def downward(j, par, c):
                wait(pe, act_done, j * (2 * NU) + (par * NU + (c + 1) * HB))
                if c >= 2:
                    wait(pe, added[par], j * NCH + (c - 1))
                elif par:
                    wait(pe, added[0], j * NCH + NCH)
                else:
                    wait(pe, added[1], j * NCH)
                for tt in range(TT):
                    for hb in range(HB):
                        last = nc.tensor.matmul(R.ps[:, 4 + c % 2, tt * P:(tt + 1) * P], hid[c % 2][:, hb, tt * P:(tt + 1) * P],
                                                w2[par][:, hb, :], start=(hb == 0), stop=(hb == HB - 1))
                last.then_inc(down, 1)

            def body(j):
                for par in range(2):
                    wait(pe, arrived[par], j * 48 + 48)
                    for c in range(NCH + 1):
                        if c < NCH:
                            upward(j, par, c)
                        if c:
                            downward(j, par, c - 1)
            schedule(pe, body)

        @block.scalar
        def _(act):
            def body(j):
                for par in range(2):
                    wait(act, arrived[par], j * 48 + 48)
                    for c in range(NCH):
                        wait(act, down, j * (2 * NCH) + (par * NCH + max(c - 1, 0)))
                        for hb in range(HB):
                            wait(act, up, j * (2 * NU) + (par * NU + c * HB + hb + 1))
                            nc.scalar.activation(hid[c % 2][:, hb, :], R.ps[:, hb, :], gelu, bias=b1[par][:, hb:hb + 1]).then_inc(act_done, 1)
            schedule(act, body)

        @block.vector
        def _(dve):
            def body(j):
                for par in range(2):
                    nc.vector.tensor_copy(gate[par][:], R.cw[:, :, bass.ds(j * 2 + par, 1)].rearrange("p t o -> p (t o)")).then_inc(gate_ready, 1)
                    wait(dve, gate_ready, j * 2 + (par + 1))
                    for c in range(NCH):
                        wait(dve, down, j * (2 * NCH) + (par * NCH + c + 1))
                        for tt in range(TT):
                            t = c * TT + tt
                            last = nc.vector.scalar_tensor_tensor(out=R.g[:, t, :], in0=R.ps[:, 4 + c % 2, tt * P:(tt + 1) * P],
                                                                  scalar=gate[par][:, t:t + 1], in1=R.g[:, t, :], op0=ALU.mult, op1=ALU.add)
                        last.then_inc(added[par], 1)
            schedule(dve, body)


def build_attention(nc, R, D, layer):
    A = 2 if layer == 0 else 1
    T = 2 * A
    VD = HD * (2 if layer == 0 else 1)
    VW = VD + 1
    DV = HEADS * VD
    DB = DV // P
    UNITS = 6 * A
    GROUPS = 2 * A
    USES = 6
    FRONT_USES = 4
    LOADS = (len(RUNS) * T + A) * 16
    LAST = BATCH - 1
    with ExitStack() as ctx:
        sem = lambda name: ctx.enter_context(nc.semaphore(f"at{layer}_{name}"))

        def sb(name, shape, dt=F32):
            return ctx.enter_context(nc.sbuf_tensor(f"at{layer}_{name}", shape, dt))

        xb = [sb(f"xb{p}", [P, SEQ]) for p in range(2)]
        whole = sb("whole", [P, T, SEQ])
        residue = sb("residue", [P, T, SEQ])
        pieces = sb("pieces", [P, T, NPIECE, SEQ], BF16)
        v_tiles = [sb(f"v{p}", [P, QB, HEADS * VW]) for p in range(2)]
        maxima = sb("maxima", [P, QB, A * HEADS])
        shift = [sb(f"shift{p}", [P, QB, A * HEADS]) for p in range(2)]
        shift_t = sb("shift_t", [A * HEADS, SEQ])
        shift_r = sb("shift_r", [A * HEADS, SEQ])
        shift_p = sb("shift_p", [A * HEADS, NPIECE, SEQ], BF16)
        probs = sb("probs", [P, 2, 3, 1024])
        rsum = sb("rsum", [P, QB, HEADS])
        out_rows = sb("out_rows", [P, QB, DV])
        yT = sb("yT", [P, DB, SEQ])
        if layer == 0:
            y = [sb(f"y{a}", [P, QB, HEADS, VD]) for a in range(A)]
            sq = sb("sq", [P, QB, HEADS, VD])
            stat = sb("stat", [P, QB * HEADS])
            rstd = sb("rstd", [P, QB * HEADS])
            half = sb("half", [P, QB * HEADS])
        else:
            zero_exp = [sb(f"zero_exp{p}", [P, HEADS]) for p in range(2)]

        passed = sem("passed")
        v_ones = sem("v_ones")
        xb_ready = sem("xb_ready")
        g_full, g_free = sem("g_full"), sem("g_free")
        residue_ready = sem("residue_ready")
        middle_ready = sem("middle_ready")
        pieces_ready = sem("pieces_ready")
        pieces_out = sem("pieces_out")
        stacked = sem("stacked")
        s_full, s_free = sem("s_full"), sem("s_free")
        max_ready = sem("max_ready")
        shift_ready = sem("shift_ready")
        shift_chain = sem("shift_chain")
        shift_p_ready = sem("shift_p_ready")
        shift_out, shift_in = sem("shift_out"), sem("shift_in")
        t_full, t_free = sem("t_full"), sem("t_free")
        weighed = sem("weighed")
        y_chain = sem("y_chain")
        rows_ready = sem("rows_ready")
        y_free = sem("y_free") if layer == 0 else rows_ready
        norm_chain = sem("norm_chain")
        rstd_ready = sem("rstd_ready")
        half_ready = sem("half_ready")
        zero_ready = sem("zero_ready")
        block = ctx.enter_context(nc.Block())

        stack = R.stack
        v = [vt[:].rearrange("p k (h d) -> p k h d", d=VW) for vt in v_tiles]
        G = [R.ps[:, i, :] for i in range(2)]
        unit = [R.ps[:, 2 + 2 * u:4 + 2 * u, :] for u in range(2)]
        Y = R.ps[:, 6:8, 0:HEADS * VW].rearrange("p q (h d) -> p q h d", d=VW)
        scr, mscr = D["scratch_pieces"], D["scratch_shift"]

        def wait(eng, s, value):
            if not (isinstance(value, int) and value <= 0):
                eng.wait_ge(s, value)

        def lone_wait(eng, s, value):
            if not (isinstance(value, int) and value <= 0):
                eng.wait_ge(s, value)
                eng.sem_inc(passed, 1)

        def use(step, k):
            if isinstance(step, int) and step == -1:
                return {0: 0, 1: 1, 2: 2, 4: 3}[k]
            if isinstance(step, int) and step == LAST:
                return FRONT_USES + USES * LAST + {3: 0, 5: 1}[k]
            return step * USES + (FRONT_USES + k)

        def bank_of(step, k):
            edge = isinstance(step, int) and step in (-1, LAST)
            return G[(use(step, k) if edge else k) % 2]

        def schedule(eng, body):
            body(-1, 1)
            body(0, 0)
            with eng.Fori(0, (LAST - 1) // 2) as j:
                body(j * 2 + 1, 1)
                body(j * 2 + 2, 0)
            body(LAST, 1)

        def has_front(step):
            return not (isinstance(step, int) and step == LAST)

        def has_back(step):
            return not (isinstance(step, int) and step == -1)

        @block.gpsimd
        def _(pool):
            def copy_tokens(b, p):
                nc.gpsimd.tensor_copy(xb[p][:], R.xnT[:, bass.ds(b * SEQ, SEQ)]).then_inc(xb_ready, 1)

            def split(b):
                lone_wait(pool, residue_ready, b + 1)
                nc.gpsimd.tensor_copy(pieces[:, :, 1, :], residue[:]).then_inc(middle_ready, 1)
                pool.wait_ge(middle_ready, b + 1)
                nc.gpsimd.tensor_tensor(pieces[:, :, 2, :], residue[:], pieces[:, :, 1, :], ALU.subtract).then_inc(pieces_ready, 1)

            def split_shift(step, b):
                pool.wait_ge(g_free, use(step, 4) + 1)
                nc.gpsimd.tensor_tensor(shift_r[:], shift_t[:], shift_p[:, 0, :], ALU.subtract).then_inc(shift_chain, 1)
                lone_wait(pool, shift_chain, b * 2 + 1)
                nc.gpsimd.tensor_copy(shift_p[:, 1, :], shift_r[:]).then_inc(shift_chain, 1)
                pool.wait_ge(shift_chain, b * 2 + 2)
                nc.gpsimd.tensor_tensor(shift_p[:, 2, :], shift_r[:], shift_p[:, 1, :], ALU.subtract).then_inc(shift_p_ready, 1)

            def head_norm(b):
                LINKS = 5 + 2 * 4
                n = [0]

                def link(ins):
                    n[0] += 1
                    ins.then_inc(norm_chain, 1)
                    lone_wait(pool, norm_chain, b * LINKS + n[0])
                y0, y1, sqv = (t[:].rearrange("p q h d -> p (q h) d") for t in (*y, sq))
                wide = lambda a: a.unsqueeze(2).broadcast_to([P, QB * HEADS, VD])

                def add_up(values):
                    w = VD // 2
                    while w:
                        dst = sqv[:, :, 0:w] if w > 1 else stat[:].unsqueeze(2)
                        link(nc.gpsimd.tensor_tensor(dst, values[:, :, 0:w], values[:, :, w:2 * w], ALU.add))
                        values, w = sqv, w // 2

                lone_wait(pool, y_free, (b + 1) * A)
                link(nc.gpsimd.tensor_tensor(y0, y0, y1, ALU.subtract))
                add_up(y0)
                link(nc.gpsimd.tensor_scalar(stat[:], stat[:], 1.0 / VD, None, ALU.mult))
                link(nc.gpsimd.tensor_tensor(y0, y0, wide(stat[:]), ALU.subtract))
                link(nc.gpsimd.tensor_tensor(sqv, y0, y0, ALU.mult))
                add_up(sqv)
                k2 = (1.0 - LAMBDA_INIT) ** -2
                link(nc.gpsimd.tensor_scalar(stat[:], stat[:], k2 / VD, k2 * EPS, ALU.mult, ALU.add))
                assert n[0] == LINKS
                nc.gpsimd.tensor_tensor(rstd[:], stat[:], half[:], ALU.pow).then_inc(rstd_ready, 1)
                lone_wait(pool, rstd_ready, b + 1)
                lone_wait(pool, g_full, b * USES + 2)
                nc.gpsimd.tensor_tensor(out_rows[:].rearrange("p q (h d) -> p (q h) d", d=VD), y0, wide(rstd[:]), ALU.mult).then_inc(rows_ready, 1)

            if layer == 0:
                nc.gpsimd.memset(half[:], -0.5).then_inc(half_ready, 1)
                pool.wait_ge(half_ready, 1)
            for vt in v_tiles:
                nc.gpsimd.memset(vt[:], 1.0).then_inc(v_ones, 1)

            def body(step, par):
                if has_front(step):
                    copy_tokens(step + 1, 1 - par)
                    split(step + 1)
                if has_back(step) and layer == 0:
                    head_norm(step)
                if has_front(step):
                    split_shift(step, step + 1)
            schedule(pool, body)

        @block.sync
        def _(sp):
            def body(step, par):
                if not has_front(step):
                    return
                b, p = step + 1, 1 - par
                lone_wait(sp, stacked, (step + 1) * LOADS)
                lone_wait(sp, pieces_ready, b + 1)
                sp.dma_start(scr.rearrange("t c p s -> p t c s")[:, 0:T], pieces[:]).then_inc(pieces_out, 16)
                lone_wait(sp, pieces_out, b * 16 + 16)
                lone_wait(sp, t_full, step * UNITS)
                for t in range(T):
                    which = K_PIECE if t % 2 else Q_PIECE
                    for first, n in RUNS:
                        piece = scr[t, which[first]]
                        src = bass.AP(piece.tensor, piece.offset, [[C * SEQ if t % 2 else 0, n], [HEADS * SEQ, HD], [1, HEADS * SEQ]])
                        sp.dma_start(stack[p][first * HD:(first + n) * HD, t, :, :].rearrange("r h s -> r (h s)"), src).then_inc(stacked, 16)
                for a in range(A):
                    sp.dma_start(stack[p][SHIFT_ROW:SHIFT_ROW + NPIECE, 2 * a, :, :],
                                 D["zeros"].rearrange("p (h t) -> p h t", h=HEADS)).then_inc(stacked, 16)
                lone_wait(sp, shift_in, b * (16 * A))
                lone_wait(sp, shift_p_ready, b + 1)
                sp.dma_start(mscr[0:A * HEADS], shift_p[:]).then_inc(shift_out, 16)
                lone_wait(sp, shift_out, b * 16 + 16)
                for a in range(A):
                    sp.dma_start(stack[p][SHIFT_ROW:SHIFT_ROW + NPIECE, 2 * a, :, :],
                                 mscr[a * HEADS:(a + 1) * HEADS].rearrange("h c s -> c h s")).then_inc(shift_in, 16)
            schedule(sp, body)
            sp.wait_ge(shift_in, 16 * A * BATCH)

        @block.tensor
        def _(pe):
            def general(step, k):
                lone_wait(pe, g_free, use(step, k) - 1)
                return bank_of(step, k)

            def project(step, b, p):
                pe.wait_ge(xb_ready, b + 1)
                for i in range(2):
                    bank = general(step, i)
                    for a in range(A):
                        last = nc.tensor.matmul(bank[:, a * SEQ:(a + 1) * SEQ], R.wqk[layer][:, A * i + a, :], xb[p][:], start=True, stop=True)
                    last.then_inc(g_full, 1)
                bank = general(step, 2)
                for kb in range(QB):
                    last = nc.tensor.matmul(bank[:, kb * DV:(kb + 1) * DV], xb[p][:, kb * P:(kb + 1) * P], R.wv[layer][:],
                                            start=True, stop=(layer == 0))
                    if layer:
                        last = nc.tensor.matmul(bank[:, kb * DV:(kb + 1) * DV], R.ones[0:1, :], R.bv[0:1, :], start=False, stop=True)
                last.then_inc(g_full, 1)

            def scores_for_max(b, p):
                n = 0
                for a in range(A):
                    q, k = stack[p][:, 2 * a], stack[p][:, 2 * a + 1]
                    for late in range(QB):
                        per, w = 4 // (late + 1), P * (late + 1)
                        mask = R.mask_late_q[layer][:] if late else R.mask_diag_q[:]
                        for g in range(HEADS // (2 * per)):
                            if n == 0:
                                pe.wait_ge(stacked, b * LOADS + LOADS)
                            if n < 2:
                                lone_wait(pe, t_free, b * UNITS)
                            else:
                                pe.wait_ge(s_free, b * UNITS + (n - 1))
                            u = unit[n % 2]
                            for i in range(2):
                                nc.tensor.matmul(u[:, i, :], R.ident_bf[:], mask, start=True, stop=True)
                                for m in range(per):
                                    h = (2 * g + i) * per + m
                                    last = nc.tensor.matmul(u[:, i, m * w:(m + 1) * w], q[:, h, late * P:(late + 1) * P], k[:, h, 0:w],
                                                            start=False, stop=True, skip_group_check=True)
                            last.then_inc(s_full, 1)
                            n += 1

            def weigh(b, p, a, group):
                g = 2 * a + group
                pe.wait_ge(t_free, b * UNITS + 3 * (g + 1))
                if group == 0:
                    wait(pe, y_free, b * A + a)
                pr = probs[:, g % 2]
                for i in range(8):
                    h = group * 8 + i
                    early = pr[:, i // 4, (i % 4) * SEQ:(i % 4 + 1) * SEQ]
                    nc.tensor.matmul(Y[:, 0, h, :], early[:, 0:P], v[p][:, 0, h, :], start=True, stop=True)
                    nc.tensor.matmul(Y[:, 1, h, :], early[:, P:SEQ], v[p][:, 0, h, :], start=True, stop=False)
                    last = nc.tensor.matmul(Y[:, 1, h, :], pr[:, 2, i * P:(i + 1) * P], v[p][:, 1, h, :], start=False, stop=True)
                last.then_inc(weighed, 1)

            def scores_and_weigh(b, p):
                pe.wait_ge(shift_in, b * (16 * A) + 16 * A)
                pe.wait_ge(g_free, b * USES + 3)
                lone_wait(pe, s_free, b * UNITS + UNITS)
                n, pending = 0, None
                for a in range(A):
                    q, k = stack[p][:, 2 * a], stack[p][:, 2 * a + 1]
                    for group in range(2):
                        for part in range(3):
                            if n >= 2:
                                pe.wait_ge(t_free, b * UNITS + (n - 1))
                            u = unit[n % 2]
                            per, mask = (2, R.mask_early_k[layer][:]) if part < 2 else (4, R.mask_diag_k[:])
                            for i in range(2):
                                nc.tensor.matmul(u[:, i, :], R.ident_bf[:], mask, start=True, stop=True)
                                for m in range(per):
                                    h = group * 8 + (part % 2) * 4 + i * per + m
                                    o = u[:, i, m * (512 // per):(m + 1) * (512 // per)]
                                    ks, qs = (slice(0, P), slice(0, SEQ)) if part < 2 else (slice(P, SEQ), slice(P, SEQ))
                                    last = nc.tensor.matmul(o, k[:, h, ks], q[:, h, qs], start=False, stop=True, skip_group_check=True)
                            last.then_inc(t_full, 1)
                            n += 1
                        if pending:
                            weigh(b, p, *pending)
                        pending = (a, group)
                weigh(b, p, *pending)

            def turn_rows(step):
                bank = general(step, 3)
                pe.wait_ge(rows_ready, step + 1)
                for db in range(DB):
                    for qb in range(QB):
                        last = nc.tensor.transpose(bank[:, (db * QB + qb) * P:(db * QB + qb + 1) * P], out_rows[:, qb, db * P:(db + 1) * P], R.ident[:])
                last.then_inc(g_full, 1)

            def turn_shift(step, b, p):
                bank = general(step, 4)
                pe.wait_ge(shift_ready, b + 1)
                for qb in range(QB):
                    last = nc.tensor.transpose(bank[0:A * HEADS, qb * P:(qb + 1) * P], shift[p][:, qb, :], R.ident[:])
                last.then_inc(g_full, 1)

            def project_out(step):
                bank = general(step, 5)
                pe.wait_ge(g_free, use(step, 3) + 1)
                for qb in range(QB):
                    for db in range(DB):
                        last = nc.tensor.matmul(bank[:, qb * C:(qb + 1) * C], yT[:, db, qb * P:(qb + 1) * P], R.wo[layer][:, db, :],
                                                start=(db == 0), stop=(db == DB - 1 and layer == 0))
                    if layer:
                        last = nc.tensor.matmul(bank[:, qb * C:(qb + 1) * C], R.ones[0:1, :], R.bo[0:1, :], start=False, stop=True)
                last.then_inc(g_full, 1)

            def body(step, par):
                if has_front(step):
                    project(step, step + 1, 1 - par)
                if has_back(step):
                    scores_and_weigh(step, par)
                if has_front(step):
                    scores_for_max(step + 1, 1 - par)
                if has_back(step):
                    turn_rows(step)
                if has_front(step):
                    turn_shift(step, step + 1, 1 - par)
                if has_back(step):
                    project_out(step)
            schedule(pe, body)

        @block.scalar
        def _(act):
            act.wait_ge(v_ones, 2)

            def copy_qkv(step, b, p):
                for i in range(2):
                    bank = bank_of(step, i)
                    if i == 0:
                        lone_wait(act, pieces_out, b * 16)
                    act.wait_ge(g_full, use(step, i) + 1)
                    if layer:
                        nc.scalar.activation(whole[:, i, :], bank[:, 0:SEQ], ACT.Identity, bias=R.bqk[:, i:i + 1])
                        nc.scalar.activation(pieces[:, i, 0, :], bank[:, 0:SEQ], ACT.Identity, bias=R.bqk[:, i:i + 1]).then_inc(g_free, 1)
                    else:
                        src = bank.rearrange("p (t s) -> p t s", t=A)
                        nc.scalar.copy(whole[:, A * i:A * i + A, :], src)
                        nc.scalar.copy(pieces[:, A * i:A * i + A, 0, :], src).then_inc(g_free, 1)
                lone_wait(act, weighed, step * GROUPS)
                act.wait_ge(g_full, use(step, 2) + 1)
                nc.scalar.copy(v[p][:, :, :, 0:VD], bank_of(step, 2)[:, 0:QB * DV].rearrange("p (k h d) -> p k h d", k=QB, d=VD)).then_inc(g_free, 1)

            def exps(b):
                for n in range(UNITS):
                    if n % 3 == 0:
                        lone_wait(act, weighed, b * GROUPS + max(n // 3 - 1, 0))
                    act.wait_ge(t_full, b * UNITS + (n + 1))
                    nc.scalar.activation(probs[:, (n // 3) % 2, n % 3, :].rearrange("p (i s) -> p i s", i=2), unit[n % 2], ACT.Exp, scale=SCALE).then_inc(t_free, 1)

            def copy_rows(step):
                act.wait_ge(g_full, use(step, 3) + 1)
                nc.scalar.copy(yT[:].rearrange("p b s -> p (b s)"), bank_of(step, 3)[:, 0:DB * SEQ]).then_inc(g_free, 1)

            def copy_shift(step, b, p):
                lone_wait(act, shift_out, b * 16)
                act.wait_ge(g_full, use(step, 4) + 1)
                src = bank_of(step, 4)[0:A * HEADS, 0:SEQ]
                nc.scalar.copy(shift_t[:], src)
                nc.scalar.copy(shift_p[:, 0, :], src).then_inc(g_free, 1)
                if layer:
                    nc.scalar.activation(zero_exp[p][:], shift[p][:, 0, :], ACT.Exp, scale=SCALE).then_inc(zero_ready, 1)

            def copy_out(step):
                lone_wait(act, g_full, use(step, 5) + 1)
                nc.scalar.copy(R.s[:, bass.ds(step * QB, QB), :], bank_of(step, 5)[:, 0:QB * C].rearrange("p (t c) -> p t c", t=QB)).then_inc(g_free, 1)

            def body(step, par):
                if has_front(step):
                    copy_qkv(step, step + 1, 1 - par)
                if has_back(step):
                    exps(step)
                    copy_rows(step)
                if has_front(step):
                    copy_shift(step, step + 1, 1 - par)
                if has_back(step):
                    copy_out(step)
            schedule(act, body)

        @block.vector
        def _(dve):
            def take_residue(step, b):
                dve.wait_ge(g_free, use(step, 1) + 1)
                nc.vector.tensor_tensor(residue[:], whole[:], pieces[:, :, 0, :], ALU.subtract).then_inc(residue_ready, 1)

            def search(b, p):
                n = 0
                for a in range(A):
                    for late in range(QB):
                        heads = 8 // (late + 1)
                        for g in range(HEADS // heads):
                            dve.wait_ge(s_full, b * UNITS + (n + 1))
                            h0 = a * HEADS + g * heads
                            nc.vector.tensor_reduce(maxima[:, late, h0:h0 + heads], unit[n % 2].rearrange("p i (m k) -> p (i m) k", k=P * (late + 1)),
                                                    AX.X, ALU.max).then_inc(s_free, 1)
                            n += 1
                dve.wait_ge(s_free, b * UNITS + UNITS)
                if layer:
                    nc.vector.tensor_scalar(maxima[:, 0, :], maxima[:, 0, :], R.no_outside[:, 0:1], None, ALU.max).then_inc(max_ready, 1)
                    dve.wait_ge(max_ready, b + 1)
                nc.vector.tensor_scalar(shift[p][:], maxima[:], -1.0, None, ALU.mult).then_inc(shift_ready, 1)

            def divide(b, p):
                LINKS = 3
                n = [0]

                def link(ins):
                    n[0] += 1
                    ins.then_inc(y_chain, 1)
                    dve.wait_ge(y_chain, b * LINKS + n[0])
                wide = lambda a: a.unsqueeze(3).broadcast_to([P, QB, HEADS, VD])
                for a in range(A):
                    dve.wait_ge(weighed, b * GROUPS + 2 * (a + 1))
                    if layer == 0:
                        link(nc.vector.reciprocal(rsum[:], Y[:, :, :, VD]))
                        if a == 0:
                            wait(dve, rows_ready, b)
                        else:
                            link(nc.vector.tensor_tensor(rsum[:], rsum[:], R.lam[:].unsqueeze(1).broadcast_to([P, QB, HEADS]), ALU.mult))
                        nc.vector.tensor_tensor(y[a][:], Y[:, :, :, 0:VD], wide(rsum[:]), ALU.mult).then_inc(y_free, 1)
                    else:
                        dve.wait_ge(zero_ready, b + 1)
                        nc.vector.scalar_tensor_tensor(out=rsum[:, 0, :], in0=zero_exp[p][:], scalar=R.outside[:, 0:1], in1=Y[:, 0, :, VD],
                                                       op0=ALU.mult, op1=ALU.add).then_inc(y_chain, 1)
                        n[0] += 1
                        link(nc.vector.tensor_copy(rsum[:, 1, :], Y[:, 1, :, VD]))
                        link(nc.vector.reciprocal(rsum[:], rsum[:]))
                        dve.wait_ge(g_full, b * USES + 2)
                        nc.vector.tensor_tensor(out_rows[:].rearrange("p q (h d) -> p q h d", d=VD), Y[:, :, :, 0:VD], wide(rsum[:]), ALU.mult).then_inc(rows_ready, 1)
                assert n[0] == LINKS

            def body(step, par):
                if has_front(step):
                    take_residue(step, step + 1)
                if has_back(step):
                    divide(step, par)
                if has_front(step):
                    search(step + 1, 1 - par)
            schedule(dve, body)


def build_output(nc, R, out):
    CH = 4
    TC = NT // CH
    with ExitStack() as ctx:
        sem = lambda name: ctx.enter_context(nc.semaphore(f"out_{name}"))
        gated, product, final, stored = (sem(n) for n in ("gated", "product", "final", "stored"))
        block = ctx.enter_context(nc.Block())
        cs = [slice(c * TC, (c + 1) * TC) for c in range(CH)]

        @block.scalar
        def _(act):
            for c in range(CH):
                nc.scalar.activation(R.g[:, cs[c], :], R.g[:, cs[c], :], ACT.Silu).then_inc(gated, 1)

        @block.vector
        def _(dve):
            for c in range(CH):
                dve.wait_ge(gated, c + 1)
                nc.vector.tensor_tensor(R.g[:, cs[c], :], R.g[:, cs[c], :], R.s[:, cs[c], :], ALU.mult).then_inc(product, 1)
                dve.wait_ge(product, c + 1)
                nc.vector.tensor_tensor(R.x[:, cs[c], :], R.x[:, cs[c], :], R.g[:, cs[c], :], ALU.add).then_inc(final, 1)

        @block.sync
        def _(sp):
            rows = out.rearrange("b s d -> (b s) d").rearrange("(t p) d -> p t d", p=P)
            for c in range(CH):
                sp.wait_ge(final, c + 1)
                sp.dma_start(rows[:, cs[c], :], R.x[:, cs[c], :]).then_inc(stored, 16)
            sp.wait_ge(stored, 16 * CH)


def build(nc, D, out):
    D["scratch_pieces"] = nc.dram_tensor("scratch_pieces", (4, NPIECE, C, SEQ), BF16).ap()
    D["scratch_shift"] = nc.dram_tensor("scratch_shift", (2 * HEADS, NPIECE, SEQ), BF16).ap()
    D["zeros"] = nc.dram_tensor("zeros", (NPIECE, HEADS * SEQ), BF16).ap()
    with ExitStack() as ctx:
        def sb(name, shape, dt=F32):
            return ctx.enter_context(nc.sbuf_tensor(name, shape, dt))
        R = Resident()
        R.ps = ctx.enter_context(nc.psum_tensor("ps", [P, 8, 512], F32))
        R.x = sb("x", [P, NT, C])
        R.xnT = sb("xnT", [P, NTOK])
        R.s = sb("s", [P, NT, C])
        R.g = sb("g", [P, NT, C])
        R.cw = sb("cw", [P, NT, EXPERTS])
        R.wqk = [sb("wqk0", [P, 4, C]), sb("wqk1", [P, 2, C])]
        R.wv = [sb("wv0", [P, 2 * C]), sb("wv1", [P, C])]
        R.wo = [sb("wo0", [P, 2, C]), sb("wo1", [P, 1, C])]
        R.bqk = sb("bqk", [P, 2])
        R.bv = sb("bv", [1, C])
        R.bo = sb("bo", [1, C])
        R.wr = [sb(f"wr{l}", [P, EXPERTS]) for l in range(2)]
        R.b2 = [sb(f"b2_{l}", [EXPERTS, C]) for l in range(2)]
        R.rank = sb("rank", [P, EXPERTS])
        R.ident = sb("ident", [P, P])
        R.ident_bf = sb("ident_bf", [P, P], BF16)
        R.ones = sb("ones", [P, P])
        R.before = sb("before", [P, P])
        R.mask_diag_q = sb("mask_diag_q", [P, 4, P], BF16)
        R.mask_diag_k = sb("mask_diag_k", [P, 4, P], BF16)
        R.mask_late_q = [sb(f"mask_late_q{l}", [P, 2, 2, P], BF16) for l in range(2)]
        R.mask_early_k = [sb(f"mask_early_k{l}", [P, 2, 2, P], BF16) for l in range(2)]
        R.lam = sb("lam", [P, HEADS])
        R.outside = sb("outside", [P, 1])
        R.no_outside = sb("no_outside", [P, 1])

        R.stack = [sb(f"stack{p}", [P, 4, HEADS, SEQ], BF16) for p in range(2)]
        build_constants(nc, R, D)
        for layer in range(2):
            build_layernorm(nc, R, layer)
            build_router(nc, R, layer)
            build_experts(nc, R, D, layer)
            build_attention(nc, R, D, layer)
        build_output(nc, R, out)


def kernel(**inputs):
    import numpy as _np
    import concourse.bacc as _bacc
    from concourse import mybir as _mybir
    from concourse.bass_utils import run_bass_kernel_spmd as _run

    laid = {k: _np.asarray(v) for k, v in inputs.items()}
    laid["L0_attn_x"] = laid["L0_attn_x"].reshape(NTOK, C)
    for k in ("L1_attn_wq", "L1_attn_wk", "L1_attn_wv", "L1_attn_wo", "L1_ffn_w_router"):
        laid[k] = laid[k].T
    for k in ("L0_attn_q1_w", "L0_attn_q2_w", "L0_attn_k1_w", "L0_attn_k2_w", "L1_attn_wq", "L1_attn_wk"):
        laid[k] = laid[k].reshape(C, HEADS, HD).transpose(0, 2, 1).reshape(C, C)
    for k in ("L1_attn_bq", "L1_attn_bk"):
        laid[k] = laid[k].reshape(HEADS, HD).T.reshape(C, 1)
    for k in ("L1_attn_bv", "L1_attn_bo", *(f"L0_attn_lambda_{a}{n}" for a in "qk" for n in "12")):
        laid[k] = laid[k].reshape(1, C)
    laid["L0_w1"], laid["L0_w2"] = laid.pop("L0_ffn_W1"), laid.pop("L0_ffn_W2")
    laid["L1_w1"] = laid.pop("L1_ffn_w1").transpose(0, 2, 1)
    laid["L1_w2"] = laid.pop("L1_ffn_w2").transpose(0, 2, 1)
    for l in range(2):
        laid[f"L{l}_b1"] = laid.pop(f"L{l}_ffn_b1").reshape(EXPERTS, HB, P).transpose(0, 2, 1)

    nc = _bacc.Bacc("TRN2", target_bir_lowering=False, num_devices=1)
    arrays, D = {}, {}
    for name, a in laid.items():
        a = _np.ascontiguousarray(a)
        arrays[f"in_{name}"] = a
        D[name] = nc.dram_tensor(f"in_{name}", a.shape, _mybir.dt.from_np(a.dtype), kind="ExternalInput").ap()
    out = nc.dram_tensor("out_dram", (BATCH, SEQ, C), F32, kind="ExternalOutput").ap()
    build(nc, D, out)
    r = _run(nc, [arrays], core_ids=[0])
    return r.results[0]["out_dram"]
```

```python
from contextlib import ExitStack
import math

import concourse.bass as bass
from concourse import mybir

ALU = mybir.AluOpType
ACT = mybir.ActivationFunctionType
AX = mybir.AxisListType
F32 = mybir.dt.float32
BF16 = mybir.dt.bfloat16

P = 128
BATCH, SEQ, C = 16, 256, 128
NTOK = BATCH * SEQ
NT = NTOK // P
QB = SEQ // P
HEADS = 16
HD = C // HEADS
EXPERTS, HIDDEN, TOPK = 8, 512, 2
HB = HIDDEN // P
CAP = int(math.ceil(NTOK * TOPK / EXPERTS * 1.05))
LAMBDA_INIT = 0.8 - 0.6 * math.exp(-0.3 * (4 - 1))
EPS = 1e-5
SCALE = 1.0 / math.sqrt(HD)
MASKED = -1.0e30
BELOW = -3.0e38

Q_PIECE = (0, 0, 0, 1, 1, 2)
K_PIECE = (0, 1, 2, 0, 1, 0)
RUNS = ((0, 3), (3, 2), (5, 1))
SHIFT_ROW = len(Q_PIECE) * HD
NPIECE = 3


class Resident:
    pass


def build_constants(nc, R, D):
    with ExitStack() as ctx:
        sb = lambda name, shape, dt=F32: ctx.enter_context(nc.sbuf_tensor(f"const_{name}", shape, dt))
        lam4, lam_sum, lam_row_t = sb("lam4", [1, 4, C]), sb("lam_sum", [1, 2, HEADS]), sb("lam_row", [1, HEADS])
        ones_bf, zeros_bf = sb("ones_bf", [NPIECE, HEADS * SEQ], BF16), sb("zeros_bf", [NPIECE, HEADS * SEQ], BF16)
        m32 = sb("m32", [P, 4, P])
        loads = ctx.enter_context(nc.semaphore("const_loads"))
        lam_loads = ctx.enter_context(nc.semaphore("lam_loads"))
        filled = ctx.enter_context(nc.semaphore("const_filled"))
        cut = ctx.enter_context(nc.semaphore("const_cut"))
        lam_chain = ctx.enter_context(nc.semaphore("lam_chain"))
        lam_exp = ctx.enter_context(nc.semaphore("lam_exp"))
        lam_row = ctx.enter_context(nc.semaphore("lam_row"))
        lam_spread = ctx.enter_context(nc.semaphore("lam_spread"))
        ones_rows = ctx.enter_context(nc.semaphore("ones_rows"))
        block = ctx.enter_context(nc.Block())
        n_loads = [0]

        @block.sync
        def _(sp):
            def load(dst, src):
                n_loads[0] += 1
                sp.dma_start(dst, src).then_inc(loads, 16)
            for t, name in enumerate(("L0_attn_lambda_q1", "L0_attn_lambda_k1", "L0_attn_lambda_q2", "L0_attn_lambda_k2")):
                sp.dma_start(lam4[0:1, t, :], D[name]).then_inc(lam_loads, 16)
            for c in range(4):
                load(R.x[:, c * 8:(c + 1) * 8, :], D["L0_attn_x"].rearrange("(t p) d -> p t d", p=P)[:, c * 8:(c + 1) * 8, :])
            for t, name in enumerate(("L0_attn_q1_w", "L0_attn_k1_w", "L0_attn_q2_w", "L0_attn_k2_w")):
                load(R.wqk[0][:, t, :], D[name])
            load(R.wv[0][:], D["L0_attn_v_w"])
            load(R.wo[0][:], D["L0_attn_c_w"].rearrange("(b p) d -> p b d", p=P))
            load(R.wqk[1][:, 0, :], D["L1_attn_wq"])
            load(R.wqk[1][:, 1, :], D["L1_attn_wk"])
            load(R.wv[1][:], D["L1_attn_wv"])
            load(R.wo[1][:, 0, :], D["L1_attn_wo"])
            load(R.bqk[:, 0:1], D["L1_attn_bq"])
            load(R.bqk[:, 1:2], D["L1_attn_bk"])
            load(R.bv[:], D["L1_attn_bv"])
            load(R.bo[:], D["L1_attn_bo"])
            load(R.wr[0][:], D["L0_ffn_Wg"])
            load(R.wr[1][:], D["L1_ffn_w_router"])
            load(R.b2[0][:], D["L0_ffn_b2"])
            load(R.b2[1][:], D["L1_ffn_b2"])
            sp.wait_ge(ones_rows, 1)
            for par in range(2):
                for t in (1, 3):
                    load(R.stack[par][SHIFT_ROW:SHIFT_ROW + NPIECE, t, :, :], ones_bf[:].rearrange("p (h t) -> p h t", h=HEADS))
            load(D["zeros"], zeros_bf[:])
            sp.wait_ge(loads, 16 * n_loads[0])

        @block.gpsimd
        def _(pool):
            nc.gpsimd.memset(R.ident[:], 0.0).then_inc(filled, 1)
            nc.gpsimd.memset(R.ones[:], 1.0).then_inc(filled, 1)
            nc.gpsimd.memset(R.before[:], 1.0).then_inc(filled, 1)
            nc.gpsimd.memset(m32[:], 0.0).then_inc(filled, 1)
            pool.wait_ge(filled, 4)
            nc.gpsimd.affine_select(out=R.ident[:], in_=R.ident[:], compare_op=ALU.not_equal, fill=1.0, base=0,
                                    pattern=[[-1, P]], channel_multiplier=1).then_inc(cut, 1)
            nc.gpsimd.affine_select(out=R.before[:], in_=R.before[:], compare_op=ALU.is_gt, fill=0.0, base=0,
                                    pattern=[[1, P]], channel_multiplier=-1).then_inc(cut, 1)
            nc.gpsimd.affine_select(out=m32[:, 0, :], in_=m32[:, 0, :], compare_op=ALU.is_ge, fill=MASKED, base=0,
                                    pattern=[[-1, P]], channel_multiplier=1).then_inc(cut, 1)
            nc.gpsimd.affine_select(out=m32[:, 1, :], in_=m32[:, 1, :], compare_op=ALU.is_ge, fill=MASKED, base=0,
                                    pattern=[[1, P]], channel_multiplier=-1).then_inc(cut, 1)
            nc.gpsimd.affine_select(out=m32[:, 2, :], in_=m32[:, 2, :], compare_op=ALU.is_gt, fill=MASKED, base=0,
                                    pattern=[[1, P]], channel_multiplier=-1).then_inc(cut, 1)
            nc.gpsimd.affine_select(out=m32[:, 3, :], in_=m32[:, 3, :], compare_op=ALU.is_gt, fill=MASKED, base=0,
                                    pattern=[[-1, P]], channel_multiplier=1).then_inc(cut, 1)
            pool.wait_ge(cut, 6)
            nc.gpsimd.tensor_copy(R.ident_bf[:], R.ident[:])
            D0q, D0k, Wq, Wk = (m32[:, i, :] for i in range(4))
            for j in range(4):
                nc.gpsimd.tensor_copy(R.mask_diag_q[:, j, :], D0q)
                nc.gpsimd.tensor_copy(R.mask_diag_k[:, j, :], D0k)
            for j in range(2):
                nc.gpsimd.tensor_copy(R.mask_late_q[:, j, 0:P], Wq)
                nc.gpsimd.tensor_copy(R.mask_late_q[:, j, P:2 * P], D0q)
                nc.gpsimd.tensor_copy(R.mask_early_k[:, j, 0:P], D0k)
                nc.gpsimd.tensor_copy(R.mask_early_k[:, j, P:2 * P], Wk)
            for e in range(EXPERTS):
                nc.gpsimd.memset(R.rank[:, e:e + 1], float(EXPERTS - e))
            nc.gpsimd.iota(R.outside[:], [[0, 1]], base=P - 1, channel_multiplier=-1, allow_small_or_imprecise_dtypes=True).then_inc(cut, 1)
            pool.wait_ge(cut, 7)
            nc.gpsimd.tensor_scalar(R.no_outside[:], R.outside[:], 0.5, BELOW, ALU.is_lt, ALU.mult)

        @block.vector
        def _(dve):
            nc.vector.memset(zeros_bf[:], 0.0)
            nc.vector.memset(ones_bf[:], 1.0)
            for par in range(2):
                for t in range(4):
                    last = nc.vector.memset(R.stack[par][:, t, :, :], 0.0)
            last.then_inc(ones_rows, 1)
            dve.wait_ge(lam_loads, 16 * 4)
            nc.vector.tensor_tensor(lam4[0:1, 0, :], lam4[0:1, 0, :], lam4[0:1, 1, :], ALU.mult).then_inc(lam_chain, 1)
            nc.vector.tensor_tensor(lam4[0:1, 2, :], lam4[0:1, 2, :], lam4[0:1, 3, :], ALU.mult).then_inc(lam_chain, 1)
            dve.wait_ge(lam_chain, 2)
            for i in range(2):
                nc.vector.tensor_reduce(lam_sum[0:1, i, :], lam4[0:1, 2 * i, :].rearrange("p (h d) -> p h d", d=HD),
                                        AX.X, ALU.add).then_inc(lam_chain, 1)
            dve.wait_ge(lam_exp, 1)
            nc.vector.tensor_tensor(lam_row_t[0:1, :], lam_sum[0:1, 0, :], lam_sum[0:1, 1, :], ALU.subtract).then_inc(lam_chain, 1)
            dve.wait_ge(lam_chain, 5)
            nc.vector.tensor_scalar(lam_row_t[0:1, :], lam_row_t[0:1, :], LAMBDA_INIT, None, ALU.add).then_inc(lam_row, 1)
            dve.wait_ge(lam_spread, 1)
            nc.vector.tensor_copy(R.lam[:], R.ps[:, 0, 0:HEADS])

        @block.scalar
        def _(act):
            act.wait_ge(lam_chain, 4)
            nc.scalar.activation(lam_sum[0:1, :, :], lam_sum[0:1, :, :], ACT.Exp).then_inc(lam_exp, 1)

        @block.tensor
        def _(pe):
            pe.wait_ge(lam_row, 1)
            pe.wait_ge(filled, 4)
            nc.tensor.matmul(R.ps[:, 0, 0:HEADS], R.ones[0:1, :], lam_row_t[0:1, :], start=True, stop=True).then_inc(lam_spread, 1)


def build_layernorm(nc, R, layer):
    CH = 4
    TC = NT // CH
    with ExitStack() as ctx:
        sem = lambda name: ctx.enter_context(nc.semaphore(f"ln{layer}_{name}"))
        sb = lambda name, shape: ctx.enter_context(nc.sbuf_tensor(f"ln{layer}_{name}", shape, F32))
        xn = sb("xn", [P, NT, C])
        total = sb("total", [P, NT])
        mean = sb("mean", [P, NT])
        sq = sb("sq", [P, TC, C])
        var = sb("var", [P, NT])
        rstd = sb("rstd", [P, NT])
        half = sb("half", [P, TC])
        chain, centred, squared, var_ready, rstd_ready, xn_ready, turned, evacuated, half_ready = (
            sem(n) for n in ("chain", "centred", "squared", "var_ready", "rstd_ready", "xn_ready", "turned", "evacuated", "half_ready"))
        block = ctx.enter_context(nc.Block())
        cs = [slice(c * TC, (c + 1) * TC) for c in range(CH)]
        wide = lambda a: a.unsqueeze(2).broadcast_to([P, TC, C])

        @block.vector
        def _(dve):
            n = [0]

            def link(ins):
                n[0] += 1
                ins.then_inc(chain, 1)
                dve.wait_ge(chain, n[0])

            def mean_of(c):
                link(nc.vector.tensor_reduce(total[:, cs[c]], R.x[:, cs[c], :], AX.X, ALU.add))
                link(nc.vector.tensor_scalar(mean[:, cs[c]], total[:, cs[c]], 1.0 / C, None, ALU.mult))
                nc.vector.tensor_tensor(xn[:, cs[c], :], R.x[:, cs[c], :], wide(mean[:, cs[c]]), ALU.subtract).then_inc(centred, 1)

            def variance(c):
                dve.wait_ge(squared, c + 1)
                link(nc.vector.tensor_reduce(total[:, cs[c]], sq[:], AX.X, ALU.add))
                nc.vector.tensor_scalar(var[:, cs[c]], total[:, cs[c]], 1.0 / C, EPS, ALU.mult, ALU.add).then_inc(var_ready, 1)

            def scale(c):
                dve.wait_ge(rstd_ready, c + 1)
                nc.vector.tensor_tensor(xn[:, cs[c], :], xn[:, cs[c], :], wide(rstd[:, cs[c]]), ALU.mult).then_inc(xn_ready, 1)

            for c in range(CH):
                mean_of(c)
                variance(c)
                if c:
                    scale(c - 1)
            scale(CH - 1)

        @block.scalar
        def _(act):
            for c in range(CH):
                act.wait_ge(centred, c + 1)
                if c:
                    act.wait_ge(var_ready, c)
                nc.scalar.activation(sq[:], xn[:, cs[c], :], ACT.Square).then_inc(squared, 1)
            for i in range(NT // 4):
                act.wait_ge(turned, i + 1)
                nc.scalar.copy(R.xnT[:, i * 4 * P:(i + 1) * 4 * P], R.ps[:, i % 4, :]).then_inc(evacuated, 1)

        @block.gpsimd
        def _(pool):
            nc.gpsimd.memset(half[:], -0.5).then_inc(half_ready, 1)
            pool.wait_ge(half_ready, 1)
            for c in range(CH):
                pool.wait_ge(var_ready, c + 1)
                nc.gpsimd.tensor_tensor(rstd[:, cs[c]], var[:, cs[c]], half[:], ALU.pow).then_inc(rstd_ready, 1)

        @block.tensor
        def _(pe):
            for i in range(NT // 4):
                pe.wait_ge(xn_ready, (4 * i) // TC + 1)
                if i >= 4:
                    pe.wait_ge(evacuated, i - 3)
                for j in range(4):
                    last = nc.tensor.transpose(R.ps[:, i % 4, j * P:(j + 1) * P], xn[:, 4 * i + j, :], R.ident[:])
                last.then_inc(turned, 1)


def build_router(nc, R, layer):
    E = EXPERTS
    with ExitStack() as ctx:
        sem = lambda name: ctx.enter_context(nc.semaphore(f"rt{layer}_{name}"))
        sb = lambda name, shape: ctx.enter_context(nc.sbuf_tensor(f"rt{layer}_{name}", shape, F32))
        logits = sb("logits", [P, NT, E])
        rest = sb("rest", [P, NT, E])
        ranked = sb("ranked", [P, NT, E])
        first = sb("first", [P, NT, E])
        second = sb("second", [P, NT, E])
        best = sb("best", [P, 2, NT])
        top_rank = sb("top_rank", [P, NT])
        gap = sb("gap", [P, NT])
        gate = sb("gate", [P, 2, NT])
        chosen = sb("chosen", [P, NT, E])
        upto = sb("upto", [P, NT, E])
        place = sb("place", [P, NT, E])
        one_row = sb("one_row", [P, NT])
        cwT = sb("cwT", [E, NTOK])
        scored, chain, gap_ready, gap_exp, chosen_ready, counted, cw_ready, cwt_ready, cwt_copied, seeded, seed_copied = (
            sem(n) for n in ("scored", "chain", "gap_ready", "gap_exp", "chosen_ready", "counted", "cw_ready", "cwt_ready", "cwt_copied", "seeded", "seed_copied"))
        block = ctx.enter_context(nc.Block())
        wide = lambda a: a.unsqueeze(2).broadcast_to([P, NT, E])
        rank_w = R.rank[:, :].unsqueeze(1).broadcast_to([P, NT, E])
        flat = lambda a: a.rearrange("p t e -> p (t e)")

        @block.tensor
        def _(pe):
            for t in range(NT):
                last = nc.tensor.matmul(R.ps[:, 0, t * E:(t + 1) * E], R.xnT[:, t * P:(t + 1) * P], R.wr[layer][:], start=True, stop=True)
            last.then_inc(scored, 1)
            if layer == 0:
                pe.wait_ge(chosen_ready, 1)
                nc.tensor.matmul(R.ps[:, 1, 0:NT * E], R.before[:], flat(chosen[:]), start=True, stop=True)
                nc.tensor.matmul(R.ps[:, 2, 0:NT * E], R.ones[:], flat(chosen[:]), start=True, stop=True).then_inc(counted, 1)
            pe.wait_ge(cw_ready, 1)
            for i in range(NT // 4):
                if i >= 2:
                    pe.wait_ge(cwt_copied, i - 1)
                for j in range(4):
                    last = nc.tensor.transpose(R.ps[0:E, 3 + i % 2, j * P:(j + 1) * P], R.cw[:, 4 * i + j, :], R.ident[:])
                last.then_inc(cwt_ready, 1)
            for i in range(NT // 4):
                pe.wait_ge(cwt_copied, i + 1)
                if i >= 2:
                    pe.wait_ge(seed_copied, i - 1)
                for j in range(4):
                    t = 4 * i + j
                    last = nc.tensor.matmul(R.ps[:, 5 + i % 2, j * P:(j + 1) * P], cwT[:, t * P:(t + 1) * P], R.b2[layer][:], start=True, stop=True)
                last.then_inc(seeded, 1)

        @block.scalar
        def _(act):
            act.wait_ge(gap_ready, 1)
            nc.scalar.activation(gap[:], gap[:], ACT.Exp).then_inc(gap_exp, 1)
            for i in range(NT // 4):
                act.wait_ge(cwt_ready, i + 1)
                nc.scalar.copy(cwT[:, i * 4 * P:(i + 1) * 4 * P], R.ps[0:E, 3 + i % 2, :]).then_inc(cwt_copied, 1)

        @block.vector
        def _(dve):
            n = [0]

            def link(ins):
                n[0] += 1
                ins.then_inc(chain, 1)
                dve.wait_ge(chain, n[0])

            def pick(onehot, scores, k):
                link(nc.vector.tensor_reduce(best[:, k, :], scores[:], AX.X, ALU.max))
                link(nc.vector.tensor_tensor(ranked[:], scores[:], wide(best[:, k, :]), ALU.is_equal))
                link(nc.vector.tensor_tensor(ranked[:], ranked[:], rank_w, ALU.mult))
                link(nc.vector.tensor_reduce(top_rank[:], ranked[:], AX.X, ALU.max))
                link(nc.vector.tensor_tensor(onehot[:], ranked[:], wide(top_rank[:]), ALU.is_equal))

            dve.wait_ge(scored, 1)
            link(nc.vector.tensor_copy(flat(logits[:]), R.ps[:, 0, 0:NT * E]))
            pick(first, logits, 0)
            link(nc.vector.scalar_tensor_tensor(out=flat(rest[:]), in0=flat(first[:]), scalar=BELOW, in1=flat(logits[:]), op0=ALU.mult, op1=ALU.add))
            pick(second, rest, 1)
            nc.vector.tensor_tensor(gap[:], best[:, 1, :], best[:, 0, :], ALU.subtract).then_inc(gap_ready, 1)
            dve.wait_ge(gap_exp, 1)
            link(nc.vector.tensor_scalar(gate[:, 1, :], gap[:], 1.0, None, ALU.add))
            link(nc.vector.reciprocal(gate[:, 0, :], gate[:, 1, :]))
            link(nc.vector.tensor_tensor(gate[:, 1, :], gap[:], gate[:, 0, :], ALU.mult))
            if layer == 0:
                ins = nc.vector.tensor_tensor(chosen[:], first[:], second[:], ALU.add)
                ins.then_inc(chosen_ready, 1)
            link(nc.vector.tensor_tensor(first[:], first[:], wide(gate[:, 0, :]), ALU.mult))
            link(nc.vector.tensor_tensor(second[:], second[:], wide(gate[:, 1, :]), ALU.mult))
            cw_ins = nc.vector.tensor_tensor(R.cw[:], first[:], second[:], ALU.add)
            if layer == 0:
                link(cw_ins)
                link(nc.vector.memset(one_row[:], 1.0))
                dve.wait_ge(counted, 1)
                link(nc.vector.tensor_copy(flat(ranked[:]), R.ps[:, 2, 0:NT * E]))
                for e in range(E):
                    link(nc.vector.tensor_tensor_scan(upto[:, :, e], one_row[:], ranked[:, :, e], 0.0, ALU.mult, ALU.add))
                link(nc.vector.tensor_tensor(upto[:], upto[:], ranked[:], ALU.subtract))
                link(nc.vector.tensor_tensor(flat(place[:]), R.ps[:, 1, 0:NT * E], flat(upto[:]), ALU.add))
                link(nc.vector.tensor_scalar(place[:], place[:], float(CAP), None, ALU.is_lt))
                nc.vector.tensor_tensor(R.cw[:], R.cw[:], place[:], ALU.mult).then_inc(cw_ready, 1)
            else:
                cw_ins.then_inc(cw_ready, 1)
            for i in range(NT // 4):
                dve.wait_ge(seeded, i + 1)
                nc.vector.tensor_copy(R.g[:, 4 * i:4 * i + 4, :].rearrange("p t c -> p (t c)"), R.ps[:, 5 + i % 2, :]).then_inc(seed_copied, 1)


def build_experts(nc, R, D, layer):
    W1, B1, W2 = D[f"L{layer}_w1"], D[f"L{layer}_b1"], D[f"L{layer}_w2"]
    TOKS = 512
    NCH = NTOK // TOKS
    TT = TOKS // P
    NU = NCH * HB
    gelu = ACT.Gelu if layer else ACT.Gelu_apprx_tanh
    with ExitStack() as ctx:
        sem = lambda name: ctx.enter_context(nc.semaphore(f"ex{layer}_{name}"))
        sb = lambda name, shape: ctx.enter_context(nc.sbuf_tensor(f"ex{layer}_{name}", shape, F32))
        w1 = [sb(f"w1_{p}", [P, HIDDEN]) for p in range(2)]
        w2 = [sb(f"w2_{p}", [P, HB, C]) for p in range(2)]
        b1 = [sb(f"b1_{p}", [P, HB]) for p in range(2)]
        gate = [sb(f"gate_{p}", [P, NT]) for p in range(2)]
        hid = [sb(f"hid_{p}", [P, HB, TOKS]) for p in range(2)]
        arrived = [sem(f"arrived_{p}") for p in range(2)]
        added = [sem(f"added_{p}") for p in range(2)]
        up, act_done, down, gate_ready = (sem(n) for n in ("up", "act_done", "down", "gate_ready"))
        block = ctx.enter_context(nc.Block())

        def wait(eng, s, value):
            if not (isinstance(value, int) and value <= 0):
                eng.wait_ge(s, value)

        def schedule(eng, body):
            body(0)
            with eng.Fori(0, EXPERTS // 2 - 1) as i:
                body(i + 1)

        @block.sync
        def _(sp):
            def body(j):
                for par in range(2):
                    e = j * 2 + par
                    wait(sp, added[par], j * NCH)
                    sp.dma_start(w1[par][:], W1[bass.ds(e, 1)].rearrange("o p h -> (o p) h")).then_inc(arrived[par], 16)
                    sp.dma_start(w2[par][:], W2[bass.ds(e, 1)].rearrange("o (b p) d -> (o p) b d", p=P)).then_inc(arrived[par], 16)
                    sp.dma_start(b1[par][:], B1[bass.ds(e, 1)].rearrange("o p h -> (o p) h")).then_inc(arrived[par], 16)
            schedule(sp, body)

        @block.tensor
        def _(pe):
            def upward(j, par, c):
                for hb in range(HB):
                    wait(pe, act_done, j * (2 * NU) + (par * NU + (c * HB + hb - (HB - 1) if c else 0)))
                    nc.tensor.matmul(R.ps[:, hb, :], w1[par][:, hb * P:(hb + 1) * P], R.xnT[:, c * TOKS:(c + 1) * TOKS],
                                     start=True, stop=True).then_inc(up, 1)

            def downward(j, par, c):
                wait(pe, act_done, j * (2 * NU) + (par * NU + (c + 1) * HB))
                if c >= 2:
                    wait(pe, added[par], j * NCH + (c - 1))
                elif par:
                    wait(pe, added[0], j * NCH + NCH)
                else:
                    wait(pe, added[1], j * NCH)
                for tt in range(TT):
                    for hb in range(HB):
                        last = nc.tensor.matmul(R.ps[:, 4 + c % 2, tt * P:(tt + 1) * P], hid[c % 2][:, hb, tt * P:(tt + 1) * P],
                                                w2[par][:, hb, :], start=(hb == 0), stop=(hb == HB - 1))
                last.then_inc(down, 1)

            def body(j):
                for par in range(2):
                    wait(pe, arrived[par], j * 48 + 48)
                    for c in range(NCH + 1):
                        if c < NCH:
                            upward(j, par, c)
                        if c:
                            downward(j, par, c - 1)
            schedule(pe, body)

        @block.scalar
        def _(act):
            def body(j):
                for par in range(2):
                    wait(act, arrived[par], j * 48 + 48)
                    for c in range(NCH):
                        wait(act, down, j * (2 * NCH) + (par * NCH + max(c - 1, 0)))
                        for hb in range(HB):
                            wait(act, up, j * (2 * NU) + (par * NU + c * HB + hb + 1))
                            nc.scalar.activation(hid[c % 2][:, hb, :], R.ps[:, hb, :], gelu, bias=b1[par][:, hb:hb + 1]).then_inc(act_done, 1)
            schedule(act, body)
            for c in range(0, NCH, 2):
                tiles = slice(c * TT, (c + 2) * TT)
                act.wait_ge(added[1], (EXPERTS // 2 - 1) * NCH + c + 2)
                nc.scalar.activation(R.g[:, tiles, :], R.g[:, tiles, :], ACT.Silu)

        @block.vector
        def _(dve):
            def body(j):
                for par in range(2):
                    nc.vector.tensor_copy(gate[par][:], R.cw[:, :, bass.ds(j * 2 + par, 1)].rearrange("p t o -> p (t o)")).then_inc(gate_ready, 1)
                    wait(dve, gate_ready, j * 2 + (par + 1))
                    for c in range(NCH):
                        wait(dve, down, j * (2 * NCH) + (par * NCH + c + 1))
                        for tt in range(TT):
                            t = c * TT + tt
                            last = nc.vector.scalar_tensor_tensor(out=R.g[:, t, :], in0=R.ps[:, 4 + c % 2, tt * P:(tt + 1) * P],
                                                                  scalar=gate[par][:, t:t + 1], in1=R.g[:, t, :], op0=ALU.mult, op1=ALU.add)
                        last.then_inc(added[par], 1)
            schedule(dve, body)


def build_attention(nc, R, D, layer):
    A = 2 if layer == 0 else 1
    T = 2 * A
    VD = HD * (2 if layer == 0 else 1)
    VW = 32
    STRIPS = P // VW
    DV = HEADS * VD
    DB = DV // P
    UNITS = 6 * A
    GROUPS = 2 * A
    LOADS = (len(RUNS) * T + A) * 16
    LAST = BATCH - 1

    if layer == 0:
        ORDER = (("qk0", -1), ("qk1", -1), ("v", -1), ("rows", 8), ("turn00", 9), ("turn01", 9), ("out", 10),
                 ("shift", UNITS), ("turn10", UNITS), ("turn11", UNITS))
    else:
        ORDER = (("qk0", -1), ("qk1", -1), ("v", -1), ("rows", 1), ("out", 3), ("shift", UNITS), ("turn00", UNITS), ("turn01", UNITS))
    SLOT = dict(ORDER)
    NAMES = [n for n, _ in ORDER]
    USES = len(NAMES)

    def has(step, name):
        if not isinstance(step, int):
            return True
        if name.startswith("qk"):
            return step + 2 <= LAST
        if name in ("v", "shift"):
            return 0 <= step + 1 <= LAST
        if name in ("rows", "out"):
            return 0 <= step - 1 <= LAST
        return 0 <= step <= LAST

    FIRST_FULL = 1

    def use(step, name):
        if isinstance(step, int):
            before = sum(has(t, n) for t in range(-2, step) for n in NAMES)
            return before + sum(has(step, n) for n in NAMES[:NAMES.index(name)])
        return step * USES + (use(FIRST_FULL, NAMES[0]) - FIRST_FULL * USES + NAMES.index(name))

    with ExitStack() as ctx:
        sem = lambda name: ctx.enter_context(nc.semaphore(f"at{layer}_{name}"))

        def sb(name, shape, dt=F32):
            return ctx.enter_context(nc.sbuf_tensor(f"at{layer}_{name}", shape, dt))

        xb = [sb(f"xb{p}", [P, SEQ]) for p in range(2)]
        whole = sb("whole", [P, T, SEQ])
        pieces = sb("pieces", [P, T, NPIECE, SEQ], BF16)
        v = [sb(f"v{p}", [P, QB, HEADS, VW]) for p in range(2)]
        maxima = sb("maxima", [P, QB, A * HEADS])
        shift = [sb(f"shift{p}", [P, QB, A * HEADS]) for p in range(2)]
        shift_t = sb("shift_t", [A * HEADS, SEQ])
        shift_r = sb("shift_r", [A * HEADS, SEQ])
        shift_p = sb("shift_p", [A * HEADS, NPIECE, SEQ], BF16)
        probs = sb("probs", [P, 2, 3, 1024])
        weighed_t = sb("weighed_t", [P, A, GROUPS // A, 2, SEQ])
        weighed_q = sb("weighed_q", [P, A, QB, HEADS, VD + 1])
        rsum_all = sb("rsum", [P, A, QB, HEADS])
        out_rows = sb("out_rows", [P, QB, DV])
        yT = sb("yT", [P, DB, SEQ])
        s_rows = sb("s_rows", [P, QB, C])
        if layer == 0:
            y = [sb(f"y{a}", [P, QB, HEADS, VD]) for a in range(A)]
            sq = sb("sq", [P, QB, HEADS, VD])
            stat = sb("stat", [P, QB * HEADS])
            rstd = sb("rstd", [P, QB * HEADS])
            half = sb("half", [P, QB * HEADS])
        else:
            zero_exp = [sb(f"zero_exp{p}", [P, HEADS]) for p in range(2)]

        passed = sem("passed")
        v_clear, v_ones = sem("v_clear"), sem("v_ones")
        xb_ready = sem("xb_ready")
        g_full, g_free = sem("g_full"), sem("g_free")
        split_chain = sem("split_chain")
        pieces_ready = sem("pieces_ready")
        pieces_out = sem("pieces_out")
        stacked = sem("stacked")
        s_full, s_free = sem("s_full"), sem("s_free")
        max_ready = sem("max_ready")
        shift_ready = sem("shift_ready")
        shift_chain = sem("shift_chain")
        shift_p_ready = sem("shift_p_ready")
        shift_out, shift_in = sem("shift_out"), sem("shift_in")
        t_full, t_free = sem("t_full"), sem("t_free")
        weighed = sem("weighed")
        y_free = sem("y_free")
        divided = sem("divided")
        div_chain = sem("div_chain")
        rows_ready = sem("rows_ready") if layer == 0 else divided
        norm_chain = sem("norm_chain")
        rstd_ready = sem("rstd_ready")
        half_ready = sem("half_ready")
        times_g = sem("times_g")
        gated = sem("gated")
        stored = sem("stored")
        zero_ready = sem("zero_ready")
        block = ctx.enter_context(nc.Block())

        stack = R.stack
        G = [R.ps[:, i, :] for i in range(2)]
        s_unit, t_unit = R.ps[:, 2:4, :], R.ps[:, 4:6, :]
        Y = [R.ps[:, 6 + i, :].rearrange("p (f s) -> p f s", f=2) for i in range(2)]
        scr, mscr = D["scratch_pieces"], D["scratch_shift"]

        def bank_of(step, name):
            return G[use(step if isinstance(step, int) else FIRST_FULL, name) % 2]

        def wait(eng, s, value):
            if not (isinstance(value, int) and value <= 0):
                eng.wait_ge(s, value)

        def lone_wait(eng, s, value):
            if not (isinstance(value, int) and value <= 0):
                eng.wait_ge(s, value)
                eng.sem_inc(passed, 1)

        def schedule(eng, body):
            for step in (-2, -1, 0):
                body(step, step % 2)
            with eng.Fori(0, (LAST - 3) // 2) as j:
                body(j * 2 + 1, 1)
                body(j * 2 + 2, 0)
            for step in range(LAST - 2, LAST + 2):
                body(step, step % 2)

        @block.gpsimd
        def _(pool):
            def copy_tokens(b, p):
                nc.gpsimd.tensor_copy(xb[p][:], R.xnT[:, bass.ds(b * SEQ, SEQ)]).then_inc(xb_ready, 1)

            def split_shift(step, b):
                pool.wait_ge(g_free, use(step, "shift") + 1)
                nc.gpsimd.tensor_tensor(shift_r[:], shift_t[:], shift_p[:, 0, :], ALU.subtract).then_inc(shift_chain, 1)
                lone_wait(pool, shift_chain, b * 2 + 1)
                nc.gpsimd.tensor_copy(shift_p[:, 1, :], shift_r[:]).then_inc(shift_chain, 1)
                pool.wait_ge(shift_chain, b * 2 + 2)
                nc.gpsimd.tensor_tensor(shift_p[:, 2, :], shift_r[:], shift_p[:, 1, :], ALU.subtract).then_inc(shift_p_ready, 1)

            def head_norm(b):
                LINKS = 5 + 2 * 4
                n = [0]

                def link(ins):
                    n[0] += 1
                    ins.then_inc(norm_chain, 1)
                    lone_wait(pool, norm_chain, b * LINKS + n[0])
                y0, y1, sqv = (t[:].rearrange("p q h d -> p (q h) d") for t in (*y, sq))
                wide = lambda a: a.unsqueeze(2).broadcast_to([P, QB * HEADS, VD])

                def add_up(values):
                    w = VD // 2
                    while w:
                        dst = sqv[:, :, 0:w] if w > 1 else stat[:].unsqueeze(2)
                        link(nc.gpsimd.tensor_tensor(dst, values[:, :, 0:w], values[:, :, w:2 * w], ALU.add))
                        values, w = sqv, w // 2

                lone_wait(pool, divided, b * A + A)
                link(nc.gpsimd.tensor_tensor(y0, y0, y1, ALU.subtract))
                add_up(y0)
                link(nc.gpsimd.tensor_scalar(stat[:], stat[:], 1.0 / VD, None, ALU.mult))
                link(nc.gpsimd.tensor_tensor(y0, y0, wide(stat[:]), ALU.subtract))
                link(nc.gpsimd.tensor_tensor(sqv, y0, y0, ALU.mult))
                add_up(sqv)
                k2 = (1.0 - LAMBDA_INIT) ** -2
                link(nc.gpsimd.tensor_scalar(stat[:], stat[:], k2 / VD, k2 * EPS, ALU.mult, ALU.add))
                assert n[0] == LINKS
                nc.gpsimd.tensor_tensor(rstd[:], stat[:], half[:], ALU.pow).then_inc(rstd_ready, 1)
                lone_wait(pool, rstd_ready, b + 1)
                nc.gpsimd.tensor_tensor(out_rows[:].rearrange("p q (h d) -> p (q h) d", d=VD), y0, wide(rstd[:]), ALU.mult).then_inc(rows_ready, 1)

            def gate(step, b):
                tiles = bass.ds(b * QB, QB)
                lone_wait(pool, g_free, use(step, "out") + 1)
                nc.gpsimd.tensor_tensor(s_rows[:], s_rows[:], R.g[:, tiles, :], ALU.mult).then_inc(times_g, 1)
                lone_wait(pool, times_g, b + 1)
                nc.gpsimd.tensor_tensor(R.x[:, tiles, :], R.x[:, tiles, :], s_rows[:], ALU.add).then_inc(gated, 1)

            if layer == 0:
                nc.gpsimd.memset(half[:], -0.5).then_inc(half_ready, 1)
                pool.wait_ge(half_ready, 1)
            for vt in v:
                nc.gpsimd.memset(vt[:], 0.0).then_inc(v_clear, 1)
            pool.wait_ge(v_clear, 2)
            for vt in v:
                nc.gpsimd.memset(vt[:, :, :, VD:VD + 1], 1.0).then_inc(v_ones, 1)

            def body(step, par):
                if has(step, "qk0"):
                    copy_tokens(step + 2, par)
                if has(step, "rows") and layer == 0:
                    head_norm(step - 1)
                if has(step, "out"):
                    gate(step, step - 1)
                if has(step, "shift"):
                    split_shift(step, step + 1)
            schedule(pool, body)

        @block.sync
        def _(sp):
            def fill_stack(step, b, p):
                lone_wait(sp, stacked, b * LOADS)
                lone_wait(sp, pieces_ready, b + 1)
                sp.dma_start(scr.rearrange("t c p s -> p t c s")[:, 0:T], pieces[:]).then_inc(pieces_out, 16)
                lone_wait(sp, pieces_out, b * 16 + 16)
                lone_wait(sp, t_full, (step + 1) * UNITS)
                for t in range(T):
                    which = K_PIECE if t % 2 else Q_PIECE
                    for first, n in RUNS:
                        piece = scr[t, which[first]]
                        src = bass.AP(piece.tensor, piece.offset, [[C * SEQ if t % 2 else 0, n], [HEADS * SEQ, HD], [1, HEADS * SEQ]])
                        sp.dma_start(stack[p][first * HD:(first + n) * HD, t, :, :].rearrange("r h s -> r (h s)"), src).then_inc(stacked, 16)
                for a in range(A):
                    sp.dma_start(stack[p][SHIFT_ROW:SHIFT_ROW + NPIECE, 2 * a, :, :],
                                 D["zeros"].rearrange("p (h t) -> p h t", h=HEADS)).then_inc(stacked, 16)

            def fill_shift(b, p):
                lone_wait(sp, shift_in, b * (16 * A))
                lone_wait(sp, shift_p_ready, b + 1)
                sp.dma_start(mscr[0:A * HEADS], shift_p[:]).then_inc(shift_out, 16)
                lone_wait(sp, shift_out, b * 16 + 16)
                for a in range(A):
                    sp.dma_start(stack[p][SHIFT_ROW:SHIFT_ROW + NPIECE, 2 * a, :, :],
                                 mscr[a * HEADS:(a + 1) * HEADS].rearrange("h c s -> c h s")).then_inc(shift_in, 16)

            def store(b):
                lone_wait(sp, gated, b + 1)
                sp.dma_start(D["out"][bass.ds(b * QB, QB)].rearrange("t p c -> p t c"), R.x[:, bass.ds(b * QB, QB), :]).then_inc(stored, 16)

            def body(step, par):
                if has(step, "qk0"):
                    fill_stack(step, step + 2, par)
                if has(step, "shift"):
                    fill_shift(step + 1, 1 - par)
                if has(step, "out") and layer == 1:
                    store(step - 1)
            schedule(sp, body)
            sp.wait_ge(shift_in, 16 * A * BATCH)
            if layer == 1:
                sp.wait_ge(stored, 16 * BATCH)

        @block.tensor
        def _(pe):
            def general(step, name):
                lone_wait(pe, g_free, use(step, name) - 1)
                return bank_of(step, name)

            def project_qk(step, b, p):
                pe.wait_ge(xb_ready, b + 1)
                for i in range(2):
                    bank = general(step, f"qk{i}")
                    for a in range(A):
                        last = nc.tensor.matmul(bank[:, a * SEQ:(a + 1) * SEQ], R.wqk[layer][:, A * i + a, :], xb[p][:], start=True, stop=True)
                    last.then_inc(g_full, 1)

            def project_v(step, p):
                bank = general(step, "v")
                for kb in range(QB):
                    last = nc.tensor.matmul(bank[:, kb * DV:(kb + 1) * DV], xb[p][:, kb * P:(kb + 1) * P], R.wv[layer][:],
                                            start=True, stop=(layer == 0))
                    if layer:
                        last = nc.tensor.matmul(bank[:, kb * DV:(kb + 1) * DV], R.ones[0:1, :], R.bv[0:1, :], start=False, stop=True)
                last.then_inc(g_full, 1)

            def masked_scores(u, i, per, masked, mask, products):
                bank = u[:, i, :].rearrange("p (m w) -> p m w", m=per)
                nc.tensor.matmul(bank[:, :, masked], R.ident_bf[:], mask, start=True, stop=True)
                for m, (lhs, rhs) in enumerate(products):
                    last = nc.tensor.matmul(bank[:, m, :], lhs, rhs, start=False, stop=True, skip_group_check=True)
                return last

            def scores_for_max(b, p, n):
                a, r = divmod(n, 6)
                q, k = stack[p][:, 2 * a], stack[p][:, 2 * a + 1]
                late = int(r >= 2)
                per, w = 4 // (late + 1), P * (late + 1)
                if n == 0:
                    pe.wait_ge(stacked, b * LOADS + LOADS)
                lone_wait(pe, s_free, b * UNITS + n)
                for i in range(2):
                    h0 = (2 * (r - 2 * late) + i) * per
                    prod = [(q[:, h, late * P:(late + 1) * P], k[:, h, 0:w]) for h in range(h0, h0 + per)]
                    if not late:
                        last = masked_scores(s_unit, i, per, slice(0, P), R.mask_diag_q[:], prod)
                    elif layer == 0:
                        last = masked_scores(s_unit, i, per, slice(P, SEQ), R.mask_diag_q[:, 0:2, :], prod)
                    else:
                        last = masked_scores(s_unit, i, per, slice(0, SEQ), R.mask_late_q[:], prod)
                last.then_inc(s_full, 1)

            def scores(b, p, n):
                g, part = divmod(n, 3)
                a, group = divmod(g, 2)
                q, k = stack[p][:, 2 * a], stack[p][:, 2 * a + 1]
                if n == 0:
                    pe.wait_ge(shift_in, b * (16 * A) + 16 * A)
                lone_wait(pe, t_free, b * UNITS + n)
                for i in range(2):
                    if part < 2:
                        h0 = group * 8 + part * 4 + i * 2
                        prod = [(k[:, h, 0:P], q[:, h, :]) for h in (h0, h0 + 1)]
                        if layer == 0:
                            last = masked_scores(t_unit, i, 2, slice(0, P), R.mask_diag_k[:, 0:2, :], prod)
                        else:
                            last = masked_scores(t_unit, i, 2, slice(0, SEQ), R.mask_early_k[:], prod)
                    else:
                        h0 = group * 8 + i * 4
                        prod = [(k[:, h, P:SEQ], q[:, h, P:SEQ]) for h in range(h0, h0 + 4)]
                        last = masked_scores(t_unit, i, 4, slice(0, P), R.mask_diag_k[:], prod)
                last.then_inc(t_full, 1)

            def weigh(b, p, g, part):
                a, group = divmod(g, 2)
                if part == 0:
                    pe.wait_ge(t_free, b * UNITS + 3 * (g + 1))
                    lone_wait(pe, y_free, b * GROUPS + (g - 1))
                pr = probs[:, g % 2]
                for late in range(2):
                    for j in range(STRIPS):
                        h = group * 8 + part * 4 + j
                        strip = Y[g % 2][j * VW:(j + 1) * VW, part, :]
                        if not late:
                            nc.tensor.matmul(strip, v[p][:, 0, h, :], pr[:, part, j * SEQ:(j + 1) * SEQ], start=True, stop=False)
                        else:
                            i = part * 4 + j
                            last = nc.tensor.matmul(strip[:, P:SEQ], v[p][:, 1, h, :], pr[:, 2, i * P:(i + 1) * P], start=False, stop=True)
                last.then_inc(weighed, 1)

            def turn_weighed(step, b, a):
                pe.wait_ge(y_free, b * GROUPS + 2 * (a + 1))
                for qb in range(QB):
                    bank = general(step, f"turn{a}{qb}")
                    for i in range(4):
                        last = nc.tensor.transpose(bank[:, i * P:(i + 1) * P], weighed_t[:, a, i // 2, i % 2, qb * P:(qb + 1) * P], R.ident[:])
                    last.then_inc(g_full, 1)

            def turn_rows(step, b):
                bank = general(step, "rows")
                pe.wait_ge(rows_ready, b + 1)
                for db in range(DB):
                    for qb in range(QB):
                        last = nc.tensor.transpose(bank[:, (db * QB + qb) * P:(db * QB + qb + 1) * P], out_rows[:, qb, db * P:(db + 1) * P], R.ident[:])
                last.then_inc(g_full, 1)

            def turn_shift(step, b, p):
                bank = general(step, "shift")
                pe.wait_ge(shift_ready, b + 1)
                for qb in range(QB):
                    last = nc.tensor.transpose(bank[0:A * HEADS, qb * P:(qb + 1) * P], shift[p][:, qb, :], R.ident[:])
                last.then_inc(g_full, 1)

            def project_out(step):
                bank = general(step, "out")
                lone_wait(pe, g_free, use(step, "rows") + 1)
                for qb in range(QB):
                    for db in range(DB):
                        last = nc.tensor.matmul(bank[:, qb * C:(qb + 1) * C], yT[:, db, qb * P:(qb + 1) * P], R.wo[layer][:, db, :],
                                                start=(db == 0), stop=(db == DB - 1 and layer == 0))
                    if layer:
                        last = nc.tensor.matmul(bank[:, qb * C:(qb + 1) * C], R.ones[0:1, :], R.bo[0:1, :], start=False, stop=True)
                last.then_inc(g_full, 1)

            pe.wait_ge(v_ones, 2)

            def body(step, par):
                now, next_ = has(step, "turn00"), has(step, "shift")
                if has(step, "qk0"):
                    project_qk(step, step + 2, par)
                if has(step, "v"):
                    project_v(step, 1 - par)
                for n in range(UNITS):
                    if next_:
                        scores_for_max(step + 1, 1 - par, n)
                    if now:
                        scores(step, par, n)
                        if n >= 3 and n % 3 < 2:
                            weigh(step, par, n // 3 - 1, n % 3)
                    if has(step, "rows") and n == SLOT["rows"]:
                        turn_rows(step, step - 1)
                    if now and n == SLOT["turn00"]:
                        turn_weighed(step, step, 0)
                    if has(step, "out") and n == SLOT["out"]:
                        project_out(step)
                if now:
                    weigh(step, par, GROUPS - 1, 0)
                if next_:
                    turn_shift(step, step + 1, 1 - par)
                if now:
                    weigh(step, par, GROUPS - 1, 1)
                    turn_weighed(step, step, A - 1)
            schedule(pe, body)

        @block.scalar
        def _(act):
            act.wait_ge(v_ones, 2)

            def copy_qk(step, b, p):
                lone_wait(act, pieces_out, b * 16)
                for i in range(2):
                    bank = bank_of(step, f"qk{i}")
                    act.wait_ge(g_full, use(step, f"qk{i}") + 1)
                    if layer:
                        nc.scalar.activation(whole[:, i, :], bank[:, 0:SEQ], ACT.Identity, bias=R.bqk[:, i:i + 1])
                        nc.scalar.activation(pieces[:, i, 0, :], bank[:, 0:SEQ], ACT.Identity, bias=R.bqk[:, i:i + 1]).then_inc(g_free, 1)
                    else:
                        src = bank.rearrange("p (t s) -> p t s", t=A)
                        nc.scalar.copy(whole[:, A * i:A * i + A, :], src)
                        nc.scalar.copy(pieces[:, A * i:A * i + A, 0, :], src).then_inc(g_free, 1)

            def copy_v(step, p):
                lone_wait(act, weighed, step * (2 * GROUPS))
                act.wait_ge(g_full, use(step, "v") + 1)
                nc.scalar.copy(v[p][:, :, :, 0:VD], bank_of(step, "v")[:, 0:QB * DV].rearrange("p (k h d) -> p k h d", k=QB, d=VD)).then_inc(g_free, 1)

            def exp(b, n):
                if n % 3 == 0:
                    lone_wait(act, weighed, b * (2 * GROUPS) + 2 * (n // 3 - 1))
                act.wait_ge(t_full, b * UNITS + (n + 1))
                nc.scalar.activation(probs[:, (n // 3) % 2, n % 3, :].rearrange("p (i s) -> p i s", i=2), t_unit, ACT.Exp, scale=SCALE).then_inc(t_free, 1)

            def copy_rows(step):
                act.wait_ge(g_full, use(step, "rows") + 1)
                nc.scalar.copy(yT[:].rearrange("p b s -> p (b s)"), bank_of(step, "rows")[:, 0:DB * SEQ]).then_inc(g_free, 1)

            def copy_turned(step, b, a):
                lone_wait(act, divided, (b - 1) * A + a + 1)
                for qb in range(QB):
                    act.wait_ge(g_full, use(step, f"turn{a}{qb}") + 1)
                    nc.scalar.copy(weighed_q[:, a, qb, :, :], bank_of(step, f"turn{a}{qb}").rearrange("p (h d) -> p h d", d=VW)[:, :, 0:VD + 1]).then_inc(g_free, 1)

            def copy_shift(step, b, p):
                lone_wait(act, shift_out, b * 16)
                act.wait_ge(g_full, use(step, "shift") + 1)
                src = bank_of(step, "shift")[0:A * HEADS, 0:SEQ]
                nc.scalar.copy(shift_t[:], src)
                nc.scalar.copy(shift_p[:, 0, :], src).then_inc(g_free, 1)
                if layer:
                    nc.scalar.activation(zero_exp[p][:], shift[p][:, 0, :], ACT.Exp, scale=SCALE).then_inc(zero_ready, 1)

            def copy_out(step, b):
                if isinstance(step, int):
                    lone_wait(act, gated, b)
                act.wait_ge(g_full, use(step, "out") + 1)
                nc.scalar.copy(s_rows[:], bank_of(step, "out")[:, 0:QB * C].rearrange("p (t c) -> p t c", t=QB)).then_inc(g_free, 1)

            def body(step, par):
                now = has(step, "turn00")
                if has(step, "qk0"):
                    copy_qk(step, step + 2, par)
                if has(step, "v"):
                    copy_v(step, 1 - par)
                for n in range(UNITS):
                    if now:
                        exp(step, n)
                    if has(step, "rows") and n == SLOT["rows"]:
                        copy_rows(step)
                    if now and n == SLOT["turn00"]:
                        copy_turned(step, step, 0)
                    if has(step, "out") and n == SLOT["out"]:
                        copy_out(step, step - 1)
                if has(step, "shift"):
                    copy_shift(step, step + 1, 1 - par)
                if now:
                    copy_turned(step, step, A - 1)
            schedule(act, body)

        @block.vector
        def _(dve):
            def split(step, b):
                dve.wait_ge(g_free, use(step, "qk1") + 1)
                nc.vector.tensor_tensor(whole[:], whole[:], pieces[:, :, 0, :], ALU.subtract).then_inc(split_chain, 1)
                dve.wait_ge(split_chain, b * 2 + 1)
                nc.vector.tensor_copy(pieces[:, :, 1, :], whole[:]).then_inc(split_chain, 1)
                dve.wait_ge(split_chain, b * 2 + 2)
                nc.vector.tensor_tensor(pieces[:, :, 2, :], whole[:], pieces[:, :, 1, :], ALU.subtract).then_inc(pieces_ready, 1)

            def search(b, n):
                a, r = divmod(n, 6)
                late = int(r >= 2)
                heads = 8 // (late + 1)
                h0 = a * HEADS + (r - 2 * late) * heads
                dve.wait_ge(s_full, b * UNITS + (n + 1))
                nc.vector.tensor_reduce(maxima[:, late, h0:h0 + heads], s_unit.rearrange("p i (m k) -> p (i m) k", k=P * (late + 1)),
                                        AX.X, ALU.max).then_inc(s_free, 1)

            def negate(b, p):
                dve.wait_ge(s_free, b * UNITS + UNITS)
                if layer:
                    nc.vector.tensor_scalar(maxima[:, 0, :], maxima[:, 0, :], R.no_outside[:, 0:1], None, ALU.max).then_inc(max_ready, 1)
                    dve.wait_ge(max_ready, b + 1)
                nc.vector.tensor_scalar(shift[p][:], maxima[:], -1.0, None, ALU.mult).then_inc(shift_ready, 1)

            def copy_weighed(b, g):
                dve.wait_ge(weighed, b * (2 * GROUPS) + 2 * (g + 1))
                nc.vector.tensor_copy(weighed_t[:, g // 2, g % 2, :, :], Y[g % 2]).then_inc(y_free, 1)

            def divide(step, b, p):
                LINKS = 3
                n = [0]

                def link(ins):
                    n[0] += 1
                    ins.then_inc(div_chain, 1)
                    dve.wait_ge(div_chain, b * LINKS + n[0])
                wide = lambda a: a.unsqueeze(3).broadcast_to([P, QB, HEADS, VD])
                for a in range(A):
                    w, rsum = weighed_q[:, a], rsum_all[:, a]
                    dve.wait_ge(g_free, use(step, f"turn{a}1") + 1)
                    if layer == 0:
                        link(nc.vector.reciprocal(rsum, w[:, :, :, VD]))
                        if a == 0:
                            wait(dve, rows_ready, b)
                        else:
                            link(nc.vector.tensor_tensor(rsum, rsum, R.lam[:].unsqueeze(1).broadcast_to([P, QB, HEADS]), ALU.mult))
                        nc.vector.tensor_tensor(y[a][:], w[:, :, :, 0:VD], wide(rsum), ALU.mult).then_inc(divided, 1)
                    else:
                        dve.wait_ge(zero_ready, b + 1)
                        nc.vector.scalar_tensor_tensor(out=rsum[:, 0, :], in0=zero_exp[p][:], scalar=R.outside[:, 0:1], in1=w[:, 0, :, VD],
                                                       op0=ALU.mult, op1=ALU.add).then_inc(div_chain, 1)
                        n[0] += 1
                        link(nc.vector.tensor_copy(rsum[:, 1, :], w[:, 1, :, VD]))
                        link(nc.vector.reciprocal(rsum, rsum))
                        nc.vector.tensor_tensor(out_rows[:].rearrange("p q (h d) -> p q h d", d=VD), w[:, :, :, 0:VD], wide(rsum), ALU.mult).then_inc(divided, 1)
                assert n[0] == LINKS

            def body(step, par):
                now, next_ = has(step, "turn00"), has(step, "shift")
                if has(step, "qk0"):
                    split(step, step + 2)
                for n in range(UNITS):
                    if next_:
                        search(step + 1, n)
                    if now and n >= 3 and n % 3 == 1:
                        copy_weighed(step, n // 3 - 1)
                if next_:
                    negate(step + 1, 1 - par)
                if now:
                    copy_weighed(step, GROUPS - 1)
                    divide(step, step, par)
            schedule(dve, body)


def build(nc, D):
    D["scratch_pieces"] = nc.dram_tensor("scratch_pieces", (4, NPIECE, C, SEQ), BF16).ap()
    D["scratch_shift"] = nc.dram_tensor("scratch_shift", (2 * HEADS, NPIECE, SEQ), BF16).ap()
    D["zeros"] = nc.dram_tensor("zeros", (NPIECE, HEADS * SEQ), BF16).ap()
    with ExitStack() as ctx:
        def sb(name, shape, dt=F32):
            return ctx.enter_context(nc.sbuf_tensor(name, shape, dt))
        R = Resident()
        R.ps = ctx.enter_context(nc.psum_tensor("ps", [P, 8, 512], F32))
        R.x = sb("x", [P, NT, C])
        R.xnT = sb("xnT", [P, NTOK])
        R.g = sb("g", [P, NT, C])
        R.cw = sb("cw", [P, NT, EXPERTS])
        R.wqk = [sb("wqk0", [P, 4, C]), sb("wqk1", [P, 2, C])]
        R.wv = [sb("wv0", [P, 2 * C]), sb("wv1", [P, C])]
        R.wo = [sb("wo0", [P, 2, C]), sb("wo1", [P, 1, C])]
        R.bqk = sb("bqk", [P, 2])
        R.bv = sb("bv", [1, C])
        R.bo = sb("bo", [1, C])
        R.wr = [sb(f"wr{l}", [P, EXPERTS]) for l in range(2)]
        R.b2 = [sb(f"b2_{l}", [EXPERTS, C]) for l in range(2)]
        R.rank = sb("rank", [P, EXPERTS])
        R.ident = sb("ident", [P, P])
        R.ident_bf = sb("ident_bf", [P, P], BF16)
        R.ones = sb("ones", [P, P])
        R.before = sb("before", [P, P])
        R.mask_diag_q = sb("mask_diag_q", [P, 4, P], BF16)
        R.mask_diag_k = sb("mask_diag_k", [P, 4, P], BF16)
        R.mask_late_q = sb("mask_late_q", [P, 2, 2 * P], BF16)
        R.mask_early_k = sb("mask_early_k", [P, 2, 2 * P], BF16)
        R.lam = sb("lam", [P, HEADS])
        R.outside = sb("outside", [P, 1])
        R.no_outside = sb("no_outside", [P, 1])

        R.stack = [sb(f"stack{p}", [P, 4, HEADS, SEQ], BF16) for p in range(2)]
        build_constants(nc, R, D)
        for layer in range(2):
            build_layernorm(nc, R, layer)
            build_router(nc, R, layer)
            build_experts(nc, R, D, layer)
            build_attention(nc, R, D, layer)


def kernel(**inputs):
    import numpy as _np
    import concourse.bacc as _bacc
    from concourse import mybir as _mybir
    from concourse.bass_utils import run_bass_kernel_spmd as _run

    laid = {k: _np.asarray(v) for k, v in inputs.items()}
    laid["L0_attn_x"] = laid["L0_attn_x"].reshape(NTOK, C)
    for k in ("L1_attn_wq", "L1_attn_wk", "L1_attn_wv", "L1_attn_wo", "L1_ffn_w_router"):
        laid[k] = laid[k].T
    for k in ("L0_attn_q1_w", "L0_attn_q2_w", "L0_attn_k1_w", "L0_attn_k2_w", "L1_attn_wq", "L1_attn_wk"):
        laid[k] = laid[k].reshape(C, HEADS, HD).transpose(0, 2, 1).reshape(C, C)
    for k in ("L1_attn_bq", "L1_attn_bk"):
        laid[k] = laid[k].reshape(HEADS, HD).T.reshape(C, 1)
    for k in ("L1_attn_bv", "L1_attn_bo", *(f"L0_attn_lambda_{a}{n}" for a in "qk" for n in "12")):
        laid[k] = laid[k].reshape(1, C)
    laid["L0_w1"], laid["L0_w2"] = laid.pop("L0_ffn_W1"), laid.pop("L0_ffn_W2")
    laid["L1_w1"] = laid.pop("L1_ffn_w1").transpose(0, 2, 1)
    laid["L1_w2"] = laid.pop("L1_ffn_w2").transpose(0, 2, 1)
    for l in range(2):
        laid[f"L{l}_b1"] = laid.pop(f"L{l}_ffn_b1").reshape(EXPERTS, HB, P).transpose(0, 2, 1)

    nc = _bacc.Bacc("TRN2", target_bir_lowering=False, num_devices=1)
    arrays, D = {}, {}
    for name, a in laid.items():
        a = _np.ascontiguousarray(a)
        arrays[f"in_{name}"] = a
        D[name] = nc.dram_tensor(f"in_{name}", a.shape, _mybir.dt.from_np(a.dtype), kind="ExternalInput").ap()
    out = nc.dram_tensor("out_dram", (BATCH, SEQ, C), F32, kind="ExternalOutput").ap()
    D["out"] = out.rearrange("b s d -> (b s) d").rearrange("(t p) d -> t p d", p=P)
    build(nc, D)
    r = _run(nc, [arrays], core_ids=[0])
    return r.results[0]["out_dram"]
```

```python
from contextlib import ExitStack
import math

import concourse.bass as bass
from concourse import mybir

ALU = mybir.AluOpType
ACT = mybir.ActivationFunctionType
AX = mybir.AxisListType
F32 = mybir.dt.float32
BF16 = mybir.dt.bfloat16
I32 = mybir.dt.int32
U32 = mybir.dt.uint32

P = 128
BATCH, SEQ, C = 16, 256, 128
NTOK = BATCH * SEQ
NT = NTOK // P
QB = SEQ // P
HEADS = 16
HD = C // HEADS
EXPERTS, HIDDEN, TOPK = 8, 512, 2
HB = HIDDEN // P
CAP = int(math.ceil(NTOK * TOPK / EXPERTS * 1.05))
LAMBDA_INIT = 0.8 - 0.6 * math.exp(-0.3 * (4 - 1))
EPS = 1e-5
SCALE = 1.0 / math.sqrt(HD)
MASKED = -1.0e30
BELOW = -3.0e38
TILES = NTOK * TOPK // P + EXPERTS

Q_PIECE = (0, 0, 0, 1, 1, 2)
K_PIECE = (0, 1, 2, 0, 1, 0)
RUNS = ((0, 3), (3, 2), (5, 1))
SHIFT_ROW = len(Q_PIECE) * HD
NPIECE = 3


class Resident:
    pass


def build_constants(nc, R, D):
    with ExitStack() as ctx:
        sb = lambda name, shape, dt=F32: ctx.enter_context(nc.sbuf_tensor(f"const_{name}", shape, dt))
        lam4, lam_sum, lam_row_t = sb("lam4", [1, 4, C]), sb("lam_sum", [1, 2, HEADS]), sb("lam_row", [1, HEADS])
        m32 = sb("m32", [P, 4, P])
        loads = ctx.enter_context(nc.semaphore("const_loads"))
        lam_loads = ctx.enter_context(nc.semaphore("lam_loads"))
        filled = ctx.enter_context(nc.semaphore("const_filled"))
        cut = ctx.enter_context(nc.semaphore("const_cut"))
        lam_chain = ctx.enter_context(nc.semaphore("lam_chain"))
        lam_exp = ctx.enter_context(nc.semaphore("lam_exp"))
        lam_row = ctx.enter_context(nc.semaphore("lam_row"))
        lam_spread = ctx.enter_context(nc.semaphore("lam_spread"))
        zero_tile_ready = ctx.enter_context(nc.semaphore("zero_tile_ready"))
        block = ctx.enter_context(nc.Block())
        n_loads = [0]

        @block.sync
        def _(sp):
            def load(dst, src):
                n_loads[0] += 1
                sp.dma_start(dst, src).then_inc(loads, 16)
            for t, name in enumerate(("L0_attn_lambda_q1", "L0_attn_lambda_k1", "L0_attn_lambda_q2", "L0_attn_lambda_k2")):
                sp.dma_start(lam4[0:1, t, :], D[name]).then_inc(lam_loads, 16)
            for c in range(4):
                load(R.x[:, c * 8:(c + 1) * 8, :], D["L0_attn_x"].rearrange("(t p) d -> p t d", p=P)[:, c * 8:(c + 1) * 8, :])
            load(R.wr[0][:], D["L0_ffn_Wg"])
            load(R.wr[1][:], D["L1_ffn_w_router"])
            sp.wait_ge(zero_tile_ready, 1)
            sp.dma_start(D["list_in"].rearrange("(j p) c -> p j c", p=P), R.zero_tile[:].unsqueeze(1).broadcast_to([P, TILES, C])).then_inc(R.list_clear, 16)
            sp.wait_ge(loads, 16 * n_loads[0])

        @block.gpsimd
        def _(pool):
            nc.gpsimd.memset(R.zero_tile[:], 0.0).then_inc(zero_tile_ready, 1)
            nc.gpsimd.memset(R.ident[:], 0.0).then_inc(filled, 1)
            nc.gpsimd.memset(R.ones[:], 1.0).then_inc(filled, 1)
            nc.gpsimd.memset(R.before[:], 1.0).then_inc(filled, 1)
            nc.gpsimd.memset(m32[:], 0.0).then_inc(filled, 1)
            pool.wait_ge(filled, 4)
            nc.gpsimd.affine_select(out=R.ident[:], in_=R.ident[:], compare_op=ALU.not_equal, fill=1.0, base=0,
                                    pattern=[[-1, P]], channel_multiplier=1).then_inc(cut, 1)
            nc.gpsimd.affine_select(out=R.before[:], in_=R.before[:], compare_op=ALU.is_gt, fill=0.0, base=0,
                                    pattern=[[1, P]], channel_multiplier=-1).then_inc(cut, 1)
            nc.gpsimd.affine_select(out=m32[:, 0, :], in_=m32[:, 0, :], compare_op=ALU.is_ge, fill=MASKED, base=0,
                                    pattern=[[-1, P]], channel_multiplier=1).then_inc(cut, 1)
            nc.gpsimd.affine_select(out=m32[:, 1, :], in_=m32[:, 1, :], compare_op=ALU.is_ge, fill=MASKED, base=0,
                                    pattern=[[1, P]], channel_multiplier=-1).then_inc(cut, 1)
            nc.gpsimd.affine_select(out=m32[:, 2, :], in_=m32[:, 2, :], compare_op=ALU.is_gt, fill=MASKED, base=0,
                                    pattern=[[1, P]], channel_multiplier=-1).then_inc(cut, 1)
            nc.gpsimd.affine_select(out=m32[:, 3, :], in_=m32[:, 3, :], compare_op=ALU.is_gt, fill=MASKED, base=0,
                                    pattern=[[-1, P]], channel_multiplier=1).then_inc(cut, 1)
            pool.wait_ge(cut, 6)
            nc.gpsimd.tensor_copy(R.ident_bf[:], R.ident[:])
            D0q, D0k, Wq, Wk = (m32[:, i, :] for i in range(4))
            for j in range(4):
                nc.gpsimd.tensor_copy(R.mask_diag_q[:, j, :], D0q)
                nc.gpsimd.tensor_copy(R.mask_diag_k[:, j, :], D0k)
            for j in range(2):
                nc.gpsimd.tensor_copy(R.mask_late_q[:, j, 0:P], Wq)
                nc.gpsimd.tensor_copy(R.mask_late_q[:, j, P:2 * P], D0q)
                nc.gpsimd.tensor_copy(R.mask_early_k[:, j, 0:P], D0k)
                nc.gpsimd.tensor_copy(R.mask_early_k[:, j, P:2 * P], Wk)
            for e in range(EXPERTS):
                nc.gpsimd.memset(R.rank[:, e:e + 1], float(EXPERTS - e))
            nc.gpsimd.iota(R.starts[:], [[P, TILES]], base=0, channel_multiplier=0, allow_small_or_imprecise_dtypes=True)
            nc.gpsimd.iota(R.outside[:], [[0, 1]], base=P - 1, channel_multiplier=-1, allow_small_or_imprecise_dtypes=True).then_inc(cut, 1)
            pool.wait_ge(cut, 7)
            nc.gpsimd.tensor_scalar(R.no_outside[:], R.outside[:], 0.5, BELOW, ALU.is_lt, ALU.mult)

        @block.vector
        def _(dve):
            dve.wait_ge(lam_loads, 16 * 4)
            nc.vector.tensor_tensor(lam4[0:1, 0, :], lam4[0:1, 0, :], lam4[0:1, 1, :], ALU.mult).then_inc(lam_chain, 1)
            nc.vector.tensor_tensor(lam4[0:1, 2, :], lam4[0:1, 2, :], lam4[0:1, 3, :], ALU.mult).then_inc(lam_chain, 1)
            dve.wait_ge(lam_chain, 2)
            for i in range(2):
                nc.vector.tensor_reduce(lam_sum[0:1, i, :], lam4[0:1, 2 * i, :].rearrange("p (h d) -> p h d", d=HD),
                                        AX.X, ALU.add).then_inc(lam_chain, 1)
            dve.wait_ge(lam_exp, 1)
            nc.vector.tensor_tensor(lam_row_t[0:1, :], lam_sum[0:1, 0, :], lam_sum[0:1, 1, :], ALU.subtract).then_inc(lam_chain, 1)
            dve.wait_ge(lam_chain, 5)
            nc.vector.tensor_scalar(lam_row_t[0:1, :], lam_row_t[0:1, :], LAMBDA_INIT, None, ALU.add).then_inc(lam_row, 1)
            dve.wait_ge(lam_spread, 1)
            nc.vector.tensor_copy(R.lam[:], R.ps[:, 0, 0:HEADS])

        @block.scalar
        def _(act):
            act.wait_ge(lam_chain, 4)
            nc.scalar.activation(lam_sum[0:1, :, :], lam_sum[0:1, :, :], ACT.Exp).then_inc(lam_exp, 1)

        @block.tensor
        def _(pe):
            pe.wait_ge(lam_row, 1)
            pe.wait_ge(filled, 4)
            nc.tensor.matmul(R.ps[:, 0, 0:HEADS], R.ones[0:1, :], lam_row_t[0:1, :], start=True, stop=True).then_inc(lam_spread, 1)


def build_layernorm(nc, R, layer):
    CH = 4
    TC = NT // CH
    with ExitStack() as ctx:
        sem = lambda name: ctx.enter_context(nc.semaphore(f"ln{layer}_{name}"))
        sb = lambda name, shape: ctx.enter_context(nc.sbuf_tensor(f"ln{layer}_{name}", shape, F32))
        xn = R.xn
        total = sb("total", [P, NT])
        mean = sb("mean", [P, NT])
        sq = sb("sq", [P, TC, C])
        var = sb("var", [P, NT])
        rstd = sb("rstd", [P, NT])
        half = sb("half", [P, TC])
        chain, centred, squared, var_ready, rstd_ready, xn_ready, turned, evacuated, half_ready = (
            sem(n) for n in ("chain", "centred", "squared", "var_ready", "rstd_ready", "xn_ready", "turned", "evacuated", "half_ready"))
        block = ctx.enter_context(nc.Block())
        cs = [slice(c * TC, (c + 1) * TC) for c in range(CH)]
        wide = lambda a: a.unsqueeze(2).broadcast_to([P, TC, C])

        @block.vector
        def _(dve):
            n = [0]

            def link(ins):
                n[0] += 1
                ins.then_inc(chain, 1)
                dve.wait_ge(chain, n[0])

            def mean_of(c):
                link(nc.vector.tensor_reduce(total[:, cs[c]], R.x[:, cs[c], :], AX.X, ALU.add))
                link(nc.vector.tensor_scalar(mean[:, cs[c]], total[:, cs[c]], 1.0 / C, None, ALU.mult))
                nc.vector.tensor_tensor(xn[:, cs[c], :], R.x[:, cs[c], :], wide(mean[:, cs[c]]), ALU.subtract).then_inc(centred, 1)

            def variance(c):
                dve.wait_ge(squared, c + 1)
                link(nc.vector.tensor_reduce(total[:, cs[c]], sq[:], AX.X, ALU.add))
                nc.vector.tensor_scalar(var[:, cs[c]], total[:, cs[c]], 1.0 / C, EPS, ALU.mult, ALU.add).then_inc(var_ready, 1)

            def scale(c):
                dve.wait_ge(rstd_ready, c + 1)
                nc.vector.tensor_tensor(xn[:, cs[c], :], xn[:, cs[c], :], wide(rstd[:, cs[c]]), ALU.mult).then_inc(xn_ready, 1)

            for c in range(CH):
                mean_of(c)
                variance(c)
                if c:
                    scale(c - 1)
            scale(CH - 1)

        @block.scalar
        def _(act):
            for c in range(CH):
                act.wait_ge(centred, c + 1)
                if c:
                    act.wait_ge(var_ready, c)
                nc.scalar.activation(sq[:], xn[:, cs[c], :], ACT.Square).then_inc(squared, 1)
            for i in range(NT // 4):
                act.wait_ge(turned, i + 1)
                nc.scalar.copy(R.xnT[:, i * 4 * P:(i + 1) * 4 * P], R.ps[:, i % 4, :]).then_inc(evacuated, 1)

        @block.gpsimd
        def _(pool):
            nc.gpsimd.memset(half[:], -0.5).then_inc(half_ready, 1)
            pool.wait_ge(half_ready, 1)
            for c in range(CH):
                pool.wait_ge(var_ready, c + 1)
                nc.gpsimd.tensor_tensor(rstd[:, cs[c]], var[:, cs[c]], half[:], ALU.pow).then_inc(rstd_ready, 1)

        @block.tensor
        def _(pe):
            for i in range(NT // 4):
                pe.wait_ge(xn_ready, (4 * i) // TC + 1)
                if i >= 4:
                    pe.wait_ge(evacuated, i - 3)
                for j in range(4):
                    last = nc.tensor.transpose(R.ps[:, i % 4, j * P:(j + 1) * P], xn[:, 4 * i + j, :], R.ident[:])
                last.then_inc(turned, 1)


def build_router(nc, R, layer):
    E = EXPERTS
    with ExitStack() as ctx:
        sem = lambda name: ctx.enter_context(nc.semaphore(f"rt{layer}_{name}"))
        sb = lambda name, shape: ctx.enter_context(nc.sbuf_tensor(f"rt{layer}_{name}", shape, F32))
        logits = sb("logits", [P, NT, E])
        rest = sb("rest", [P, NT, E])
        ranked = sb("ranked", [P, NT, E])
        onehot = [sb("first", [P, NT, E]), sb("second", [P, NT, E])]
        best = sb("best", [P, 2, NT])
        top_rank = sb("top_rank", [P, NT])
        gap = sb("gap", [P, NT])
        gate = sb("gate", [P, 2, NT])
        keep = sb("keep", [P, 2, NT])
        chosen = sb("chosen", [P, NT, E])
        totals = sb("totals", [P, NT, E])
        upto = sb("upto", [P, NT, E])
        place = sb("place", [P, NT, E])
        picked = sb("picked", [P, NT, E])
        ones = sb("ones", [P, NT])
        begun = sb("begun", [P, E, NT])
        tiles = sb("tiles", [P, E])
        ends = sb("ends", [P, E])
        bases = sb("bases", [P, E])
        past = sb("past", [1, TILES, E])
        owner = sb("owner", [1, TILES])
        scored, chain, gap_ready, gap_exp, chosen_ready, counted = (
            sem(n) for n in ("scored", "chain", "gap_ready", "gap_exp", "chosen_ready", "counted"))
        block = ctx.enter_context(nc.Block())
        wide = lambda a: a.unsqueeze(2).broadcast_to([P, NT, E])
        rank_w = R.rank[:, :].unsqueeze(1).broadcast_to([P, NT, E])
        flat = lambda a: a.rearrange("p t e -> p (t e)")

        @block.tensor
        def _(pe):
            for t in range(NT):
                last = nc.tensor.matmul(R.ps[:, 0, t * E:(t + 1) * E], R.xnT[:, t * P:(t + 1) * P], R.wr[layer][:], start=True, stop=True)
            last.then_inc(scored, 1)
            pe.wait_ge(chosen_ready, 1)
            nc.tensor.matmul(R.ps[:, 1, 0:NT * E], R.before[:], flat(chosen[:]), start=True, stop=True)
            nc.tensor.matmul(R.ps[:, 2, 0:NT * E], R.ones[:], flat(chosen[:]), start=True, stop=True).then_inc(counted, 1)

        @block.scalar
        def _(act):
            act.wait_ge(gap_ready, 1)
            nc.scalar.activation(gap[:], gap[:], ACT.Exp).then_inc(gap_exp, 1)

        @block.vector
        def _(dve):
            n = [0]

            def link(ins):
                n[0] += 1
                ins.then_inc(chain, 1)
                dve.wait_ge(chain, n[0])

            def pick(k, scores):
                link(nc.vector.tensor_reduce(best[:, k, :], scores[:], AX.X, ALU.max))
                link(nc.vector.tensor_tensor(ranked[:], scores[:], wide(best[:, k, :]), ALU.is_equal))
                link(nc.vector.tensor_tensor(ranked[:], ranked[:], rank_w, ALU.mult))
                link(nc.vector.tensor_reduce(top_rank[:], ranked[:], AX.X, ALU.max))
                link(nc.vector.tensor_tensor(onehot[k][:], ranked[:], wide(top_rank[:]), ALU.is_equal))

            dve.wait_ge(scored, 1)
            link(nc.vector.tensor_copy(flat(logits[:]), R.ps[:, 0, 0:NT * E]))
            pick(0, logits)
            link(nc.vector.scalar_tensor_tensor(out=flat(rest[:]), in0=flat(onehot[0][:]), scalar=BELOW, in1=flat(logits[:]), op0=ALU.mult, op1=ALU.add))
            pick(1, rest)
            nc.vector.tensor_tensor(chosen[:], onehot[0][:], onehot[1][:], ALU.add).then_inc(chosen_ready, 1)
            nc.vector.tensor_tensor(gap[:], best[:, 1, :], best[:, 0, :], ALU.subtract).then_inc(gap_ready, 1)
            link(nc.vector.memset(ones[:], 1.0))
            dve.wait_ge(counted, 1)
            link(nc.vector.tensor_copy(flat(totals[:]), R.ps[:, 2, 0:NT * E]))
            for e in range(E):
                last = nc.vector.tensor_tensor_scan(upto[:, :, e], ones[:], totals[:, :, e], 0.0, ALU.mult, ALU.add)
            link(last)
            link(nc.vector.tensor_tensor(begun[:], upto[:, NT - 1, :].unsqueeze(2).broadcast_to([P, E, NT]),
                                         R.starts[:, 0:NT].unsqueeze(1).broadcast_to([P, E, NT]), ALU.is_gt))
            link(nc.vector.tensor_reduce(tiles[:], begun[:], AX.X, ALU.add))
            link(nc.vector.tensor_scalar(tiles[:], tiles[:], float(P), None, ALU.mult))
            link(nc.vector.tensor_tensor_scan(ends[:], ones[:, 0:E], tiles[:], 0.0, ALU.mult, ALU.add))
            link(nc.vector.tensor_tensor(bases[:], ends[:], tiles[:], ALU.subtract))
            link(nc.vector.tensor_tensor(upto[:], upto[:], totals[:], ALU.subtract))
            link(nc.vector.tensor_tensor(flat(place[:]), R.ps[:, 1, 0:NT * E], flat(upto[:]), ALU.add))
            if layer == 0:
                link(nc.vector.tensor_scalar(totals[:], place[:], float(CAP), None, ALU.is_lt))
                for k in range(TOPK):
                    link(nc.vector.tensor_tensor(picked[:], onehot[k][:], totals[:], ALU.mult))
                    link(nc.vector.tensor_reduce(keep[:, k, :], picked[:], AX.X, ALU.add))
            link(nc.vector.tensor_tensor(place[:], place[:], bases[:].unsqueeze(1).broadcast_to([P, NT, E]), ALU.add))
            for k in range(TOPK):
                link(nc.vector.tensor_tensor(picked[:], onehot[k][:], place[:], ALU.mult))
                link(nc.vector.tensor_reduce(top_rank[:], picked[:], AX.X, ALU.add))
                link(nc.vector.tensor_copy(R.slot[:, :, k], top_rank[:]))
            link(nc.vector.tensor_tensor(past[:], R.starts[0:1, :].unsqueeze(2).broadcast_to([1, TILES, E]),
                                         ends[0:1, :].unsqueeze(1).broadcast_to([1, TILES, E]), ALU.is_ge))
            link(nc.vector.tensor_reduce(owner[:], past[:], AX.X, ALU.add))
            link(nc.vector.tensor_scalar(owner[:], owner[:], float(EXPERTS - 1), None, ALU.min))
            nc.vector.tensor_copy(R.owner[:], owner[:])
            dve.wait_ge(gap_exp, 1)
            link(nc.vector.tensor_scalar(gate[:, 1, :], gap[:], 1.0, None, ALU.add))
            link(nc.vector.reciprocal(gate[:, 0, :], gate[:, 1, :]))
            link(nc.vector.tensor_tensor(gate[:, 1, :], gap[:], gate[:, 0, :], ALU.mult))
            for k in range(TOPK):
                if layer == 0:
                    nc.vector.tensor_tensor(R.gate[:, :, k], gate[:, k, :], keep[:, k, :], ALU.mult)
                else:
                    nc.vector.tensor_copy(R.gate[:, :, k], gate[:, k, :])


def build_experts(nc, R, D, layer):
    gelu = ACT.Gelu if layer else ACT.Gelu_apprx_tanh
    W1, W2, B1, B2 = 0, HIDDEN, HIDDEN + HB * C, HIDDEN + HB * C + HB
    WIDTH = B2 + C
    DEPTH = 4
    with ExitStack() as ctx:
        sem = lambda name: ctx.enter_context(nc.semaphore(f"ex{layer}_{name}"))
        sb = lambda name, shape, dt=F32: ctx.enter_context(nc.sbuf_tensor(f"ex{layer}_{name}", shape, dt))
        weights = sb("weights", [P, EXPERTS, WIDTH])
        w = [sb(f"w{q}", [P, WIDTH]) for q in range(DEPTH)]
        rows = [sb(f"rows{q}", [P, C]) for q in range(DEPTH)]
        slots = [[sb(f"slots{q}{k}", [P, 1], U32) for k in range(TOPK)] for q in range(DEPTH)]
        rowsT = [sb(f"rowsT{p}", [P, P]) for p in range(2)]
        hid = [sb(f"hid{p}", [P, HB, P]) for p in range(2)]
        result = [sb(f"result{q}", [P, C]) for q in range(DEPTH)]
        passed = R.passed
        if layer == 0:
            ones_bf, zeros_bf = sb("ones_bf", [NPIECE, HEADS * SEQ], BF16), sb("zeros_bf", [NPIECE, HEADS * SEQ], BF16)
            attn_loads, stacks_clear = sem("attn_loads"), sem("stacks_clear")
        weights_in = sem("weights_in")
        staged = sem("staged")
        scattered = [sem(f"scattered{q}") for q in range(DEPTH)]
        loaded = [sem(f"loaded{q}") for q in range(DEPTH)]
        stored = [sem(f"stored{q}") for q in range(DEPTH)]
        turned, turned_out, up, act_done, down, result_ready = (
            sem(n) for n in ("turned", "turned_out", "up", "act_done", "down", "result_ready"))
        block = ctx.enter_context(nc.Block())
        hid_ps, out_ps, turn_ps = ([R.ps[:, 2 * i + p, :] for p in range(2)] for i in range(3))

        def wait(eng, s, value):
            if not (isinstance(value, int) and value <= 0):
                eng.wait_ge(s, value)

        def lone_wait(eng, s, value):
            if not (isinstance(value, int) and value <= 0):
                eng.wait_ge(s, value)
                eng.sem_inc(passed, 1)

        def load_for_attention(sp):
            n_loads = [0]

            def load(dst, src):
                n_loads[0] += 1
                sp.dma_start(dst, src).then_inc(attn_loads, 16)
            for t, name in enumerate(("L0_attn_q1_w", "L0_attn_k1_w", "L0_attn_q2_w", "L0_attn_k2_w")):
                load(R.wqk[0][:, t, :], D[name])
            load(R.wv[0][:], D["L0_attn_v_w"])
            load(R.wo[0][:], D["L0_attn_c_w"].rearrange("(b p) d -> p b d", p=P))
            load(R.wqk[1][:, 0, :], D["L1_attn_wq"])
            load(R.wqk[1][:, 1, :], D["L1_attn_wk"])
            load(R.wv[1][:], D["L1_attn_wv"])
            load(R.wo[1][:, 0, :], D["L1_attn_wo"])
            load(R.bqk[:, 0:1], D["L1_attn_bq"])
            load(R.bqk[:, 1:2], D["L1_attn_bk"])
            load(R.bv[:], D["L1_attn_bv"])
            load(R.bo[:], D["L1_attn_bo"])
            sp.wait_ge(stacks_clear, 1)
            for par in range(2):
                for t in (1, 3):
                    load(R.stack[par][SHIFT_ROW:SHIFT_ROW + NPIECE, t, :, :], ones_bf[:].rearrange("p (h t) -> p h t", h=HEADS))
            load(D["zeros"], zeros_bf[:])
            sp.wait_ge(attn_loads, 16 * n_loads[0])

        def dispatch(eng, body):
            body(0)
            with eng.Fori(0, NT // DEPTH - 1) as i:
                body(i + 1)

        def schedule(eng, body):
            for r in range(-3, 1):
                body(0, r)
            for r in range(-3, 1):
                body(1, r)
            with eng.Fori(0, TILES // DEPTH - 3) as i:
                for r in range(-3, 1):
                    body(i + 2, r)
            for j in range(TILES // DEPTH - 1, TILES // DEPTH + 1):
                for r in range(-3, 1):
                    body(j, r)

        def at(j, r, ahead):
            turn, q = j + (r + ahead) // DEPTH, (r + ahead) % DEPTH
            if isinstance(turn, int) and not 0 <= turn < TILES // DEPTH:
                return None
            return turn, q, turn * DEPTH + q

        @block.gpsimd
        def _(pool):
            pool.wait_ge(R.list_clear, 16)

            def body(j):
                for q in range(DEPTH):
                    lone_wait(pool, staged, j * DEPTH + (q + 1))
                    for k in range(TOPK):
                        nc.gpsimd.indirect_dma_start(D["list_in"], bass.IndirectOffsetOnAxis(slots[q][k][:], 0),
                                                     rows[q][:], None).then_inc(scattered[q], 16)
            dispatch(pool, body)

        @block.sync
        def _(sp):
            for e0 in range(0, EXPERTS, 4):
                es = slice(e0, e0 + 4)
                sp.dma_start(weights[:, es, W1:W2], D[f"L{layer}_w1"][es].rearrange("e p h -> p e h")).then_inc(weights_in, 16)
                for hb in range(HB):
                    sp.dma_start(weights[:, es, W2 + hb * C:W2 + (hb + 1) * C],
                                 D[f"L{layer}_w2"][es, hb * P:(hb + 1) * P, :].rearrange("e p d -> p e d")).then_inc(weights_in, 16)
            sp.dma_start(weights[:, :, B1:B2], D[f"L{layer}_b1"].rearrange("e p h -> p e h")).then_inc(weights_in, 16)
            b2 = D[f"L{layer}_ffn_b2"]
            sp.dma_start(weights[:, :, B2:WIDTH], bass.AP(b2.tensor, b2.offset, [[0, P], [C, EXPERTS], [1, C]])).then_inc(weights_in, 16)
            if layer == 0:
                load_for_attention(sp)
            for q in range(DEPTH):
                sp.wait_ge(scattered[q], NT // DEPTH * 16 * TOPK)

            for t in range(2):
                sp.dma_start(rows[t][:], D["list_in"][t * P:(t + 1) * P, :]).then_inc(loaded[t], 16)

            def body(j, r):
                tile = at(j, r, 5)
                if tile:
                    turn, q, t = tile
                    lone_wait(sp, turned, t - (DEPTH - 1))
                    sp.dma_start(rows[q][:], D["list_in"][bass.ds(t * P, P), :]).then_inc(loaded[q], 16)
                tile = at(j, r, -1)
                if tile:
                    turn, q, t = tile
                    lone_wait(sp, result_ready, t + 1)
                    sp.dma_start(D["list_out"][bass.ds(t * P, P), :], result[q][:]).then_inc(stored[q], 16)
            schedule(sp, body)
            for q in range(DEPTH):
                sp.wait_ge(stored[q], TILES // DEPTH * 16)

        @block.tensor
        def _(pe):
            def body(j, r):
                tile = at(j, r, 2)
                if tile:
                    turn, q, t = tile
                    lone_wait(pe, loaded[q], turn * 16 + 16)
                    wait(pe, turned_out, t - 1)
                    nc.tensor.transpose(turn_ps[q % 2][:, 0:P], rows[q][:], R.ident[:]).then_inc(turned, 1)
                tile = at(j, r, 1)
                if tile:
                    turn, q, t = tile
                    lone_wait(pe, turned_out, t + 1)
                    lone_wait(pe, act_done, t - 1)
                    for hb in range(HB):
                        last = nc.tensor.matmul(hid_ps[q % 2][:, hb * P:(hb + 1) * P], w[q][:, W1 + hb * P:W1 + (hb + 1) * P],
                                                rowsT[q % 2][:], start=True, stop=True)
                    last.then_inc(up, 1)
                tile = at(j, r, 0)
                if tile:
                    turn, q, t = tile
                    lone_wait(pe, act_done, t + 1)
                    lone_wait(pe, result_ready, t - 1)
                    for hb in range(HB):
                        last = nc.tensor.matmul(out_ps[q % 2][:, 0:C], hid[q % 2][:, hb, :], w[q][:, W2 + hb * C:W2 + (hb + 1) * C],
                                                start=(hb == 0), stop=(hb == HB - 1))
                    last.then_inc(down, 1)
            schedule(pe, body)

        @block.scalar
        def _(act):
            if layer == 0:
                spread = lambda a, shape: a.unsqueeze(1).broadcast_to(shape)
                nc.scalar.copy(ones_bf[:].rearrange("p (n c) -> p n c", c=C), spread(R.ones[0:NPIECE, :], [NPIECE, HEADS * SEQ // C, C]))
                nc.scalar.copy(zeros_bf[:].rearrange("p (n c) -> p n c", c=C), spread(R.zero_tile[0:NPIECE, :], [NPIECE, HEADS * SEQ // C, C]))
                for par in range(2):
                    for t in range(4):
                        last = nc.scalar.copy(R.stack[par][:, t, :, :].rearrange("p h (n c) -> p (h n) c", c=C),
                                              spread(R.zero_tile[:], [P, HEADS * SEQ // C, C]))
                last.then_inc(stacks_clear, 1)

            def body(j, r):
                tile = at(j, r, 1)
                if tile:
                    turn, q, t = tile
                    lone_wait(act, down, t - 1)
                    act.wait_ge(up, t + 1)
                    for hb in range(HB):
                        last = nc.scalar.activation(hid[q % 2][:, hb, :], hid_ps[q % 2][:, hb * P:(hb + 1) * P], gelu,
                                                    bias=w[q][:, B1 + hb:B1 + hb + 1])
                    last.then_inc(act_done, 1)
            schedule(act, body)

        @block.vector
        def _(dve):
            def stage(j):
                for q in range(DEPTH):
                    lone_wait(dve, scattered[q], j * (16 * TOPK))
                    nc.vector.tensor_copy(rows[q][:], R.xn[:, bass.ds(j * DEPTH + q, 1), :].rearrange("p o c -> p (o c)"))
                    for k in range(TOPK):
                        last = nc.vector.tensor_copy(slots[q][k][:], R.slot[:, bass.ds(j * DEPTH + q, 1), k])
                    last.then_inc(staged, 1)
            dispatch(dve, stage)
            dve.wait_ge(weights_in, 16 * 12)

            def body(j, r):
                tile = at(j, r, 2)
                if tile:
                    turn, q, t = tile
                    dve.wait_ge(turned, t + 1)
                    nc.vector.tensor_copy(rowsT[q % 2][:], turn_ps[q % 2][:, 0:P]).then_inc(turned_out, 1)
                tile = at(j, r, 3)
                if tile:
                    turn, q, t = tile
                    lone_wait(dve, result_ready, t - (DEPTH - 1))
                    e = dve.value_load(R.owner[0:1, bass.ds(t, 1)], min_val=0, max_val=EXPERTS - 1)
                    nc.vector.tensor_copy(w[q][:], weights[:, bass.ds(e, 1), :].rearrange("p o w -> p (o w)"))
                tile = at(j, r, 0)
                if tile:
                    turn, q, t = tile
                    lone_wait(dve, stored[q], turn * 16)
                    dve.wait_ge(down, t + 1)
                    nc.vector.tensor_tensor(result[q][:], out_ps[q % 2][:, 0:C], w[q][:, B2:WIDTH], ALU.add).then_inc(result_ready, 1)
            schedule(dve, body)


def build_attention(nc, R, D, layer):
    A = 2 if layer == 0 else 1
    T = 2 * A
    VD = HD * (2 if layer == 0 else 1)
    VW = 32
    STRIPS = P // VW
    DV = HEADS * VD
    DB = DV // P
    UNITS = 6 * A
    BANKS = 2 * UNITS
    GROUPS = 2 * A
    LOADS = (len(RUNS) * 2 + 1) * 16
    SHIFTS = (NPIECE if layer else A) * 16
    LAST = BATCH - 1

    if layer == 0:
        ORDER = (("qk0", 0), ("qk1", 1), ("turn10", 2), ("turn11", 2), ("v", 5),
                 ("turn00", 8), ("turn01", 8), ("shift", 9), ("rows", 11), ("out", 11))
        DIVIDE = {3: 1, 9: 0}
        SIGMOID = 8
        LEAD_SLOTS = 9
        SPLIT = {2: (0,), 3: (1,), 4: (2,)}
    else:
        ORDER = (("qk0", 0), ("qk1", 0), ("turn00", 2), ("turn01", 2), ("v", 3), ("shift", 4), ("rows", 4), ("out", 5))
        DIVIDE = {3: 0}
        SIGMOID = 5
        LEAD_SLOTS = 5
        SPLIT = {0: (0,), 1: (1, 2)}
    SLOT = dict(ORDER)
    NAMES = [n for n, _ in ORDER]
    USES = len(NAMES)
    LEAD = {n: tuple(range(-(-n * UNITS // LEAD_SLOTS), -(-(n + 1) * UNITS // LEAD_SLOTS))) for n in range(LEAD_SLOTS)}
    LAST_LEAD = max(LEAD)

    def has(step, name):
        if not isinstance(step, int):
            return True
        if name.startswith("qk"):
            return step + 2 <= LAST
        if name in ("v", "shift", "maxima"):
            return 0 <= step + 1 <= LAST
        if name in ("rows", "out", "last", f"turn{A - 1}0", f"turn{A - 1}1"):
            return 0 <= step - 1 <= LAST
        return 0 <= step <= LAST

    FIRST_FULL = 2

    def use(step, name):
        if isinstance(step, int):
            before = sum(has(t, n) for t in range(-2, step) for n in NAMES)
            return before + sum(has(step, n) for n in NAMES[:NAMES.index(name)])
        return step * USES + (use(FIRST_FULL, NAMES[0]) - FIRST_FULL * USES + NAMES.index(name))

    with ExitStack() as ctx:
        sem = lambda name: ctx.enter_context(nc.semaphore(f"at{layer}_{name}"))

        def sb(name, shape, dt=F32):
            return ctx.enter_context(nc.sbuf_tensor(f"at{layer}_{name}", shape, dt))

        xb = [sb(f"xb{p}", [P, SEQ]) for p in range(2)]
        whole = sb("whole", [P, T, SEQ])
        pieces = sb("pieces", [P, T, NPIECE, SEQ], BF16)
        v = [sb(f"v{p}", [P, QB, HEADS, VW]) for p in range(2)]
        maxima = sb("maxima", [P, QB, A * HEADS])
        shift = [sb(f"shift{p}", [P, QB, A * HEADS]) for p in range(2)]
        shift_t = sb("shift_t", [A * HEADS, SEQ])
        shift_r = sb("shift_r", [A * HEADS, SEQ])
        shift_p = sb("shift_p", [A * HEADS, NPIECE, SEQ], BF16)
        probs = sb("probs", [P, 2, 3, 1024])
        weighed_t = sb("weighed_t", [P, A, GROUPS // A, 2, SEQ])
        weighed_q = sb("weighed_q", [P, A, QB, HEADS, VD + 1])
        rsum_all = sb("rsum", [P, A, QB, HEADS])
        out_rows = sb("out_rows", [P, QB, DV])
        yT = sb("yT", [P, DB, SEQ])
        s_rows = sb("s_rows", [P, QB, C])
        slot = sb("slot", [P, QB * TOPK], U32)
        chosen_y = [[sb(f"chosen_y{t}{k}", [P, C]) for k in range(TOPK)] for t in range(QB)]
        ffn = sb("ffn", [P, QB, C])
        silu = sb("silu", [P, QB, C])
        if layer == 0:
            y = [sb(f"y{a}", [P, QB, HEADS, VD]) for a in range(A)]
            sq = sb("sq", [P, QB, HEADS, VD])
            stat = sb("stat", [P, QB * HEADS])
            rstd = sb("rstd", [P, QB * HEADS])
            half = sb("half", [P, QB * HEADS])
        else:
            zero_exp = [sb(f"zero_exp{p}", [P, HEADS]) for p in range(2)]

        passed = R.passed
        v_clear, v_ones = sem("v_clear"), sem("v_ones")
        xb_ready = sem("xb_ready")
        g_full, g_free = sem("g_full"), sem("g_free")
        split_chain = sem("split_chain")
        pieces_ready = sem("pieces_ready")
        pieces_out = sem("pieces_out")
        stacked = [sem(f"stacked{a}") for a in range(A)]
        s_full, s_free = sem("s_full"), sem("s_free")
        shift_ready = sem("shift_ready")
        shift_chain = sem("shift_chain")
        shift_p_ready = sem("shift_p_ready")
        shift_out, shift_in = sem("shift_out"), sem("shift_in")
        t_full, t_free = sem("t_full"), sem("t_free")
        weighed = sem("weighed")
        y_free = sem("y_free")
        divided = sem("divided")
        div_chain = sem("div_chain")
        rows_ready = sem("rows_ready") if layer == 0 else divided
        if layer == 0:
            norm_chain, rstd_ready, half_ready = sem("norm_chain"), sem("rstd_ready"), sem("half_ready")
        slot_ready = sem("slot_ready")
        gathered = sem("gathered")
        mix_chain = sem("mix_chain")
        ffn_ready = sem("ffn_ready")
        silu_exp, silu_chain, silu_ready = sem("silu_exp"), sem("silu_chain"), sem("silu_ready")
        times_g = sem("times_g")
        gated = sem("gated")
        if layer == 1:
            stored = sem("stored")
            zero_ready = sem("zero_ready")
            max_ready = sem("max_ready")
        block = ctx.enter_context(nc.Block())

        stack = R.stack
        G = [R.ps[:, i, :] for i in range(2)]
        s_bank, t_bank = ([R.ps[:, 2 * u + i, :] for i in range(2)] for u in (1, 2))
        Y = [R.ps[:, 6 + i, :].rearrange("p (f s) -> p f s", f=2) for i in range(2)]
        scr, mscr = D["scratch_pieces"], D["scratch_shift"]

        def bank_of(step, name):
            return G[use(step if isinstance(step, int) else FIRST_FULL, name) % 2]

        def wait(eng, s, value):
            if not (isinstance(value, int) and value <= 0):
                eng.wait_ge(s, value)

        def lone_wait(eng, s, value):
            if not (isinstance(value, int) and value <= 0):
                eng.wait_ge(s, value)
                eng.sem_inc(passed, 1)

        def schedule(eng, body):
            for step in (-2, -1, 0, 1):
                body(step, step % 4)
            with eng.Fori(0, (LAST - 3) // 4) as j:
                for r in range(4):
                    body(j * 4 + (FIRST_FULL + r), (FIRST_FULL + r) % 4)
            for step in range(LAST - 1, LAST + 2):
                body(step, step % 4)

        def stack_of(r, a, tensor):
            return stack[r % 2][:, 2 * (r // 2 % 2 if layer else a) + tensor]

        @block.gpsimd
        def _(pool):
            def head_norm(b):
                LINKS = 5 + 2 * 4
                n = [0]

                def link(ins):
                    n[0] += 1
                    ins.then_inc(norm_chain, 1)
                    lone_wait(pool, norm_chain, b * LINKS + n[0])
                y0, y1, sqv = (t[:].rearrange("p q h d -> p (q h) d") for t in (*y, sq))
                wide = lambda a: a.unsqueeze(2).broadcast_to([P, QB * HEADS, VD])

                def add_up(values):
                    w = VD // 2
                    while w:
                        dst = sqv[:, :, 0:w] if w > 1 else stat[:].unsqueeze(2)
                        link(nc.gpsimd.tensor_tensor(dst, values[:, :, 0:w], values[:, :, w:2 * w], ALU.add))
                        values, w = sqv, w // 2

                lone_wait(pool, divided, b * A + A)
                link(nc.gpsimd.tensor_tensor(y0, y0, y1, ALU.subtract))
                add_up(y0)
                link(nc.gpsimd.tensor_scalar(stat[:], stat[:], 1.0 / VD, None, ALU.mult))
                link(nc.gpsimd.tensor_tensor(y0, y0, wide(stat[:]), ALU.subtract))
                link(nc.gpsimd.tensor_tensor(sqv, y0, y0, ALU.mult))
                add_up(sqv)
                k2 = (1.0 - LAMBDA_INIT) ** -2
                link(nc.gpsimd.tensor_scalar(stat[:], stat[:], k2 / VD, k2 * EPS, ALU.mult, ALU.add))
                assert n[0] == LINKS
                nc.gpsimd.tensor_tensor(rstd[:], stat[:], half[:], ALU.pow).then_inc(rstd_ready, 1)
                lone_wait(pool, rstd_ready, b + 1)
                nc.gpsimd.tensor_tensor(out_rows[:].rearrange("p q (h d) -> p (q h) d", d=VD), y0, wide(rstd[:]), ALU.mult).then_inc(rows_ready, 1)

            def fetch_ffn(b):
                nc.gpsimd.tensor_copy(slot[:].rearrange("p (t k) -> p t k", k=TOPK), R.slot[:, bass.ds(b * QB, QB), :]).then_inc(slot_ready, 1)
                lone_wait(pool, slot_ready, b + 1)
                for t in range(QB):
                    for k in range(TOPK):
                        i = t * TOPK + k
                        nc.gpsimd.indirect_dma_start(chosen_y[t][k][:], None, D["list_out"],
                                                     bass.IndirectOffsetOnAxis(slot[:, i:i + 1], 0)).then_inc(gathered, 16)

            def mix_ffn(b):
                lone_wait(pool, gathered, (b + 1) * (16 * QB * TOPK))
                for t in range(QB):
                    for k in range(TOPK):
                        coef = R.gate[:, bass.ds(b * QB + t, 1), k].broadcast_to([P, C])
                        nc.gpsimd.tensor_tensor(chosen_y[t][k][:], chosen_y[t][k][:], coef, ALU.mult).then_inc(mix_chain, 1)
                lone_wait(pool, mix_chain, b * 6 + 4)
                for t in range(QB):
                    nc.gpsimd.tensor_tensor(ffn[:, t, :], chosen_y[t][0][:], chosen_y[t][1][:], ALU.add).then_inc(mix_chain, 1)
                lone_wait(pool, mix_chain, b * 6 + 6)
                pool.sem_inc(ffn_ready, 1)

            def gate(step, b):
                tiles = bass.ds(b * QB, QB)
                lone_wait(pool, g_free, use(step, "out") + 1)
                nc.gpsimd.tensor_tensor(s_rows[:], s_rows[:], ffn[:], ALU.mult).then_inc(times_g, 1)
                lone_wait(pool, silu_ready, b + 1)
                lone_wait(pool, times_g, b * 2 + 1)
                nc.gpsimd.tensor_tensor(s_rows[:], s_rows[:], silu[:], ALU.mult).then_inc(times_g, 1)
                lone_wait(pool, times_g, b * 2 + 2)
                nc.gpsimd.tensor_tensor(R.x[:, tiles, :], R.x[:, tiles, :], s_rows[:], ALU.add).then_inc(gated, 1)

            if layer == 0:
                nc.gpsimd.memset(half[:], -0.5).then_inc(half_ready, 1)
                pool.wait_ge(half_ready, 1)
            for vt in v:
                nc.gpsimd.memset(vt[:], 0.0).then_inc(v_clear, 1)
            pool.wait_ge(v_clear, 2)
            for vt in v:
                nc.gpsimd.memset(vt[:, :, :, VD:VD + 1], 1.0).then_inc(v_ones, 1)

            def body(step, r):
                if has(step, "out"):
                    mix_ffn(step - 1)
                if has(step, "rows") and layer == 0:
                    head_norm(step - 1)
                if has(step, "now"):
                    fetch_ffn(step)
                if has(step, "out"):
                    gate(step, step - 1)
            schedule(pool, body)

        @block.sync
        def _(sp):
            def store_pieces(b):
                for a in range(A):
                    lone_wait(sp, stacked[a], b * LOADS)
                lone_wait(sp, pieces_ready, b + 1)
                sp.dma_start(scr.rearrange("t c p s -> p t c s")[:, 0:T], pieces[:]).then_inc(pieces_out, 16)

            def fill_stack(step, b, r, a):
                lone_wait(sp, pieces_out, b * 16 + 16)
                lone_wait(sp, t_full, step * BANKS if layer else step * BANKS + 12 * (a + 1))
                for tensor, which in enumerate((Q_PIECE, K_PIECE)):
                    for first, n in RUNS:
                        piece = scr[2 * a + tensor, which[first]]
                        src = bass.AP(piece.tensor, piece.offset, [[C * SEQ if tensor else 0, n], [HEADS * SEQ, HD], [1, HEADS * SEQ]])
                        sp.dma_start(stack_of(r, a, tensor)[first * HD:(first + n) * HD].rearrange("r h s -> r (h s)"), src).then_inc(stacked[a], 16)
                sp.dma_start(stack_of(r, a, 0)[SHIFT_ROW:SHIFT_ROW + NPIECE],
                             D["zeros"].rearrange("p (h t) -> p h t", h=HEADS)).then_inc(stacked[a], 16)

            def fill_shift(b, r):
                lone_wait(sp, shift_p_ready, b + 1)
                if layer == 0:
                    lone_wait(sp, shift_in, b * SHIFTS)
                    sp.dma_start(mscr, shift_p[:]).then_inc(shift_out, 16)
                    lone_wait(sp, shift_out, b * 16 + 16)
                    for a in range(A):
                        sp.dma_start(stack_of(r, a, 0)[SHIFT_ROW:SHIFT_ROW + NPIECE],
                                     mscr[a * HEADS:(a + 1) * HEADS].rearrange("h c s -> c h s")).then_inc(shift_in, 16)
                else:
                    for c in range(NPIECE):
                        row = SHIFT_ROW + c
                        sp.dma_start(stack_of(r, 0, 0)[row:row + 1], shift_p[:, c, :]).then_inc(shift_in, 16)

            def store(b):
                lone_wait(sp, gated, b + 1)
                sp.dma_start(D["out"][bass.ds(b * QB, QB)].rearrange("t p c -> p t c"), R.x[:, bass.ds(b * QB, QB), :]).then_inc(stored, 16)

            def body(step, r):
                if has(step, "qk0"):
                    store_pieces(step + 2)
                    fill_stack(step, step + 2, r + 2, 0)
                if has(step, "shift"):
                    fill_shift(step + 1, r + 1)
                if has(step, "qk0") and layer == 0:
                    fill_stack(step, step + 2, r + 2, 1)
                if has(step, "out") and layer == 1:
                    store(step - 1)
            schedule(sp, body)
            sp.wait_ge(shift_in, SHIFTS * BATCH)
            if layer == 1:
                sp.wait_ge(stored, 16 * BATCH)

        @block.tensor
        def _(pe):
            def general(step, name):
                lone_wait(pe, g_free, use(step, name) - 1)
                return bank_of(step, name)

            def project_qk(step, b, p, i):
                pe.wait_ge(xb_ready, b + 1)
                bank = general(step, f"qk{i}")
                for a in range(A):
                    last = nc.tensor.matmul(bank[:, a * SEQ:(a + 1) * SEQ], R.wqk[layer][:, A * i + a, :], xb[p][:], start=True, stop=True)
                last.then_inc(g_full, 1)

            def project_v(step, p):
                bank = general(step, "v")
                for kb in range(QB):
                    last = nc.tensor.matmul(bank[:, kb * DV:(kb + 1) * DV], xb[p][:, kb * P:(kb + 1) * P], R.wv[layer][:],
                                            start=True, stop=(layer == 0))
                    if layer:
                        last = nc.tensor.matmul(bank[:, kb * DV:(kb + 1) * DV], R.ones[0:1, :], R.bv[0:1, :], start=False, stop=True)
                last.then_inc(g_full, 1)

            def masked_scores(bank, per, masked, mask, products):
                bank = bank.rearrange("p (m w) -> p m w", m=per)
                nc.tensor.matmul(bank[:, :, masked], R.ident_bf[:], mask, start=True, stop=True)
                for m, (lhs, rhs) in enumerate(products):
                    last = nc.tensor.matmul(bank[:, m, :], lhs, rhs, start=False, stop=True, skip_group_check=True)
                return last

            def scores_for_max(b, batch_r, n, i):
                a, r = divmod(n, 6)
                q, k = (stack_of(batch_r, a, tensor) for tensor in range(2))
                late = int(r >= 2)
                per, w = 4 // (late + 1), P * (late + 1)
                if r == 0:
                    pe.wait_ge(stacked[a], b * LOADS + LOADS)
                lone_wait(pe, s_free, b * BANKS + (2 * n + i - 1))
                h0 = (2 * (r - 2 * late) + i) * per
                prod = [(q[:, h, late * P:(late + 1) * P], k[:, h, 0:w]) for h in range(h0, h0 + per)]
                if not late:
                    last = masked_scores(s_bank[i], per, slice(0, P), R.mask_diag_q[:], prod)
                elif layer == 0:
                    last = masked_scores(s_bank[i], per, slice(P, SEQ), R.mask_diag_q[:, 0:2, :], prod)
                else:
                    last = masked_scores(s_bank[i], per, slice(0, SEQ), R.mask_late_q[:], prod)
                last.then_inc(s_full, 1)

            def scores(b, batch_r, n, i):
                g, part = divmod(n, 3)
                a, group = divmod(g, 2)
                q, k = (stack_of(batch_r, a, tensor) for tensor in range(2))
                if n == 0 and i == 0:
                    pe.wait_ge(shift_in, b * SHIFTS + SHIFTS)
                lone_wait(pe, t_free, b * BANKS + (2 * n + i - 1))
                if part < 2:
                    h0 = group * 8 + part * 4 + i * 2
                    prod = [(k[:, h, 0:P], q[:, h, :]) for h in (h0, h0 + 1)]
                    if layer == 0:
                        last = masked_scores(t_bank[i], 2, slice(0, P), R.mask_diag_k[:, 0:2, :], prod)
                    else:
                        last = masked_scores(t_bank[i], 2, slice(0, SEQ), R.mask_early_k[:], prod)
                else:
                    h0 = group * 8 + i * 4
                    prod = [(k[:, h, P:SEQ], q[:, h, P:SEQ]) for h in range(h0, h0 + 4)]
                    last = masked_scores(t_bank[i], 4, slice(0, P), R.mask_diag_k[:], prod)
                last.then_inc(t_full, 1)

            def weigh(b, p, g, part):
                a, group = divmod(g, 2)
                if part == 0:
                    pe.wait_ge(t_free, b * BANKS + 6 * (g + 1))
                    lone_wait(pe, y_free, b * GROUPS + (g - 1))
                pr = probs[:, g % 2]
                for late in range(2):
                    for j in range(STRIPS):
                        h = group * 8 + part * 4 + j
                        strip = Y[g % 2][j * VW:(j + 1) * VW, part, :]
                        if not late:
                            nc.tensor.matmul(strip, v[p][:, 0, h, :], pr[:, part, j * SEQ:(j + 1) * SEQ], start=True, stop=False)
                        else:
                            i = part * 4 + j
                            last = nc.tensor.matmul(strip[:, P:SEQ], v[p][:, 1, h, :], pr[:, 2, i * P:(i + 1) * P], start=False, stop=True)
                last.then_inc(weighed, 1)

            def turn_weighed(step, b, a, qb):
                pe.wait_ge(y_free, b * GROUPS + 2 * (a + 1))
                bank = general(step, f"turn{a}{qb}")
                for i in range(4):
                    last = nc.tensor.transpose(bank[:, i * P:(i + 1) * P], weighed_t[:, a, i // 2, i % 2, qb * P:(qb + 1) * P], R.ident[:])
                last.then_inc(g_full, 1)

            def turn_rows(step, b):
                bank = general(step, "rows")
                pe.wait_ge(rows_ready, b + 1)
                for db in range(DB):
                    for qb in range(QB):
                        last = nc.tensor.transpose(bank[:, (db * QB + qb) * P:(db * QB + qb + 1) * P], out_rows[:, qb, db * P:(db + 1) * P], R.ident[:])
                last.then_inc(g_full, 1)

            def turn_shift(step, b, p):
                bank = general(step, "shift")
                pe.wait_ge(shift_ready, b + 1)
                for qb in range(QB):
                    last = nc.tensor.transpose(bank[0:A * HEADS, qb * P:(qb + 1) * P], shift[p][:, qb, :], R.ident[:])
                last.then_inc(g_full, 1)

            def project_out(step):
                bank = general(step, "out")
                lone_wait(pe, g_free, use(step, "rows") + 1)
                for qb in range(QB):
                    for db in range(DB):
                        last = nc.tensor.matmul(bank[:, qb * C:(qb + 1) * C], yT[:, db, qb * P:(qb + 1) * P], R.wo[layer][:, db, :],
                                                start=(db == 0), stop=(db == DB - 1 and layer == 0))
                    if layer:
                        last = nc.tensor.matmul(bank[:, qb * C:(qb + 1) * C], R.ones[0:1, :], R.bo[0:1, :], start=False, stop=True)
                last.then_inc(g_full, 1)

            pe.wait_ge(v_ones, 2)

            def general_use(step, r, name):
                if name.startswith("qk"):
                    project_qk(step, step + 2, r % 2, int(name[2]))
                elif name == "v":
                    project_v(step, 1 - r % 2)
                elif name.startswith("turn"):
                    a = int(name[4])
                    turn_weighed(step, step - 1 if a == A - 1 else step, a, int(name[5]))
                elif name == "shift":
                    turn_shift(step, step + 1, 1 - r % 2)
                elif name == "rows":
                    turn_rows(step, step - 1)
                else:
                    project_out(step)

            def body(step, r):
                par = r % 2
                for n in range(UNITS):
                    lead = [(m, i) for m in LEAD.get(n, ()) for i in range(2)] if has(step, "maxima") else []
                    for i in range(2):
                        before = len(lead) // 2 if len(lead) == 2 else 1 if i == 0 else 2
                        for m, bank in lead[0:before] if i == 0 else lead[1:1 + before]:
                            scores_for_max(step + 1, r + 1, m, bank)
                        if has(step, "now"):
                            scores(step, r, n, i)
                    for m, bank in lead[3:4]:
                        scores_for_max(step + 1, r + 1, m, bank)
                    if n < 2 and has(step, "last"):
                        weigh(step - 1, 1 - par, GROUPS - 1, n)
                    if has(step, "now") and n >= 3 and n % 3 < 2:
                        weigh(step, par, n // 3 - 1, n % 3)
                    for name in NAMES:
                        if has(step, name) and n == SLOT[name]:
                            general_use(step, r, name)
            schedule(pe, body)

        @block.scalar
        def _(act):
            act.wait_ge(v_ones, 2)

            def copy_tokens(step, b, p):
                if not isinstance(step, int) or step >= 0:
                    lone_wait(act, g_full, use(step - 1, "v") + 1)
                nc.scalar.copy(xb[p][:], R.xnT[:, bass.ds(b * SEQ, SEQ)]).then_inc(xb_ready, 1)

            def copy_qk(step, b, i):
                if i == 0:
                    lone_wait(act, pieces_out, b * 16)
                bank = bank_of(step, f"qk{i}")
                act.wait_ge(g_full, use(step, f"qk{i}") + 1)
                if layer:
                    nc.scalar.activation(whole[:, i, :], bank[:, 0:SEQ], ACT.Identity, bias=R.bqk[:, i:i + 1])
                    nc.scalar.activation(pieces[:, i, 0, :], bank[:, 0:SEQ], ACT.Identity, bias=R.bqk[:, i:i + 1]).then_inc(g_free, 1)
                else:
                    src = bank.rearrange("p (t s) -> p t s", t=A)
                    nc.scalar.copy(whole[:, A * i:A * i + A, :], src)
                    nc.scalar.copy(pieces[:, A * i:A * i + A, 0, :], src).then_inc(g_free, 1)

            def copy_v(step, p):
                lone_wait(act, weighed, step * (2 * GROUPS))
                act.wait_ge(g_full, use(step, "v") + 1)
                nc.scalar.copy(v[p][:, :, :, 0:VD], bank_of(step, "v")[:, 0:QB * DV].rearrange("p (k h d) -> p k h d", k=QB, d=VD)).then_inc(g_free, 1)

            def exp(b, n):
                if n % 3 == 0:
                    lone_wait(act, weighed, b * (2 * GROUPS) + 2 * (n // 3 - 1))
                for i in range(2):
                    act.wait_ge(t_full, b * BANKS + (2 * n + i + 1))
                    nc.scalar.activation(probs[:, (n // 3) % 2, n % 3, i * 512:(i + 1) * 512], t_bank[i], ACT.Exp, scale=SCALE).then_inc(t_free, 1)

            def copy_weighed(b, g):
                act.wait_ge(weighed, b * (2 * GROUPS) + 2 * (g + 1))
                nc.scalar.copy(weighed_t[:, g // 2, g % 2, :, :], Y[g % 2]).then_inc(y_free, 1)

            def exp_ffn(b):
                act.wait_ge(ffn_ready, b + 1)
                nc.scalar.activation(silu[:], ffn[:], ACT.Exp, scale=-1.0).then_inc(silu_exp, 1)

            def copy_rows(step):
                act.wait_ge(g_full, use(step, "rows") + 1)
                nc.scalar.copy(yT[:].rearrange("p b s -> p (b s)"), bank_of(step, "rows")[:, 0:DB * SEQ]).then_inc(g_free, 1)

            def copy_turned(step, b, a, qb):
                if qb == 0:
                    lone_wait(act, divided, (b - 1) * A + a + 1)
                act.wait_ge(g_full, use(step, f"turn{a}{qb}") + 1)
                nc.scalar.copy(weighed_q[:, a, qb, :, :], bank_of(step, f"turn{a}{qb}").rearrange("p (h d) -> p h d", d=VW)[:, :, 0:VD + 1]).then_inc(g_free, 1)

            def copy_shift(step, b, p):
                if layer == 0:
                    lone_wait(act, shift_out, b * 16)
                else:
                    lone_wait(act, shift_in, b * SHIFTS)
                act.wait_ge(g_full, use(step, "shift") + 1)
                src = bank_of(step, "shift")[0:A * HEADS, 0:SEQ]
                nc.scalar.copy(shift_t[:], src)
                nc.scalar.copy(shift_p[:, 0, :], src).then_inc(g_free, 1)
                if layer:
                    lone_wait(act, divided, b - 1)
                    nc.scalar.activation(zero_exp[p][:], shift[p][:, 0, :], ACT.Exp, scale=SCALE).then_inc(zero_ready, 1)

            def copy_out(step, b):
                act.wait_ge(g_full, use(step, "out") + 1)
                nc.scalar.copy(s_rows[:], bank_of(step, "out")[:, 0:QB * C].rearrange("p (t c) -> p t c", t=QB)).then_inc(g_free, 1)

            def general_use(step, r, name):
                if name.startswith("qk"):
                    copy_qk(step, step + 2, int(name[2]))
                elif name == "v":
                    copy_v(step, 1 - r % 2)
                elif name.startswith("turn"):
                    a = int(name[4])
                    copy_turned(step, step - 1 if a == A - 1 else step, a, int(name[5]))
                elif name == "shift":
                    copy_shift(step, step + 1, 1 - r % 2)
                elif name == "rows":
                    copy_rows(step)
                else:
                    copy_out(step, step - 1)

            def body(step, r):
                if has(step, "qk0"):
                    copy_tokens(step, step + 2, r % 2)
                for n in range(UNITS):
                    if has(step, "now"):
                        exp(step, n)
                    if n == 1 and has(step, "last"):
                        copy_weighed(step - 1, GROUPS - 1)
                    if has(step, "now") and n >= 3 and n % 3 == 1:
                        copy_weighed(step, n // 3 - 1)
                    if has(step, "out") and n == SIGMOID - 1:
                        exp_ffn(step - 1)
                    for name in NAMES:
                        if has(step, name) and n == SLOT[name]:
                            general_use(step, r, name)
            schedule(act, body)

        @block.vector
        def _(dve):
            def split(step, b, part):
                if part == 0:
                    dve.wait_ge(g_free, use(step, "qk1") + 1)
                    nc.vector.tensor_tensor(whole[:], whole[:], pieces[:, :, 0, :], ALU.subtract).then_inc(split_chain, 1)
                elif part == 1:
                    dve.wait_ge(split_chain, b * 2 + 1)
                    nc.vector.tensor_copy(pieces[:, :, 1, :], whole[:]).then_inc(split_chain, 1)
                else:
                    dve.wait_ge(split_chain, b * 2 + 2)
                    nc.vector.tensor_tensor(pieces[:, :, 2, :], whole[:], pieces[:, :, 1, :], ALU.subtract).then_inc(pieces_ready, 1)

            def search(b, n):
                a, r = divmod(n, 6)
                late = int(r >= 2)
                heads = 4 // (late + 1)
                for i in range(2):
                    h0 = a * HEADS + (2 * (r - 2 * late) + i) * heads
                    dve.wait_ge(s_full, b * BANKS + (2 * n + i + 1))
                    nc.vector.tensor_reduce(maxima[:, late, h0:h0 + heads], s_bank[i].rearrange("p (m k) -> p m k", k=P * (late + 1)),
                                            AX.X, ALU.max).then_inc(s_free, 1)

            def negate(b, p):
                dve.wait_ge(s_free, b * BANKS + BANKS)
                if layer:
                    nc.vector.tensor_scalar(maxima[:, 0, :], maxima[:, 0, :], R.no_outside[:, 0:1], None, ALU.max).then_inc(max_ready, 1)
                    dve.wait_ge(max_ready, b + 1)
                nc.vector.tensor_scalar(shift[p][:], maxima[:], -1.0, None, ALU.mult).then_inc(shift_ready, 1)

            def split_shift(step, b):
                dve.wait_ge(g_free, use(step, "shift") + 1)
                nc.vector.tensor_tensor(shift_r[:], shift_t[:], shift_p[:, 0, :], ALU.subtract).then_inc(shift_chain, 1)
                dve.wait_ge(shift_chain, b * 2 + 1)
                nc.vector.tensor_copy(shift_p[:, 1, :], shift_r[:]).then_inc(shift_chain, 1)
                dve.wait_ge(shift_chain, b * 2 + 2)
                nc.vector.tensor_tensor(shift_p[:, 2, :], shift_r[:], shift_p[:, 1, :], ALU.subtract).then_inc(shift_p_ready, 1)

            def sigmoid(b):
                dve.wait_ge(silu_exp, b + 1)
                nc.vector.tensor_scalar(silu[:], silu[:], 1.0, None, ALU.add).then_inc(silu_chain, 1)
                dve.wait_ge(silu_chain, b + 1)
                nc.vector.reciprocal(silu[:], silu[:]).then_inc(silu_ready, 1)

            def divide(step, b, p, a):
                LINKS = 3
                n = [1 if layer == 0 and a else 0]

                def link(ins):
                    n[0] += 1
                    ins.then_inc(div_chain, 1)
                    dve.wait_ge(div_chain, b * LINKS + n[0])
                wide = lambda a: a.unsqueeze(3).broadcast_to([P, QB, HEADS, VD])
                w, rsum = weighed_q[:, a], rsum_all[:, a]
                dve.wait_ge(g_free, use(step, f"turn{a}1") + 1)
                if layer == 0:
                    link(nc.vector.reciprocal(rsum, w[:, :, :, VD]))
                    if a == 0:
                        wait(dve, rows_ready, b)
                    else:
                        link(nc.vector.tensor_tensor(rsum, rsum, R.lam[:].unsqueeze(1).broadcast_to([P, QB, HEADS]), ALU.mult))
                    nc.vector.tensor_tensor(y[a][:], w[:, :, :, 0:VD], wide(rsum), ALU.mult).then_inc(divided, 1)
                else:
                    dve.wait_ge(zero_ready, b + 1)
                    nc.vector.scalar_tensor_tensor(out=rsum[:, 0, :], in0=zero_exp[p][:], scalar=R.outside[:, 0:1], in1=w[:, 0, :, VD],
                                                   op0=ALU.mult, op1=ALU.add).then_inc(div_chain, 1)
                    n[0] += 1
                    link(nc.vector.tensor_copy(rsum[:, 1, :], w[:, 1, :, VD]))
                    link(nc.vector.reciprocal(rsum, rsum))
                    nc.vector.tensor_tensor(out_rows[:].rearrange("p q (h d) -> p q h d", d=VD), w[:, :, :, 0:VD], wide(rsum), ALU.mult).then_inc(divided, 1)
                assert n[0] == (LINKS if a == A - 1 else 1)

            def body(step, r):
                par = r % 2
                for n in range(UNITS):
                    if has(step, "maxima"):
                        for m in LEAD.get(n, ()):
                            search(step + 1, m)
                        if n == LAST_LEAD:
                            negate(step + 1, 1 - par)
                    if has(step, "out") and n == SIGMOID:
                        sigmoid(step - 1)
                    if has(step, "shift") and n == SLOT["shift"]:
                        split_shift(step, step + 1)
                    if n in DIVIDE:
                        a = DIVIDE[n]
                        if has(step, f"turn{a}1"):
                            late = a == A - 1
                            divide(step, step - 1 if late else step, 1 - par if late else par, a)
                    if has(step, "qk1"):
                        for part in SPLIT.get(n, ()):
                            split(step, step + 2, part)
            schedule(dve, body)


def build(nc, D):
    D["list_in"] = nc.dram_tensor("list_in", (TILES * P, C), F32).ap()
    D["list_out"] = nc.dram_tensor("list_out", (TILES * P, C), F32).ap()
    D["scratch_pieces"] = nc.dram_tensor("scratch_pieces", (4, NPIECE, C, SEQ), BF16).ap()
    D["scratch_shift"] = nc.dram_tensor("scratch_shift", (2 * HEADS, NPIECE, SEQ), BF16).ap()
    D["zeros"] = nc.dram_tensor("zeros", (NPIECE, HEADS * SEQ), BF16).ap()
    with ExitStack() as ctx:
        def sb(name, shape, dt=F32):
            return ctx.enter_context(nc.sbuf_tensor(name, shape, dt))
        R = Resident()
        R.ps = ctx.enter_context(nc.psum_tensor("ps", [P, 8, 512], F32))
        R.passed = ctx.enter_context(nc.semaphore("passed"))
        R.list_clear = ctx.enter_context(nc.semaphore("list_clear"))
        R.x = sb("x", [P, NT, C])
        R.xnT = sb("xnT", [P, NTOK])
        R.xn = sb("xn", [P, NT, C])
        R.gate = sb("gate", [P, NT, TOPK])
        R.slot = sb("slot", [P, NT, TOPK], U32)
        R.owner = sb("owner", [1, TILES], I32)
        R.zero_tile = sb("zero_tile", [P, C])
        R.starts = sb("starts", [P, TILES])
        R.wqk = [sb("wqk0", [P, 4, C]), sb("wqk1", [P, 2, C])]
        R.wv = [sb("wv0", [P, 2 * C]), sb("wv1", [P, C])]
        R.wo = [sb("wo0", [P, 2, C]), sb("wo1", [P, 1, C])]
        R.bqk = sb("bqk", [P, 2])
        R.bv = sb("bv", [1, C])
        R.bo = sb("bo", [1, C])
        R.wr = [sb(f"wr{l}", [P, EXPERTS]) for l in range(2)]
        R.rank = sb("rank", [P, EXPERTS])
        R.ident = sb("ident", [P, P])
        R.ident_bf = sb("ident_bf", [P, P], BF16)
        R.ones = sb("ones", [P, P])
        R.before = sb("before", [P, P])
        R.mask_diag_q = sb("mask_diag_q", [P, 4, P], BF16)
        R.mask_diag_k = sb("mask_diag_k", [P, 4, P], BF16)
        R.mask_late_q = sb("mask_late_q", [P, 2, 2 * P], BF16)
        R.mask_early_k = sb("mask_early_k", [P, 2, 2 * P], BF16)
        R.lam = sb("lam", [P, HEADS])
        R.outside = sb("outside", [P, 1])
        R.no_outside = sb("no_outside", [P, 1])

        R.stack = [sb(f"stack{p}", [P, 4, HEADS, SEQ], BF16) for p in range(2)]
        build_constants(nc, R, D)
        for layer in range(2):
            build_layernorm(nc, R, layer)
            build_router(nc, R, layer)
            build_experts(nc, R, D, layer)
            build_attention(nc, R, D, layer)


def kernel(**inputs):
    import numpy as _np
    import concourse.bacc as _bacc
    from concourse import mybir as _mybir
    from concourse.bass_utils import run_bass_kernel_spmd as _run

    laid = {k: _np.asarray(v) for k, v in inputs.items()}
    laid["L0_attn_x"] = laid["L0_attn_x"].reshape(NTOK, C)
    for k in ("L1_attn_wq", "L1_attn_wk", "L1_attn_wv", "L1_attn_wo", "L1_ffn_w_router"):
        laid[k] = laid[k].T
    for k in ("L0_attn_q1_w", "L0_attn_q2_w", "L0_attn_k1_w", "L0_attn_k2_w", "L1_attn_wq", "L1_attn_wk"):
        laid[k] = laid[k].reshape(C, HEADS, HD).transpose(0, 2, 1).reshape(C, C)
    for k in ("L1_attn_bq", "L1_attn_bk"):
        laid[k] = laid[k].reshape(HEADS, HD).T.reshape(C, 1)
    for k in ("L1_attn_bv", "L1_attn_bo", *(f"L0_attn_lambda_{a}{n}" for a in "qk" for n in "12")):
        laid[k] = laid[k].reshape(1, C)
    laid["L0_w1"], laid["L0_w2"] = laid.pop("L0_ffn_W1"), laid.pop("L0_ffn_W2")
    laid["L1_w1"] = laid.pop("L1_ffn_w1").transpose(0, 2, 1)
    laid["L1_w2"] = laid.pop("L1_ffn_w2").transpose(0, 2, 1)
    for l in range(2):
        laid[f"L{l}_b1"] = laid.pop(f"L{l}_ffn_b1").reshape(EXPERTS, HB, P).transpose(0, 2, 1)

    nc = _bacc.Bacc("TRN2", target_bir_lowering=False, num_devices=1)
    arrays, D = {}, {}
    for name, a in laid.items():
        a = _np.ascontiguousarray(a)
        arrays[f"in_{name}"] = a
        D[name] = nc.dram_tensor(f"in_{name}", a.shape, _mybir.dt.from_np(a.dtype), kind="ExternalInput").ap()
    out = nc.dram_tensor("out_dram", (BATCH, SEQ, C), F32, kind="ExternalOutput").ap()
    D["out"] = out.rearrange("b s d -> (b s) d").rearrange("(t p) d -> t p d", p=P)
    build(nc, D)
    r = _run(nc, [arrays], core_ids=[0])
    return r.results[0]["out_dram"]
```
